# Optimizing a Trainium2 kernel written in Bass

```python
import numpy as np
import jax
import jax.numpy as jnp

def _softmax(x, axis=-1):
    return jax.nn.softmax(x, axis=axis)

def _gelu(x):
    return jax.nn.gelu(x, approximate=True)

def _silu(x):
    return jax.nn.silu(x)

def _sigmoid(x):
    return jax.nn.sigmoid(x)

def _layernorm(x, axis=-1, eps=1e-05):
    m = jnp.mean(x, axis=axis, keepdims=True)
    v = jnp.var(x, axis=axis, keepdims=True)
    return (x - m) / jnp.sqrt(v + eps)

def _scatter_add(tgt, idx, src, axis=0):
    return tgt.at[idx].add(src)

def _segment_sum(src, seg, n):
    return jax.ops.segment_sum(src, seg, n)
kernel_name = 'mk_audio_tower_d1_tok_audfeat512_r4_f85d8a'

def setup_inputs(seed: int=0):
    np.random.seed(seed)
    _w = jnp.asarray

    def _rec_inputs():
        import jax
        import jax.numpy as jnp
        _rk = jax.random.key(seed)
        x = 7.22013e-05 + 1.00017 * jax.random.normal(jax.random.fold_in(_rk, 1), (8, 375, 128), jnp.float32)
        return x
    x = _rec_inputs()

    def _L0_tok_setup():
        import jax, jax.numpy as jnp
        import numpy as np
        B, T, D, H, K = (16, 256, 128, 128, 2)
        key = jax.random.key(seed)
        ks = jax.random.split(key, 7)
        scale = 1.0 / np.sqrt(D * K)
        x = jax.random.normal(ks[0], (B, T, D), dtype=jnp.float32)
        W_z = jax.random.uniform(ks[1], (H, D, K), jnp.float32, -scale, scale)
        b_z = jax.random.uniform(ks[2], (H,), jnp.float32, -scale, scale)
        W_f = jax.random.uniform(ks[3], (H, D, K), jnp.float32, -scale, scale)
        b_f = jax.random.uniform(ks[4], (H,), jnp.float32, -scale, scale)
        W_o = jax.random.uniform(ks[5], (H, D, K), jnp.float32, -scale, scale)
        b_o = jax.random.uniform(ks[6], (H,), jnp.float32, -scale, scale)
        return {'x': x, 'W_z': W_z, 'b_z': b_z, 'W_f': W_f, 'b_f': b_f, 'W_o': W_o, 'b_o': b_o}
    _L0_tok_all = _L0_tok_setup()
    _L0_tok_in = {k: v for k, v in _L0_tok_all.items() if k in ('W_z', 'b_z', 'W_f', 'b_f', 'W_o', 'b_o')}
    del _L0_tok_all

    def _L0_attn_setup():
        import jax, jax.numpy as jnp
        import numpy as np
        NUM_HEADS = 8
        D_MODEL = 128
        HEAD_DIM = D_MODEL // NUM_HEADS
        LN_EPS = 1e-05

        def _rel_shift(x):
            b, h, s, p = x.shape
            x = jnp.pad(x, ((0, 0), (0, 0), (0, 0), (1, 0)))
            x = x.reshape(b, h, p + 1, s)[:, :, 1:, :]
            x = x.reshape(b, h, s, p)
            return x[:, :, :, :s]
        key = jax.random.key(seed)
        ks = jax.random.split(key, 12)
        B, S = (8, 256)
        P = 2 * S - 1
        s = 0.02
        return {'x': jax.random.normal(ks[0], (B, S, D_MODEL), jnp.float32), 'pos_emb': jax.random.normal(ks[1], (P, D_MODEL), jnp.float32), 'ln_w': jnp.ones((D_MODEL,), jnp.float32), 'ln_b': jnp.zeros((D_MODEL,), jnp.float32), 'Wq': jax.random.normal(ks[2], (D_MODEL, D_MODEL), jnp.float32) * s, 'bq': jax.random.normal(ks[3], (D_MODEL,), jnp.float32) * s, 'Wk': jax.random.normal(ks[4], (D_MODEL, D_MODEL), jnp.float32) * s, 'bk': jax.random.normal(ks[5], (D_MODEL,), jnp.float32) * s, 'Wv': jax.random.normal(ks[6], (D_MODEL, D_MODEL), jnp.float32) * s, 'bv': jax.random.normal(ks[7], (D_MODEL,), jnp.float32) * s, 'Wo': jax.random.normal(ks[8], (D_MODEL, D_MODEL), jnp.float32) * s, 'bo': jax.random.normal(ks[9], (D_MODEL,), jnp.float32) * s, 'Wp': jax.random.normal(ks[10], (D_MODEL, D_MODEL), jnp.float32) * s, 'pos_bias_u': jax.random.normal(ks[11], (D_MODEL,), jnp.float32) * s, 'pos_bias_v': jax.random.normal(jax.random.fold_in(key, 99), (D_MODEL,), jnp.float32) * s}
    _L0_attn_all = _L0_attn_setup()
    _L0_attn_in = {k: v for k, v in _L0_attn_all.items() if k in ('pos_emb', 'ln_w', 'ln_b', 'Wq', 'bq', 'Wk', 'bk', 'Wv', 'bv', 'Wo', 'bo', 'Wp', 'pos_bias_u', 'pos_bias_v')}
    del _L0_attn_all

    def _L0_ffn_setup():
        import jax, jax.numpy as jnp
        import numpy as np
        E = 16
        K = 4
        NEG = jnp.float32(-1e+20)

        def _swiglu(x, w1, w2, w3):
            a = x @ w1
            return a * jax.nn.sigmoid(a) * (x @ w2) @ w3
        key = jax.random.key(seed)
        ks = jax.random.split(key, 9)
        B, S, D, H = (32, 128, 128, 1365)
        s = 0.02
        return {'x': jax.random.normal(ks[0], (B, S, D), jnp.float32), 'gate_w': jax.random.normal(ks[1], (D, E), jnp.float32) * s, 'routing_bias': jnp.zeros((E,), jnp.float32), 'w1': jax.random.normal(ks[2], (E, D, H), jnp.float32) * s, 'w2': jax.random.normal(ks[3], (E, D, H), jnp.float32) * s, 'w3': jax.random.normal(ks[4], (E, H, D), jnp.float32) * s, 'sw1': jax.random.normal(ks[5], (D, H), jnp.float32) * s, 'sw2': jax.random.normal(ks[6], (D, H), jnp.float32) * s, 'sw3': jax.random.normal(ks[7], (H, D), jnp.float32) * s}
    _L0_ffn_all = _L0_ffn_setup()
    _L0_ffn_in = {k: v for k, v in _L0_ffn_all.items() if k in ('gate_w', 'routing_bias', 'w1', 'w2', 'w3', 'sw1', 'sw2', 'sw3')}
    del _L0_ffn_all
    return {'x': x, 'L0_tok_W_z': _L0_tok_in['W_z'], 'L0_tok_b_z': _L0_tok_in['b_z'], 'L0_tok_W_f': _L0_tok_in['W_f'], 'L0_tok_b_f': _L0_tok_in['b_f'], 'L0_tok_W_o': _L0_tok_in['W_o'], 'L0_tok_b_o': _L0_tok_in['b_o'], 'L0_attn_pos_emb': _L0_attn_in['pos_emb'], 'L0_attn_ln_w': _L0_attn_in['ln_w'], 'L0_attn_ln_b': _L0_attn_in['ln_b'], 'L0_attn_Wq': _L0_attn_in['Wq'], 'L0_attn_bq': _L0_attn_in['bq'], 'L0_attn_Wk': _L0_attn_in['Wk'], 'L0_attn_bk': _L0_attn_in['bk'], 'L0_attn_Wv': _L0_attn_in['Wv'], 'L0_attn_bv': _L0_attn_in['bv'], 'L0_attn_Wo': _L0_attn_in['Wo'], 'L0_attn_bo': _L0_attn_in['bo'], 'L0_attn_Wp': _L0_attn_in['Wp'], 'L0_attn_pos_bias_u': _L0_attn_in['pos_bias_u'], 'L0_attn_pos_bias_v': _L0_attn_in['pos_bias_v'], 'L0_ffn_gate_w': _L0_ffn_in['gate_w'], 'L0_ffn_routing_bias': _L0_ffn_in['routing_bias'], 'L0_ffn_w1': _L0_ffn_in['w1'], 'L0_ffn_w2': _L0_ffn_in['w2'], 'L0_ffn_w3': _L0_ffn_in['w3'], 'L0_ffn_sw1': _L0_ffn_in['sw1'], 'L0_ffn_sw2': _L0_ffn_in['sw2'], 'L0_ffn_sw3': _L0_ffn_in['sw3']}

def reference(x, L0_tok_W_z, L0_tok_b_z, L0_tok_W_f, L0_tok_b_f, L0_tok_W_o, L0_tok_b_o, L0_attn_pos_emb, L0_attn_ln_w, L0_attn_ln_b, L0_attn_Wq, L0_attn_bq, L0_attn_Wk, L0_attn_bk, L0_attn_Wv, L0_attn_bv, L0_attn_Wo, L0_attn_bo, L0_attn_Wp, L0_attn_pos_bias_u, L0_attn_pos_bias_v, L0_ffn_gate_w, L0_ffn_routing_bias, L0_ffn_w1, L0_ffn_w2, L0_ffn_w3, L0_ffn_sw1, L0_ffn_sw2, L0_ffn_sw3):
    import jax
    import jax.numpy as jnp

    def _L0_tok_ref(x, W_z, b_z, W_f, b_f, W_o, b_o):
        import jax, jax.numpy as jnp
        import numpy as np
        B, T, D, H, K = (16, 256, 128, 128, 2)

        def conv(W, b):
            return jnp.einsum('btd,hd->bth', x[:, :-1, :], W[:, :, 0]) + jnp.einsum('btd,hd->bth', x[:, 1:, :], W[:, :, 1]) + b
        z = jnp.tanh(conv(W_z, b_z))
        f = jax.nn.sigmoid(conv(W_f, b_f))
        o = jax.nn.sigmoid(conv(W_o, b_o))

        def step(c, zfo):
            zt, ft, ot = zfo
            c = ft * c + (1.0 - ft) * zt
            return (c, ot * c)
        c0 = jnp.zeros_like(z[:, 0, :])
        zT = jnp.swapaxes(z, 0, 1)
        fT = jnp.swapaxes(f, 0, 1)
        oT = jnp.swapaxes(o, 0, 1)
        _, h = jax.lax.scan(step, c0, (zT, fT, oT))
        return jnp.swapaxes(h, 0, 1)

    def _L0_attn_ref(x, pos_emb, ln_w, ln_b, Wq, bq, Wk, bk, Wv, bv, Wo, bo, Wp, pos_bias_u, pos_bias_v):
        import jax, jax.numpy as jnp
        import numpy as np
        NUM_HEADS = 8
        D_MODEL = 128
        HEAD_DIM = D_MODEL // NUM_HEADS
        LN_EPS = 1e-05

        def _rel_shift(x):
            b, h, s, p = x.shape
            x = jnp.pad(x, ((0, 0), (0, 0), (0, 0), (1, 0)))
            x = x.reshape(b, h, p + 1, s)[:, :, 1:, :]
            x = x.reshape(b, h, s, p)
            return x[:, :, :, :s]
        B, S, D = x.shape
        H, hd = (NUM_HEADS, HEAD_DIM)
        mu = jnp.mean(x, axis=-1, keepdims=True)
        var = jnp.mean(jnp.square(x - mu), axis=-1, keepdims=True)
        h_ = (x - mu) * jax.lax.rsqrt(var + LN_EPS) * ln_w + ln_b
        q = (h_ @ Wq.T + bq).reshape(B, S, H, hd).transpose(0, 2, 1, 3)
        k = (h_ @ Wk.T + bk).reshape(B, S, H, hd).transpose(0, 2, 1, 3)
        v = (h_ @ Wv.T + bv).reshape(B, S, H, hd).transpose(0, 2, 1, 3)
        bias_u = pos_bias_u.reshape(1, H, 1, hd)
        bias_v = pos_bias_v.reshape(1, H, 1, hd)
        content = jnp.einsum('bhqd,bhkd->bhqk', q + bias_u, k)
        p = (pos_emb @ Wp.T).reshape(-1, H, hd).transpose(1, 0, 2)
        pos_score = jnp.einsum('bhqd,hpd->bhqp', q + bias_v, p)
        pos_score = _rel_shift(pos_score)
        scale = 1.0 / np.sqrt(hd).astype(np.float32)
        attn = jax.nn.softmax((content + pos_score) * scale, axis=-1)
        out = jnp.einsum('bhqk,bhkd->bhqd', attn, v)
        out = out.transpose(0, 2, 1, 3).reshape(B, S, D)
        out = out @ Wo.T + bo
        return x + out

    def _L0_ffn_ref(x, gate_w, routing_bias, w1, w2, w3, sw1, sw2, sw3):
        import jax, jax.numpy as jnp
        import numpy as np
        E = 16
        K = 4
        NEG = jnp.float32(-1e+20)

        def _swiglu(x, w1, w2, w3):
            a = x @ w1
            return a * jax.nn.sigmoid(a) * (x @ w2) @ w3
        gate_out = x @ gate_w + routing_bias
        top_v, top_i = jax.lax.top_k(gate_out, K)
        chosen = jax.nn.one_hot(top_i, E, dtype=x.dtype).sum(axis=-2)
        masked = jnp.where(chosen > 0, gate_out, NEG)
        probs = jax.nn.softmax(masked, axis=-1)
        weights = probs * chosen
        out = _swiglu(x, sw1, sw2, sw3)
        for e in range(E):
            out = out + _swiglu(x, w1[e], w2[e], w3[e]) * weights[..., e:e + 1]
        return out
    h = _L0_tok_ref(x, L0_tok_W_z, L0_tok_b_z, L0_tok_W_f, L0_tok_b_f, L0_tok_W_o, L0_tok_b_o)
    h = h + _L0_attn_ref(_layernorm(h, axis=-1), L0_attn_pos_emb, L0_attn_ln_w, L0_attn_ln_b, L0_attn_Wq, L0_attn_bq, L0_attn_Wk, L0_attn_bk, L0_attn_Wv, L0_attn_bv, L0_attn_Wo, L0_attn_bo, L0_attn_Wp, L0_attn_pos_bias_u, L0_attn_pos_bias_v)
    h = h + _L0_ffn_ref(_layernorm(h, axis=-1), L0_ffn_gate_w, L0_ffn_routing_bias, L0_ffn_w1, L0_ffn_w2, L0_ffn_w3, L0_ffn_sw1, L0_ffn_sw2, L0_ffn_sw3)
    return h

_drawn_inputs = setup_inputs


def setup_inputs(seed=0):
    import zlib

    import numpy as np

    out = dict(_drawn_inputs(seed))
    spreads = {'L0_attn_ln_w': (1.0, 0.6), 'L0_attn_ln_b': (0.0, 0.8), 'L0_ffn_routing_bias': (0.0, 0.8)}
    factors = {'L0_tok_b_f': 3.529,
     'L0_tok_b_o': 3.396,
     'L0_attn_pos_emb': 8.0,
     'L0_attn_Wq': 8.0,
     'L0_attn_bq': 8.0,
     'L0_attn_Wk': 8.0,
     'L0_attn_bk': 8.0,
     'L0_attn_Wv': 6.774,
     'L0_attn_bv': 8.0,
     'L0_attn_Wo': 6.556,
     'L0_attn_bo': 2.882,
     'L0_attn_Wp': 8.0,
     'L0_attn_pos_bias_u': 8.0,
     'L0_attn_pos_bias_v': 8.0,
     'L0_ffn_gate_w': 7.886,
     'L0_ffn_w1': 6.72,
     'L0_ffn_w2': 6.691,
     'L0_ffn_w3': 6.685,
     'L0_ffn_sw1': 3.376,
     'L0_ffn_sw2': 3.367,
     'L0_ffn_sw3': 3.359}
    for name, (base, spread) in spreads.items():
        noise = np.random.default_rng([zlib.crc32(name.encode()), seed]).standard_normal(out[name].shape)
        drawn = base * np.exp(spread * noise) if base else spread * noise
        out[name] = jnp.asarray(drawn.astype(out[name].dtype))
    for name, factor in factors.items():
        out[name] = (out[name] * factor).astype(out[name].dtype)
    return out
```

```python
from contextlib import ExitStack

import numpy as np

import concourse.bass as bass
from concourse import mybir

F32 = mybir.dt.float32
F32R = mybir.dt.float32r
I32 = mybir.dt.int32
U32 = mybir.dt.uint32
ALU = mybir.AluOpType
ACT = mybir.ActivationFunctionType
AX = mybir.AxisListType

P = 128
B = 8
T_IN = 375
T = T_IN - 1
NT = 3
TP = NT * P
T_LAST = T - (NT - 1) * P
X_LAST = T_IN - (NT - 1) * P
D = 128
NH = 8
HD = D // NH
NPAIR = NH // 2
NPOS = 511
POSW = NPOS + 1
E = 16
TOPK = 4
F = 1365
FC = (F + P - 1) // P
F_LAST = F - (FC - 1) * P
EPS = 1e-5
UNITS = NH * NT
NTILES = B * NT

GT = 2 * P
ROUTED = (B * T * TOPK + E * (GT - 1)) // GT
ROUTED += ROUTED % 2
SHARED = NTILES * P // GT
REGION = -(-(B * T + GT) // GT) * GT
ZERO_ROW = E * REGION
DUMP_ROW = ZERO_ROW + GT
XG_ROWS = DUMP_ROW + NT * P * TOPK


class Steps:

    def __init__(self, engine, sem, alone=None):
        self.engine, self.sem, self.alone, self.base, self.n = engine, sem, alone, 0, 0

    def did(self, instruction):
        instruction.then_inc(self.sem, 1)
        self.n += 1

    def settle(self, alone=None):
        wait(self.engine, self.sem, self.base + self.n, alone or self.alone)

    def enter(self, i, per_turn):
        self.outer = self.base + self.n
        self.base, self.n = self.outer + i * per_turn, 0

    def leave(self, turns, per_turn):
        assert self.n == per_turn, (self.n, per_turn)
        self.base, self.n = self.outer + turns * per_turn, 0


def wait(engine, sem, value, alone=None):
    if not (isinstance(value, int) and value <= 0):
        engine.wait_ge(sem, value)
        if alone is not None and not isinstance(value, int):
            engine.sem_inc(alone, 1)


POS_AT = {s: [s - 4] for s in range(4, 20)}
POS_AT.update({s: [2 * s - 24, 2 * s - 23] for s in range(20, 24)})


def side_jobs(prev, nxt):
    jobs = []
    if nxt:
        jobs += [(0, "q", 0), (1, "k", 0), (2, "v", 0), (3, "sqv", 0), (6, "sk", 0), (7, "squ", 0), (8, "sqv", 1),
                 (12, "sk", 1), (13, "squ", 1), (14, "sqv", 2), (17, "sqv", 3), (18, "sk", 2), (19, "squ", 2),
                 (24, "sk", 3), (25, "squ", 3)]
    if prev:
        jobs += [(4, "rt", 0), (5, "rb", 0), (9, "wo", 0), (11, "x2t", 0), (15, "gate", 0), (21, "count", 0)]
    return sorted(jobs, key=lambda j: j[0])


J_NEXT, J_PREV = len(side_jobs(False, True)), len(side_jobs(True, False))
J_FULL = J_NEXT + J_PREV


def jobs_before(b):
    if isinstance(b, int) and b <= 0:
        return J_NEXT * (b + 1)
    if isinstance(b, int) and b == B:
        return 2 * J_NEXT + (B - 2) * J_FULL + J_PREV
    return 2 * J_NEXT + (b - 1) * J_FULL


def build(nc, a, out):
    ctx = ExitStack()
    with ctx:
        def sb(name, shape, dt=F32):
            return ctx.enter_context(nc.sbuf_tensor(name, shape, dt))

        def sem(name):
            return ctx.enter_context(nc.semaphore(name))

        bank = [ctx.enter_context(nc.psum_tensor(f"bank{i}", [P, 512], F32)) for i in range(8)]

        pos_dram = nc.dram_tensor("pos_scores", (NH, TP * POSW), F32).ap()
        xg_dram = nc.dram_tensor("dispatched_x", (XG_ROWS, D), F32).ap()
        xs_dram = nc.dram_tensor("shared_x", (NTILES * P, D), F32).ap()
        yg_dram = nc.dram_tensor("routed_y", (ROUTED * GT, D), F32).ap()
        ys_dram = nc.dram_tensor("shared_y", (NTILES * P, D), F32).ap()

        ident = sb("ident", [P, P])
        ones = sb("ones", [P, P])
        tri = sb("tri", [P, P])
        head_rows = sb("head_rows", [NH, D])
        template = sb("template", [P, 4, P])
        spread_q_hi = sb("spread_q_hi", [P, NPAIR, P], F32R)
        spread_q_lo = sb("spread_q_lo", [P, NPAIR, P], F32R)
        spread_k_hi = sb("spread_k_hi", [P, NPAIR, P], F32R)
        spread_k_lo = sb("spread_k_lo", [P, NPAIR, P], F32R)
        iota_e = sb("iota_e", [P, E])
        region_e = sb("region_e", [P, E])
        iota_tile = sb("iota_tile", [1, 64])
        valid = sb("valid", [P, NT * TOPK])
        dump_rows = sb("dump_rows", [P, NT * TOPK])
        minus_half = sb("minus_half", [P, NT])
        zeros = sb("zeros", [P, 2, D])
        arena = sb("arena", [P, 4 * F])
        used = [0]

        def early(shape):
            n = int(np.prod(shape[1:]))
            flat = arena[:, used[0]:used[0] + n]
            used[0] += n
            if len(shape) == 2:
                return flat
            return flat.rearrange("p (a b) -> p a b", a=shape[1])

        gate_raw = early([P, 3, 2 * D])
        att_raw = early([P, 5, D])
        pos_raw = early([P, 4, D])
        wT = sb("wT", [P, 11, P])
        posT = sb("posT", [P, 512])
        cols = sb("cols", [P, 9])
        qbias = sb("qbias", [P, 2])
        bv_row = sb("bv_row", [P, D])
        bo_row = sb("bo_row", [P, D])
        rb_row = sb("rb_row", [P, E])
        gate_w = sb("gate_w", [P, E])
        hnT = sb("hnT", [P, B * TP])
        HX = sb("HX", [P, B, TP])
        H2 = sb("H2", [P, B, TP])
        p_stack = sb("p_stack", [P, NPAIR, 512], F32R)
        x_in = early([P, NT, D])
        xT = early([P, T_IN + 1])
        gates = early([P, 3, T])
        fz = early([P, T])
        cell = early([P, T])
        hT = early([P, TP])
        stats = sb("stats", [P, NT, 6])
        mv = sb("mv", [P, NT, 2])
        vareps = sb("vareps", [P, NT])
        rstd = sb("rstd", [P, NT])
        x1 = sb("x1", [P, NT, D])
        n2 = sb("n2", [P, NT, D])
        hx_part = early([P, TP])
        hnb = sb("hnb", [P, TP])
        t_qu = sb("t_qu", [P, TP])
        t_qv = sb("t_qv", [P, TP])
        t_k = sb("t_k", [P, 512])
        hi_qu, lo_qu = sb("hi_qu", [P, TP], F32R), sb("lo_qu", [P, TP], F32R)
        hi_qv, lo_qv = sb("hi_qv", [P, TP], F32R), sb("lo_qv", [P, TP], F32R)
        hi_k, lo_k = sb("hi_k", [P, 512], F32R), sb("lo_k", [P, 512], F32R)
        qu_stack = sb("qu_stack", [P, NPAIR, TP], F32R)
        qv_stack = sb("qv_stack", [P, NPAIR, TP], F32R)
        k_stack = sb("k_stack", [P, NPAIR, TP], F32R)
        v_rows = sb("v_rows", [P, NT, D])
        v_diag = sb("v_diag", [P, NT, NH, D])
        pos_out = sb("pos_out", [P, 2, NT, POSW])
        pos_in = sb("pos_in", [P, 4, NT, T])
        score = sb("score", [P, 2, T])
        least = sb("least", [P, 2])
        probs = sb("probs", [P, 2, TP])
        rowsum = sb("rowsum", [P, UNITS])
        inv_rowsum = sb("inv_rowsum", [P, UNITS])
        probsT = sb("probsT", [P, 2, NT, TP])
        oT_raw = sb("oT_raw", [P, TP])
        inv_T = sb("inv_T", [NH, TP])
        oT = sb("oT", [P, TP])
        h2 = sb("h2", [P, NT, D])
        x2 = sb("x2", [P, NT, D])
        x2T = sb("x2T", [P, TP])
        logits = sb("logits", [P, NT, E])
        top_v = sb("top_v", [P, NT, 8])
        top_i = sb("top_i", [P, NT, 8], U32)
        top_f = sb("top_f", [P, NT, TOPK])
        onehot = sb("onehot", [P, NT * TOPK, E])
        picked = sb("picked", [P, NT * TOPK, E])
        chosen = sb("chosen", [P, NT, E])
        before = sb("before", [P, NT + 1, E])
        place = sb("place", [P, NT, E])
        slot_f = sb("slot_f", [P, NT * TOPK])
        slot_i = sb("slot_i", [P, NT * TOPK], I32)
        all_slot = sb("all_slot", [P, NTILES, TOPK])
        all_expert = sb("all_expert", [P, NTILES, TOPK])
        all_top = sb("all_top", [P, NTILES, TOPK])
        all_weight = sb("all_weight", [P, NTILES, TOPK])
        weight_sum = sb("weight_sum", [P, NTILES])
        y_index = sb("y_index", [P, NTILES, TOPK], I32)
        count_i = sb("count_i", [P, E], I32)
        tiles_f = sb("tiles_f", [P, E])
        tiles_end = sb("tiles_end", [P, E])
        shift_e = sb("shift_e", [P, E])
        pad_row = sb("pad_row", [1, E], I32)
        tile_cmp = sb("tile_cmp", [1, 64, E])
        tile_e = sb("tile_e", [1, 64])
        tile_row = sb("tile_row", [1, 64])
        tile_fix = sb("tile_fix", [1, 64])
        table = sb("table", [1, 2, 64], I32)

        def view(tensor, shape):
            n = int(np.prod(shape[1:]))
            letters = "abcd"[:len(shape) - 1]
            names = " ".join(letters)
            return tensor[:, 0:n].rearrange(f"p ({names}) -> p {names}", **dict(zip(letters, shape[1:])))

        assert used[0] <= 4 * F
        w1s = arena[:, 0:2 * F].rearrange("p (s f) -> p s f", s=2)
        w2s = arena[:, 2 * F:4 * F].rearrange("p (s f) -> p s f", s=2)
        flatten = v_diag[:, :, :, :].rearrange("p a b c -> p (a b c)")
        w3s = [view(flatten, [P, FC, D]),
               view(pos_out[:, :, :, :].rearrange("p a b c -> p (a b c)"), [P, FC, D])]
        room = pos_in[:, :, :, :].rearrange("p a b c -> p (a b c)")
        xe = room[:, 0:512].rearrange("p (s t d) -> p s t d", s=2, t=2)
        xeT = room[:, 512:1024].rearrange("p (s t) -> p s t", s=2)
        act_a = room[:, 1024:2048].rearrange("p (s t) -> p s t", s=2)
        gated = room[:, 2048:3072].rearrange("p (s t) -> p s t", s=2)
        yT = room[:, 3072:3584].rearrange("p (s t) -> p s t", s=2)
        y_rows = room[:, 3584:4096].rearrange("p (s t d) -> p s t d", s=2, t=2)
        room2 = probsT[:, :, :, :].rearrange("p a b c -> p (a b c)")
        gathered = hnT[:, 0:2 * NT * TOPK * D].rearrange("p (s t d) -> p s t d", s=2, t=NT * TOPK)
        shared_in = room2[:, 0:2 * TP].rearrange("p (s t) -> p s t", s=2)
        total = HX

        weights_in = sem("weights_in")
        pool_step, dve_step, act_step = sem("pool_step"), sem("dve_step"), sem("act_step")
        pool_gate, dve_gate, sp_gate = sem("pool_gate"), sem("dve_gate"), sem("sp_gate")
        consts_ready = sem("consts_ready")
        setup_ps, setup_sb = sem("setup_ps"), sem("setup_sb")
        x_loaded = sem("x_loaded")
        xT_ps, xT_sb = sem("xT_ps"), sem("xT_sb")
        conv_ps, conv_sb = sem("conv_ps"), sem("conv_sb")
        hT_ready, h_ps = sem("hT_ready"), sem("h_ps")
        var_ready, rstd_ready = sem("var_ready"), sem("rstd_ready")
        n2_ready, n2_ps, hn_ready = sem("n2_ready"), sem("n2_ps"), sem("hn_ready")
        hx_ready, hx_done = sem("hx_ready"), sem("hx_done")
        misc_ps, misc_free = sem("misc_ps"), sem("misc_free")
        hnb_ready = sem("hnb_ready")
        t_ready, split_ready = sem("t_ready"), sem("split_ready")
        v_ready, v_diag_ready = sem("v_ready"), sem("v_diag_ready")
        pos_ps, pos_sb = sem("pos_ps"), sem("pos_sb")
        pos_written = [sem(f"pos_written{i}") for i in range(2)]
        pos_read = [sem(f"pos_read{i}") for i in range(4)]
        content_ps, scored, probs_ready = sem("content_ps"), sem("scored"), sem("probs_ready")
        probsT_ps, probsT_sb, av_done = sem("probsT_ps"), sem("probsT_sb"), sem("av_done")
        inv_ready, oT_copied = sem("inv_ready"), sem("oT_copied")
        h2_ready, x2_ready, h2_kept = sem("h2_ready"), sem("x2_ready"), sem("h2_kept")
        x2_stored, chosen_ready = sem("x2_stored"), sem("chosen_ready")
        slot_ready, scattered = sem("slot_ready"), sem("scattered")
        table_ready, pads_written = sem("table_ready"), sem("pads_written")
        top_shifted, top_exp, weights_ready = sem("top_shifted"), sem("top_exp"), sem("weights_ready")
        w_loaded = [sem(f"w_loaded{i}") for i in range(2)]
        xe_loaded = [sem(f"xe_loaded{i}") for i in range(2)]
        xe_ps, xe_sb = sem("xe_ps"), sem("xe_sb")
        up_ps, act_ready, gated_ready = sem("up_ps"), sem("act_ready"), sem("gated_ready")
        y_ps, y_sb, yT_ps, y_rows_ready = sem("y_ps"), sem("y_sb"), sem("yT_ps"), sem("y_rows_ready")
        y_stored = [sem(f"y_stored{i}") for i in range(2)]
        gather_done = [sem(f"gather_done{i}") for i in range(2)]
        shared_loaded = [sem(f"shared_loaded{i}") for i in range(2)]
        combined, out_stored = sem("combined"), sem("out_stored")

        pos_rows = pos_dram.rearrange("h (s w) -> s h w", w=POSW)

        def shifted(h, t):
            base = pos_dram[h:h + 1, 0:TP * POSW]
            return bass.AP(base.tensor, base.offset + T + t * P * NPOS, [[NPOS, P], [1, T]])

        block = ctx.enter_context(nc.Block())
        N_SMALL = 3 + 5 + 2 + 9 + 4

        @block.sync
        def _(sp):
            for i, n in enumerate(["tok_W_z", "tok_W_f", "tok_W_o"]):
                sp.dma_start(gate_raw[:, i, :], a[n].rearrange("h d k -> h (d k)")).then_inc(weights_in, 16)
            for i, n in enumerate(["attn_Wq", "attn_Wk", "attn_Wv", "attn_Wo", "attn_Wp"]):
                sp.dma_start(att_raw[:, i, :], a[n]).then_inc(weights_in, 16)
            sp.dma_start(pos_raw[:, 0:3, :], a["attn_pos_emb"][0:3 * P, :].rearrange("(t p) d -> p t d", p=P)).then_inc(weights_in, 16)
            sp.dma_start(pos_raw[0:NPOS - 3 * P, 3, :], a["attn_pos_emb"][3 * P:NPOS, :]).then_inc(weights_in, 16)
            for i, n in enumerate(["tok_b_z", "tok_b_f", "tok_b_o", "attn_bq", "attn_bk", "attn_pos_bias_u",
                                   "attn_pos_bias_v", "attn_ln_w", "attn_ln_b"]):
                sp.dma_start(cols[:, i:i + 1], a[n].rearrange("(p o) -> p o", o=1)).then_inc(weights_in, 16)
            for dst, n in ((bv_row, "attn_bv"), (bo_row, "attn_bo"), (rb_row, "ffn_routing_bias")):
                src = a[n].rearrange("(o n) -> o n", o=1)
                sp.dma_start(dst[:, :], src.to_broadcast([P, src.shape[1]])).then_inc(weights_in, 16)
            sp.dma_start(gate_w[:, :], a["ffn_gate_w"]).then_inc(weights_in, 16)

            def load_x(b):
                wait(sp, xT_ps, b)
                sp.dma_start(x_in[:, 0:NT - 1, :], a["x"][bass.ds(b, 1), 0:(NT - 1) * P, :].rearrange(
                    "o (t p) d -> p (o t) d", p=P)).then_inc(x_loaded, 16)
                sp.dma_start(x_in[0:X_LAST, NT - 1, :], a["x"][bass.ds(b, 1), (NT - 1) * P:T_IN, :].rearrange(
                    "o p d -> (o p) d")).then_inc(x_loaded, 16)
            load_x(0)
            with sp.Fori(1, B) as b:
                load_x(b)

            def write_pos(b, h):
                wait(sp, pos_sb, UNITS * b + NT * h + NT, sp_gate)
                wait(sp, pos_read[h % 4], 16 * NT * (2 * b - 1 + h // 4))
                sp.dma_start(pos_rows[:, h, :].rearrange("(t p) w -> p t w", p=P), pos_out[:, h % 2, :, :]).then_inc(
                    pos_written[h % 2], 16)

            def read_pos(b, h):
                wait(sp, scored, UNITS * b + NT * (h - 3))
                wait(sp, pos_written[h % 2], 16 * (4 * b + h // 2 + 1))
                for t in range(NT):
                    sp.dma_start(pos_in[:, h % 4, t, :], shifted(h, t)).then_inc(pos_read[h % 4], 16)

            def sp_body(b, att, prev, nxt):
                order = []
                if nxt:
                    done = {m: s for s, ms in POS_AT.items() for m in ms}
                    order += [(done[NT * h + NT - 1] + 0.5, write_pos, b + 1, h) for h in range(NH)]
                if att:
                    order += [(NT * h + 2.2, read_pos, b, h + 4) for h in range(4)]
                if nxt:
                    order += [(NT * h + 2.2 if att else 23.6 + h, read_pos, b + 1, h - 4) for h in range(4, NH)]
                if prev:
                    order += [(12.1, None, b, 0)]
                for _, what, bb, h in sorted(order, key=lambda o: o[0]):
                    if what is not None:
                        what(bb, h)
                        continue
                    wait(sp, x2_ready, bb)
                    sp.dma_start(xs_dram[bass.ds((bb - 1) * TP, TP), :].rearrange("(t p) d -> p t d", p=P),
                                 x2[:, :, :]).then_inc(x2_stored, 16)

            sp_body(-1, False, False, True)
            sp_body(0, True, False, True)
            with sp.Fori(1, B - 1) as b:
                sp_body(b, True, True, True)
            sp_body(B - 1, True, True, False)
            sp_body(B, False, True, False)

            sp.wait_ge(table_ready, 1)
            sp.wait_ge(scattered, 16 * B * NT * TOPK)
            for e in range(E):
                row = sp.value_load(pad_row[0:1, e:e + 1], min_val=0, max_val=ZERO_ROW - GT)
                sp.dma_start(xg_dram[bass.ds(row, GT), :].rearrange("(t p) d -> p t d", p=P), zeros[:, :, :]).then_inc(pads_written, 16)
            sp.dma_start(xg_dram[ZERO_ROW:ZERO_ROW + GT, :].rearrange("(t p) d -> p t d", p=P), zeros[:, :, :]).then_inc(pads_written, 16)
            sp.wait_ge(pads_written, 16 * (E + 1))

            def load_weights(s, w1, w2, w3a, w3b):
                sp.dma_start(w1s[:, s, :], w1).then_inc(w_loaded[s], 16)
                sp.dma_start(w2s[:, s, :], w2).then_inc(w_loaded[s], 16)
                sp.dma_start(w3s[s][:, 0:FC - 1, :], w3a).then_inc(w_loaded[s], 16)
                sp.dma_start(w3s[s][0:F_LAST, FC - 1, :], w3b).then_inc(w_loaded[s], 16)

            def load_routed(j, s):
                wait(sp, y_ps, j - 1, sp_gate)
                wait(sp, xe_ps, j - 1, sp_gate)
                e = sp.value_load(table[0:1, 0, bass.ds(j, 1)], min_val=0, max_val=E - 1)
                row = sp.value_load(table[0:1, 1, bass.ds(j, 1)], min_val=0, max_val=ZERO_ROW)
                sp.dma_start(xe[:, s, :, :], xg_dram[bass.ds(row, GT), :].rearrange("(t p) d -> p t d", p=P)).then_inc(xe_loaded[s], 16)
                load_weights(s, a["ffn_w1"][bass.ds(e, 1), :, :].rearrange("o d f -> (o d) f"),
                             a["ffn_w2"][bass.ds(e, 1), :, :].rearrange("o d f -> (o d) f"),
                             a["ffn_w3"][bass.ds(e, 1), 0:(FC - 1) * P, :].rearrange("o (c p) d -> p (o c) d", p=P),
                             a["ffn_w3"][bass.ds(e, 1), (FC - 1) * P:F, :].rearrange("o p d -> (o p) d"))

            def store_y(j, s, dram, row):
                sp.wait_ge(y_rows_ready, j + 1)
                sp.dma_start(dram[bass.ds(row, GT), :].rearrange("(t p) d -> p t d", p=P), y_rows[:, s, :, :]).then_inc(y_stored[s], 16)

            load_routed(0, 0)
            load_routed(1, 1)
            with sp.Fori(0, ROUTED // 2 - 1) as i:
                for s in range(2):
                    load_routed(2 * i + s + 2, s)
                    store_y(2 * i + s, s, yg_dram, (2 * i + s) * GT)

            def load_shared(j, s):
                wait(sp, xe_ps, ROUTED + j - 1)
                sp.dma_start(xe[:, s, :, :], xs_dram[bass.ds(j * GT, GT), :].rearrange("(t p) d -> p t d", p=P)).then_inc(xe_loaded[s], 16)

            wait(sp, y_ps, ROUTED - 1)
            load_weights(0, a["ffn_sw1"], a["ffn_sw2"],
                         a["ffn_sw3"][0:(FC - 1) * P, :].rearrange("(c p) d -> p c d", p=P), a["ffn_sw3"][(FC - 1) * P:F, :])
            load_shared(0, 0)
            store_y(ROUTED - 2, 0, yg_dram, (ROUTED - 2) * GT)
            load_shared(1, 1)
            store_y(ROUTED - 1, 1, yg_dram, (ROUTED - 1) * GT)
            with sp.Fori(0, SHARED // 2 - 1) as i:
                for s in range(2):
                    load_shared(2 * i + s + 2, s)
                    store_y(2 * i + s + ROUTED, s, ys_dram, (2 * i + s) * GT)
            for s in range(2):
                store_y(ROUTED + SHARED - 2 + s, s, ys_dram, (SHARED - 2 + s) * GT)

            for s in range(2):
                sp.wait_ge(y_stored[s], 16 * (ROUTED + SHARED) // 2)

            def load_shared_rows(b, s):
                wait(sp, combined, b - 1)
                sp.dma_start(shared_in[:, s, :].rearrange("p (t d) -> p t d", t=NT),
                             ys_dram[bass.ds(b * TP, TP), :].rearrange("(t p) d -> p t d", p=P)).then_inc(shared_loaded[s], 16)

            def store_out(b):
                sp.wait_ge(combined, b + 1)
                rows = out[bass.ds(b, 1), :, :]
                sp.dma_start(rows[:, 0:(NT - 1) * P, :].rearrange("o (t p) d -> p (o t) d", p=P),
                             total[:, bass.ds(b, 1), 0:(NT - 1) * D].rearrange("p o (t d) -> p (o t) d", d=D)).then_inc(out_stored, 16)
                sp.dma_start(rows[:, (NT - 1) * P:T, :].rearrange("o p d -> (o p) d"),
                             total[0:T_LAST, bass.ds(b, 1), (NT - 1) * D:TP].rearrange("p o d -> p (o d)")).then_inc(out_stored, 16)
            load_shared_rows(0, 0)
            load_shared_rows(1, 1)
            with sp.Fori(0, B // 2 - 1) as i:
                for s in range(2):
                    load_shared_rows(2 * i + s + 2, s)
                    store_out(2 * i + s)
            store_out(B - 2)
            store_out(B - 1)
            sp.wait_ge(out_stored, 32 * B)

        @block.gpsimd
        def _(pool):
            g = nc.gpsimd
            step = Steps(pool, pool_step, pool_gate)

            def pw(sem_, value):
                wait(pool, sem_, value, pool_gate)

            step.did(g.memset(ones[:], 1.0))
            step.did(g.memset(template[:], 0.0))
            step.did(g.memset(zeros[:], 0.0))
            step.did(g.memset(v_diag[:, :, :, :], 0.0))
            step.settle()
            step.did(g.affine_select(out=ident[:], in_=ones[:], compare_op=ALU.is_equal, fill=0.0, base=0,
                                     pattern=[[-1, P]], channel_multiplier=1))
            step.did(g.affine_select(out=tri[:], in_=ones[:], compare_op=ALU.is_gt, fill=0.0, base=0,
                                     pattern=[[1, P]], channel_multiplier=-1))
            step.did(g.affine_select(out=head_rows[:], in_=ones[0:NH, :], compare_op=ALU.is_ge, fill=0.0, base=0,
                                     pattern=[[1, D]], channel_multiplier=-HD))
            for n, copies in enumerate(((0, 2), (1, 3), (0, 1), (2, 3))):
                tv = template[:, n, :].rearrange("p (i c f) -> p i c f", i=2, c=4)
                for c in copies:
                    step.did(g.memset(tv[:, :, c, :], 1.0))
            step.settle()
            step.did(g.affine_select(out=head_rows[:], in_=head_rows[:], compare_op=ALU.is_ge, fill=0.0, base=HD - 1,
                                     pattern=[[-1, D]], channel_multiplier=HD))
            for n, spread in enumerate((spread_q_hi, spread_q_lo, spread_k_hi, spread_k_lo)):
                for j in range(NPAIR):
                    step.did(g.affine_select(out=spread[:, j, :], in_=template[:, n, :], compare_op=ALU.is_equal, fill=0.0,
                                             base=-2 * HD * j, pattern=[[-HD, 2], [0, 4], [-1, HD]], channel_multiplier=1))
            step.did(g.iota(iota_e[:], pattern=[[1, E]], base=0, channel_multiplier=0, allow_small_or_imprecise_dtypes=True))
            step.did(g.iota(region_e[:], pattern=[[REGION, E]], base=0, channel_multiplier=0, allow_small_or_imprecise_dtypes=True))
            step.did(g.iota(iota_tile[:], pattern=[[1, 64]], base=0, channel_multiplier=0, allow_small_or_imprecise_dtypes=True))
            step.did(g.iota(dump_rows[:], pattern=[[P * TOPK, NT], [1, TOPK]], base=DUMP_ROW, channel_multiplier=TOPK,
                            allow_small_or_imprecise_dtypes=True))
            step.did(g.memset(minus_half[:], -0.5))
            step.did(g.memset(before[:], 0.0))
            step.did(g.memset(hT[:, T:TP], 0.0))
            step.did(g.memset(probs[:, :, T:TP], 0.0))
            step.did(g.memset(pos_out[:, :, :, 0:1], 0.0))
            step.did(g.memset(posT[:, NPOS:512], 0.0))
            step.settle()
            step.did(g.affine_select(out=valid[:], in_=ones[:, 0:NT * TOPK], compare_op=ALU.is_gt, fill=0.0, base=T,
                                     pattern=[[-P, NT], [0, TOPK]], channel_multiplier=-1))
            step.did(g.affine_select(out=dump_rows[:], in_=dump_rows[:], compare_op=ALU.is_ge, fill=0.0, base=-T,
                                     pattern=[[P, NT], [0, TOPK]], channel_multiplier=1))
            step.settle()
            g.memset(vareps[:], 1.0).then_inc(consts_ready, 1)

            def inverse_root(n):
                pw(var_ready, n + 1)
                step.did(g.tensor_scalar_add(vareps[:], mv[:, :, 1], EPS))
                step.settle()
                g.tensor_tensor(rstd[:], vareps[:], minus_half[:], ALU.pow).then_inc(rstd_ready, 1)

            def pool_mixer(b):
                inverse_root(2 * b)
                inverse_root(2 * b + 1)
                pw(hx_ready, b + 1)
                g.tensor_tensor(HX[:, bass.ds(b, 1), :].rearrange("p o (t d) -> p (o t) d", d=D),
                                hx_part[:].rearrange("p (t d) -> p t d", d=D),
                                bo_row[:, :].unsqueeze(1).to_broadcast([P, NT, D]), ALU.add).then_inc(hx_done, 1)
            def split(n, t, hi, lo, w):
                pw(t_ready, n)
                g.tensor_copy(hi[:, 0:w], t[:, 0:w]).then_inc(pool_step, 1)
                step.n += 1
                step.settle()
                g.tensor_tensor(lo[:, 0:w], t[:, 0:w], hi[:, 0:w].bitcast(F32), ALU.subtract).then_inc(split_ready, 1)

            pw(weights_in, 16 * N_SMALL)
            split(1, t_k, hi_k, lo_k, 512)
            PER = 2
            with pool.Fori(0, B) as b:
                step.enter(b, PER)
                pool_mixer(b)
            step.leave(B, PER)

            def diag(b, h):
                pw(av_done, NH * (b - 1) + h + 1)
                pw(v_ready, b + 1)
                g.tensor_copy(v_diag[:, :, h, h * HD:(h + 1) * HD], v_rows[:, :, h * HD:(h + 1) * HD]).then_inc(v_diag_ready, 1)

            def pool_body(b, att, prev, nxt):
                if nxt:
                    pw(misc_ps, jobs_before(b))
                    pw(hn_ready, b + 2)
                    g.tensor_copy(hnb[:, :], hnT[:, bass.ds((b + 1) * TP, TP)]).then_inc(hnb_ready, 1)
                if att and not (isinstance(b, int) and b == 0):
                    diag(b, NH - 1)
                if nxt:
                    pw(misc_ps, jobs_before(b) + 1)
                    split(3 * b + 5, t_qv, hi_qv, lo_qv, TP)
                    split(3 * b + 6, t_qu, hi_qu, lo_qu, TP)
                    split(3 * b + 7, t_k, hi_k, lo_k, TP)
                heads = range(NH if not att else NH - 1) if nxt else []
                rooted = not prev
                for h in heads:
                    if h >= 2 and not rooted:
                        inverse_root(2 * B + b - 1)
                        rooted = True
                    diag(b + 1, h)
                if not rooted:
                    inverse_root(2 * B + b - 1)
                if prev:
                    pw(slot_ready, b)
                    g.tensor_copy(H2[:, bass.ds(b - 1, 1), :].rearrange("p o (t d) -> p (o t) d", d=D), h2[:, :, :]).then_inc(h2_kept, 1)
                    g.tensor_copy(all_top[:, bass.ds((b - 1) * NT, NT), :], top_v[:, :, 0:TOPK]).then_inc(h2_kept, 1)
                    g.tensor_copy(all_expert[:, bass.ds((b - 1) * NT, NT), :], top_f[:, :, :]).then_inc(h2_kept, 1)
                    g.tensor_copy(all_slot[:, bass.ds((b - 1) * NT, NT), :].rearrange("p t k -> p (t k)"), slot_f[:, :]).then_inc(h2_kept, 1)
                    for t in range(NT):
                        for k in range(TOPK):
                            c = t * TOPK + k
                            pool.indirect_dma_start(xg_dram[:, :], bass.IndirectOffsetOnAxis(slot_i[:, c:c + 1], 0),
                                                    x2[:, t, :], None).then_inc(scattered, 16)

            PER = 4
            pool_body(-1, False, False, True)
            pool_body(0, True, False, True)
            with pool.Fori(1, B - 1) as b:
                step.enter(b - 1, PER)
                pool_body(b, True, True, True)
            step.leave(B - 2, PER)
            pool_body(B - 1, True, True, False)
            pool_body(B, False, True, False)

            for s in range(2):
                pw(y_stored[s], 16 * ROUTED // 2)
            pw(weights_ready, 1)

            def gather(b, s):
                pw(combined, b - 1)
                for t in range(NT):
                    for k in range(TOPK):
                        c = t * TOPK + k
                        step.did(g.tensor_copy(slot_i[:, c:c + 1], y_index[:, bass.ds(b * NT + t, 1), k]))
                        step.settle()
                        pool.indirect_dma_start(gathered[:, s, c, :], None, yg_dram[:, :],
                                                bass.IndirectOffsetOnAxis(slot_i[:, c:c + 1], 0)).then_inc(gather_done[s], 16)
            gather(0, 0)
            pw(gather_done[0], 16 * NT * TOPK)
            gather(1, 1)
            PER = 2 * NT * TOPK
            with pool.Fori(1, B // 2) as i:
                step.enter(i - 1, PER)
                for s in range(2):
                    pw(gather_done[1 - s], 16 * NT * TOPK * (i + s))
                    gather(2 * i + s, s)
            step.leave(B // 2 - 1, PER)

        @block.tensor
        def _(pe):
            mm, tr = nc.tensor.matmul, nc.tensor.transpose
            pe.wait_ge(weights_in, 16 * N_SMALL)
            pe.wait_ge(consts_ready, 1)
            raws = [gate_raw[:, i, :].rearrange("h (d k) -> h k d", k=2)[:, k, :] for i in range(3) for k in range(2)]
            raws += [att_raw[:, i, :] for i in range(5)]
            for n, raw in enumerate(raws):
                ins = tr(bank[n // 4][:, (n % 4) * P:(n % 4 + 1) * P], raw, ident[:])
                if n % 4 == 3 or n == len(raws) - 1:
                    ins.then_inc(setup_ps, 1)
            for t in range(4):
                rows = P if t < 3 else NPOS - 3 * P
                ins = tr(bank[3][:, t * P:t * P + rows], pos_raw[0:rows, t, :], ident[0:rows, 0:rows])
            ins.then_inc(setup_ps, 1)
            pe.wait_ge(setup_sb, 5)
            mm(bank[4][:, :], wT[:, 10, :], posT[:, :], start=True, stop=True).then_inc(setup_ps, 1)
            pe.wait_ge(split_ready, 1)
            for j in range(NPAIR):
                wait(pe, setup_sb, 5 + j)
                mm(bank[5][:, :], spread_k_hi[:, j, :], hi_k[:, :], start=True, stop=False)
                mm(bank[5][:, :], spread_k_lo[:, j, :], lo_k[:, :], start=False, stop=True).then_inc(setup_ps, 1)

            def pe_mixer(b):
                pe.wait_ge(x_loaded, 32 * b + 32)
                for t in range(NT):
                    rows = P if t < NT - 1 else X_LAST
                    ins = tr(bank[0][:, t * P:t * P + rows], x_in[0:rows, t, :], ident[0:rows, 0:rows])
                ins.then_inc(xT_ps, 1)
                pe.wait_ge(xT_sb, b + 1)
                for i in range(3):
                    mm(bank[1 + i][:, 0:T], wT[:, 2 * i, :], xT[:, 0:T], start=True, stop=False)
                    mm(bank[1 + i][:, 0:T], wT[:, 2 * i + 1, :], xT[:, 1:T_IN], start=False, stop=True).then_inc(conv_ps, 1)
                pe.wait_ge(hT_ready, b + 1)
                for t in range(NT):
                    ins = tr(bank[4][:, t * P:(t + 1) * P], hT[:, t * P:(t + 1) * P], ident[:])
                ins.then_inc(h_ps, 1)
                pe.wait_ge(n2_ready, b + 1)
                for t in range(NT):
                    ins = tr(bank[5][:, t * P:(t + 1) * P], n2[:, t, :], ident[:])
                ins.then_inc(n2_ps, 1)
            pe.wait_ge(setup_sb, 9)
            with pe.Fori(0, B) as b:
                pe_mixer(b)
            pe.wait_ge(hn_ready, B)

            mi = bank[7]

            def side(b, pos_in_list, name, j):
                index = jobs_before(b) + pos_in_list
                wait(pe, misc_free, index)
                if name == "q":
                    pe.wait_ge(hnb_ready, b + 2)
                    ins = mm(mi[:, 0:TP], wT[:, 6, :], hnb[:, :], start=True, stop=True)
                elif name == "k":
                    ins = mm(mi[:, 0:TP], wT[:, 7, :], hnb[:, :], start=True, stop=True)
                elif name == "v":
                    for t in range(NT):
                        ins = mm(mi[:, t * P:(t + 1) * P], hnb[:, t * P:(t + 1) * P], wT[:, 8, :], start=True, stop=True)
                elif name in ("sqv", "squ", "sk"):
                    hi, lo, sh, sl = {"sqv": (hi_qv, lo_qv, spread_q_hi, spread_q_lo),
                                      "squ": (hi_qu, lo_qu, spread_q_hi, spread_q_lo),
                                      "sk": (hi_k, lo_k, spread_k_hi, spread_k_lo)}[name]
                    if j == 0:
                        pe.wait_ge(split_ready, 3 * b + {"sqv": 5, "squ": 6, "sk": 7}[name])
                    mm(mi[:, 0:TP], sh[:, j, :], hi[:, 0:TP], start=True, stop=False)
                    ins = mm(mi[:, 0:TP], sl[:, j, :], lo[:, 0:TP], start=False, stop=True)
                elif name == "rt":
                    pe.wait_ge(inv_ready, b)
                    for t in range(NT):
                        ins = tr(mi[0:NH, t * P:(t + 1) * P], inv_rowsum[:].rearrange("p (h t) -> p t h", t=NT)[:, t, :], ident[:])
                elif name == "rb":
                    ins = mm(mi[:, 0:TP], head_rows[:, :], inv_T[:, :], start=True, stop=True)
                elif name == "wo":
                    for t in range(NT):
                        ins = mm(mi[:, t * P:(t + 1) * P], oT[:, t * P:(t + 1) * P], wT[:, 9, :], start=True, stop=True)
                elif name == "x2t":
                    pe.wait_ge(x2_ready, b)
                    for t in range(NT):
                        ins = tr(mi[:, t * P:(t + 1) * P], x2[:, t, :], ident[:])
                elif name == "gate":
                    for t in range(NT):
                        ins = mm(mi[:, t * E:(t + 1) * E], x2T[:, t * P:(t + 1) * P], gate_w[:, :], start=True, stop=True)
                elif name == "count":
                    pe.wait_ge(chosen_ready, b)
                    flat = chosen[:, :, :].rearrange("p t e -> p (t e)")
                    mm(mi[:, 0:NT * E], tri[:, :], flat, start=True, stop=True)
                    ins = mm(mi[:, NT * E:2 * NT * E], ones[:, :], flat, start=True, stop=True)
                ins.then_inc(misc_ps, 1)

            def pe_body(b, att, prev, nxt):
                jobs = side_jobs(prev, nxt)
                where = {(name, j): i for i, (_, name, j) in enumerate(jobs)}
                for s in range(UNITS + 2):
                    u = UNITS * b + s
                    h, t = s // NT, s % NT
                    if att and s < UNITS:
                        wait(pe, scored, u - 1)
                        pair, half = h // 2, 64 * (h % 2)
                        mm(bank[s % 2][:, 0:T], qu_stack[half:half + 64, pair, t * P:(t + 1) * P],
                           k_stack[half:half + 64, pair, 0:T], start=True, stop=True).then_inc(content_ps, 1)
                    for i, (at, name, j) in enumerate(jobs):
                        if at == s:
                            side(b, i, name, j)
                    if nxt:
                        for m in POS_AT.get(s, []):
                            h1, t1 = m // NT, m % NT
                            pair, half = h1 // 2, 64 * (h1 % 2)
                            if m % (2 * NT) == 0:
                                pe.wait_ge(misc_free, jobs_before(b) + where["sqv", pair] + 1)
                            wait(pe, pos_sb, UNITS * (b + 1) + m - 1)
                            mm(bank[2 + m % 2][:, :], qv_stack[half:half + 64, pair, t1 * P:(t1 + 1) * P],
                               p_stack[half:half + 64, pair, :], start=True, stop=True).then_inc(pos_ps, 1)
                    started = not (isinstance(b, int) and b <= 0)
                    if (att and 1 <= s < UNITS) or (s == 0 and started):
                        wait(pe, probs_ready, u)
                        wait(pe, probsT_sb, u - 2)
                        for c in range(NT):
                            ins = tr(bank[4 + (s + 1) % 2][:, c * P:(c + 1) * P], probs[:, (s + 1) % 2, c * P:(c + 1) * P], ident[:])
                        ins.then_inc(probsT_ps, 1)
                    if (att and s >= 4 and s % NT == 1 and s < UNITS) or (s == 1 and started):
                        gh = NH * b + (s - 4) // NT
                        hh = (s - 4) // NT % NH
                        wait(pe, probsT_sb, NT * gh + NT)
                        pe.wait_ge(v_diag_ready, gh + 1)
                        if hh == 0:
                            wait(pe, oT_copied, b)
                        for c in range(NT):
                            rows = P if c < NT - 1 else T_LAST
                            ins = mm(bank[6][:, 0:TP], v_diag[0:rows, c, hh, :], probsT[0:rows, hh % 2, c, :],
                                     start=hh == 0 and c == 0, stop=hh == NH - 1 and c == NT - 1)
                        ins.then_inc(av_done, 1)

            pe_body(-1, False, False, True)
            pe_body(0, True, False, True)
            with pe.Fori(1, B - 1) as b:
                pe_body(b, True, True, True)
            pe_body(B - 1, True, True, False)
            pe_body(B, False, True, False)

            PAIRS = (FC + 1) // 2

            def chunks(c):
                return [k for k in (2 * c, 2 * c + 1) if k < FC]

            def width(k):
                return P if k < FC - 1 else F_LAST

            def transposes(j, s, n):
                pe.wait_ge(xe_loaded[s], 16 * n)
                wait(pe, xe_sb, j)
                for t in range(2):
                    ins = tr(bank[6][:, t * P:(t + 1) * P], xe[:, s, t, :], ident[:])
                ins.then_inc(xe_ps, 1)

            def y_transposes(j, s):
                wait(pe, y_sb, j + 1)
                wait(pe, y_rows_ready, j)
                for t in range(2):
                    ins = tr(bank[7][:, t * P:(t + 1) * P], yT[:, s, t * P:(t + 1) * P], ident[:])
                ins.then_inc(yT_ps, 1)

            def tile(j, s, ws, n, w_count, after, before_this):
                wait(pe, xe_sb, j + 1)
                if w_count is not None:
                    pe.wait_ge(w_loaded[ws], w_count)
                wait(pe, y_sb, j - 1)

                def down(c):
                    pe.wait_ge(gated_ready, PAIRS * j + c + 1)
                    for i, k in enumerate(chunks(c)):
                        ins = mm(bank[4 + s][:, 0:GT], w3s[ws][0:width(k), k, :], gated[0:width(k), c % 2, i * GT:(i + 1) * GT],
                                 start=k == 0, stop=k == FC - 1)
                    return ins
                for c in range(PAIRS):
                    wait(pe, gated_ready, PAIRS * j + c - 1)
                    for w, b0 in ((w1s, 0), (w2s, 2)):
                        for i, k in enumerate(chunks(c)):
                            ins = mm(bank[b0 + c % 2][0:width(k), i * GT:(i + 1) * GT], w[:, ws, k * P:k * P + width(k)],
                                     xeT[:, s, :], start=True, stop=True)
                    ins.then_inc(up_ps, 1)
                    if c >= 1:
                        down(c - 1)
                    if c == 1 and after is not None:
                        transposes(j + 1, 1 - s, after)
                    if c == 2 and before_this:
                        y_transposes(j - 1, 1 - s)
                down(PAIRS - 1).then_inc(y_ps, 1)

            transposes(0, 0, 1)
            tile(0, 0, 0, 1, 64, 1, False)
            tile(1, 1, 1, 1, 64, 2, True)
            with pe.Fori(1, ROUTED // 2) as i:
                for s in range(2):
                    tile(2 * i + s, s, s, None, 64 * (i + 1), i + 1 + s, True)
            R2 = ROUTED // 2
            with pe.Fori(0, SHARED // 2 - 1) as i:
                for s in range(2):
                    tile(ROUTED + 2 * i + s, s, 0, None, 64 * (R2 + 1), R2 + i + 1 + s, True)
            last = ROUTED + SHARED - 2
            tile(last, 0, 0, None, 64 * (R2 + 1), R2 + SHARED // 2, True)
            tile(last + 1, 1, 0, None, 64 * (R2 + 1), None, True)
            y_transposes(last + 1, 1)

        @block.scalar
        def _(act):
            f = nc.scalar.activation
            step = Steps(act, act_step)
            pe_ready = setup_ps
            for n in range(3):
                act.wait_ge(pe_ready, n + 1)
                w = 4 if n < 2 else 3
                nc.scalar.copy(wT[:, 4 * n:4 * n + w, :].rearrange("p a b -> p (a b)"), bank[n][:, 0:w * P]).then_inc(setup_sb, 1)
            act.wait_ge(pe_ready, 4)
            act.wait_ge(consts_ready, 1)
            nc.scalar.copy(posT[:, 0:NPOS], bank[3][:, 0:NPOS]).then_inc(setup_sb, 1)
            act.wait_ge(weights_in, 16 * N_SMALL)
            step.did(nc.scalar.mul(qbias[:, :], cols[:, 5:7], -0.25))
            step.did(nc.scalar.mul(fz[:, 0:1], cols[:, 3:4], -0.25))
            step.settle()
            f(qbias[:, :], qbias[:, :], ACT.Identity, bias=fz[:, 0:1]).then_inc(setup_sb, 1)
            act.wait_ge(pe_ready, 5)
            nc.scalar.copy(t_k[:, :], bank[4][:, :]).then_inc(t_ready, 1)
            for j in range(NPAIR):
                act.wait_ge(pe_ready, 6 + j)
                nc.scalar.copy(p_stack[:, j, :], bank[5][:, :]).then_inc(setup_sb, 1)

            def act_mixer(b):
                act.wait_ge(xT_ps, b + 1)
                nc.scalar.copy(xT[:, 0:T_IN], bank[0][:, 0:T_IN]).then_inc(xT_sb, 1)
                for i, fn in enumerate((ACT.Tanh, ACT.Sigmoid, ACT.Sigmoid)):
                    act.wait_ge(conv_ps, 3 * b + i + 1)
                    if i == 0:
                        wait(act, hT_ready, b)
                    f(gates[:, i, :], bank[1 + i][:, 0:T], fn, bias=cols[:, i:i + 1]).then_inc(conv_sb, 1)
                act.wait_ge(n2_ps, b + 1)
                f(hnT[:, bass.ds(b * TP, TP)], bank[5][:, 0:TP], ACT.Identity, bias=cols[:, 8:9],
                  scale=cols[:, 7:8]).then_inc(hn_ready, 1)
            act_mixer(0)
            with act.Fori(1, B) as b:
                act_mixer(b)

            mi = bank[7]

            def act_side(b, i, name, j):
                n = jobs_before(b) + i
                if name == "q":
                    act.wait_ge(misc_ps, n + 1)
                    wait(act, split_ready, 3 * b + 4)
                    f(t_qv[:, :], mi[:, 0:TP], ACT.Identity, bias=qbias[:, 1:2], scale=-0.25).then_inc(t_ready, 1)
                    f(t_qu[:, :], mi[:, 0:TP], ACT.Identity, bias=qbias[:, 0:1], scale=-0.25).then_inc(t_ready, 1)
                    act.wait_ge(t_ready, 3 * b + 6)
                    nc.scalar.copy(act_done[:, 0:1], qbias[:, 0:1]).then_inc(misc_free, 1)
                elif name == "k":
                    act.wait_ge(misc_ps, n + 1)
                    f(t_k[:, 0:TP], mi[:, 0:TP], ACT.Identity, bias=cols[:, 4:5]).then_inc(t_ready, 1)
                    act.wait_ge(t_ready, 3 * b + 7)
                    nc.scalar.copy(act_done[:, 0:1], qbias[:, 0:1]).then_inc(misc_free, 1)
                elif name in ("sqv", "squ", "sk"):
                    act.wait_ge(misc_ps, n + 1)
                    dst = {"sqv": qv_stack, "squ": qu_stack, "sk": k_stack}[name]
                    nc.scalar.copy(dst[:, j, :], mi[:, 0:TP]).then_inc(misc_free, 1)
                elif name == "x2t":
                    act.wait_ge(misc_ps, n + 1)
                    nc.scalar.copy(x2T[:, :], mi[:, 0:TP]).then_inc(misc_free, 1)

            act_done = sb("act_done", [P, 1])

            def act_body(b, att, prev, nxt):
                jobs = side_jobs(prev, nxt)
                for s in range(UNITS + 2):
                    u = UNITS * b + s
                    if att and s < UNITS:
                        act.wait_ge(scored, u + 1)
                        wait(act, probsT_ps, u - 1)
                        if s == 0:
                            wait(act, inv_ready, b)
                        f(probs[:, s % 2, 0:T], score[:, s % 2, :], ACT.Exp, bias=least[:, s % 2:s % 2 + 1], scale=-1.0,
                          accum_out=rowsum[:, s:s + 1]).then_inc(probs_ready, 1)
                    if nxt:
                        for m in POS_AT.get(s, []):
                            h1, t1 = m // NT, m % NT
                            act.wait_ge(pos_ps, UNITS * (b + 1) + m + 1)
                            if t1 == 0:
                                n = 4 * (b + 1) + h1 // 2
                                wait(act, pos_written[h1 % 2], 16 * n)
                            nc.scalar.copy(pos_out[:, h1 % 2, t1, 1:POSW], bank[2 + m % 2][:, 0:NPOS]).then_inc(pos_sb, 1)
                    if s == 2 and prev:
                        act.wait_ge(av_done, NH * b)
                        wait(act, misc_free, jobs_before(b - 1) + J_FULL - J_NEXT if False else 0)
                        nc.scalar.copy(oT_raw[:, :], bank[6][:, 0:TP]).then_inc(oT_copied, 1)
                    for i, (at, name, j) in enumerate(jobs):
                        if at == s:
                            act_side(b, i, name, j)

            act_body(-1, False, False, True)
            act_body(0, True, False, True)
            with act.Fori(1, B - 1) as b:
                act_body(b, True, True, True)
            act_body(B - 1, True, True, False)
            act_body(B, False, True, False)

            act.wait_ge(top_shifted, 1)
            f(all_top[:, :, :], all_top[:, :, :], ACT.Exp).then_inc(top_exp, 1)

            PAIRS = (FC + 1) // 2

            def act_tile(j, s):
                for c in range(PAIRS):
                    full = 2 * c + 1 < FC
                    act.wait_ge(up_ps, PAIRS * j + c + 1)
                    wait(act, gated_ready, PAIRS * j + c - 1)
                    if full:
                        ins = f(act_a[:, c % 2, :], bank[c % 2][:, :], ACT.Silu)
                    else:
                        ins = f(act_a[0:F_LAST, c % 2, 0:GT], bank[c % 2][0:F_LAST, 0:GT], ACT.Silu)
                    ins.then_inc(act_ready, 1)
                act.wait_ge(y_ps, j + 1)
                wait(act, yT_ps, j - 1)
                nc.scalar.copy(yT[:, s, :], bank[4 + s][:, 0:GT]).then_inc(y_sb, 1)
            act_tile(0, 0)
            act_tile(1, 1)
            with act.Fori(1, (ROUTED + SHARED) // 2) as i:
                for s in range(2):
                    act_tile(2 * i + s, s)

        @block.vector
        def _(dve):
            v = nc.vector
            step = Steps(dve, dve_step)

            def norm_stats(srcs):
                for t, src in enumerate(srcs):
                    step.did(v.bn_stats(stats[:, t, :], src))
                step.settle(dve_gate)
                for t in range(NT):
                    ins = v.bn_aggr(mv[:, t, :], stats[:, t, :])
                    if t == NT - 1:
                        ins.then_inc(var_ready, 1)

            def normalise(dst, srcs, n, sem_):
                dve.wait_ge(rstd_ready, n + 1)
                for t, src in enumerate(srcs):
                    ins = v.tensor_scalar(dst[:, t, :], src, mv[:, t, 0:1], rstd[:, t:t + 1], ALU.subtract, ALU.mult)
                    if sem_ is None:
                        step.did(ins)
                if sem_ is not None:
                    ins.then_inc(sem_, 1)

            def dve_mixer(b):
                dve.wait_ge(conv_sb, 3 * b + 2)
                step.did(v.scalar_tensor_tensor(out=fz[:, :], in0=gates[:, 1, :], scalar=1.0, in1=gates[:, 0, :],
                                                op0=ALU.subtract, op1=ALU.mult))
                step.settle()
                step.did(v.tensor_tensor_scan(cell[:, :], gates[:, 1, :], fz[:, :], 0.0, ALU.mult, ALU.subtract))
                step.settle()
                dve.wait_ge(conv_sb, 3 * b + 3)
                v.tensor_tensor(hT[:, 0:T], cell[:, :], gates[:, 2, :], ALU.mult).then_inc(hT_ready, 1)
                dve.wait_ge(h_ps, b + 1)
                h_rows = [bank[4][:, t * P:(t + 1) * P] for t in range(NT)]
                x1_rows = [x1[:, t, :] for t in range(NT)]
                norm_stats(h_rows)
                normalise(x1, h_rows, 2 * b, None)
                step.settle()
                norm_stats(x1_rows)
                wait(dve, hx_done, b)
                v.tensor_tensor(hx_part[:, :], bank[4][:, 0:TP], x1[:, :, :].rearrange("p t d -> p (t d)"), ALU.add).then_inc(hx_ready, 1)
                wait(dve, n2_ps, b)
                normalise(n2, x1_rows, 2 * b + 1, n2_ready)
            dve.wait_ge(consts_ready, 1)
            dve.wait_ge(setup_sb, 9)
            PER = 2 + 3 + 3 + 3
            with dve.Fori(0, B) as b:
                step.enter(b, PER)
                dve_mixer(b)
            step.leave(B, PER)

            mi = bank[7]

            def dve_side(b, i, name):
                n = jobs_before(b) + i
                if name not in ("v", "rt", "rb", "wo", "gate", "count"):
                    return
                dve.wait_ge(misc_ps, n + 1)
                if name == "v":
                    wait(dve, v_diag_ready, NH * (b + 1))
                    v.tensor_tensor(v_rows[:, :, :], mi[:, 0:TP].rearrange("p (t d) -> p t d", t=NT),
                                    bv_row[:, :].unsqueeze(1).to_broadcast([P, NT, D]), ALU.add).then_inc(v_ready, 1)
                    dve.wait_ge(v_ready, b + 2)
                    v.memset(dve_done[:, :], 0.0).then_inc(misc_free, 1)
                elif name == "rt":
                    v.tensor_copy(inv_T[:, :], mi[0:NH, 0:TP]).then_inc(misc_free, 1)
                elif name == "rb":
                    dve.wait_ge(oT_copied, b)
                    v.tensor_tensor(oT[:, :], oT_raw[:, :], mi[:, 0:TP], ALU.mult).then_inc(misc_free, 1)
                elif name == "wo":
                    wait(dve, h2_kept, 4 * (b - 1))
                    wait(dve, x2_stored, 16 * (b - 1))
                    wait(dve, scattered, 16 * NT * TOPK * (b - 1))
                    v.tensor_tensor(h2[:, :, :].rearrange("p t d -> p (t d)"), mi[:, 0:TP],
                                    HX[:, bass.ds(b - 1, 1), :].rearrange("p o d -> p (o d)"), ALU.add).then_inc(misc_free, 1)
                    dve.wait_ge(misc_free, n + 1)
                    rows = [h2[:, t, :] for t in range(NT)]
                    norm_stats(rows)
                    normalise(x2, rows, 2 * B + b - 1, x2_ready)
                elif name == "gate":
                    v.tensor_tensor(logits[:, :, :], mi[:, 0:NT * E].rearrange("p (t e) -> p t e", t=NT),
                                    rb_row[:, :].unsqueeze(1).to_broadcast([P, NT, E]), ALU.add).then_inc(misc_free, 1)
                    wait(dve, misc_free, n + 1, dve_gate)
                    for t in range(NT):
                        step.did(v.max(top_v[:, t, :], logits[:, t, :]))
                    step.settle(dve_gate)
                    for t in range(NT):
                        step.did(v.max_index(top_i[:, t, :], top_v[:, t, :], logits[:, t, :]))
                    step.settle()
                    step.did(v.tensor_copy(top_f[:, :, :], top_i[:, :, 0:TOPK]))
                    step.settle()
                    flat = top_f[:, :, :].rearrange("p t k -> p (t k)")
                    step.did(v.tensor_tensor(onehot[:, :, :], flat.unsqueeze(2).to_broadcast([P, NT * TOPK, E]),
                                             iota_e[:, :].unsqueeze(1).to_broadcast([P, NT * TOPK, E]), ALU.is_equal))
                    step.settle()
                    step.did(v.tensor_tensor(onehot[:, :, :], onehot[:, :, :],
                                             valid[:, :].unsqueeze(2).to_broadcast([P, NT * TOPK, E]), ALU.mult))
                    step.settle()
                    v.tensor_reduce(chosen[:, :, :], onehot[:, :, :].rearrange("p (t k) e -> p t e k", t=NT), AX.X,
                                    ALU.add).then_inc(chosen_ready, 1)
                elif name == "count":
                    for t in range(NT):
                        step.did(v.tensor_tensor(before[:, t + 1, :], before[:, t, :], mi[:, (NT + t) * E:(NT + t + 1) * E], ALU.add))
                        step.settle()
                    step.did(v.tensor_tensor(place[:, :, :], before[:, 0:NT, :], mi[:, 0:NT * E].rearrange("p (t e) -> p t e", t=NT), ALU.add))
                    step.settle()
                    v.tensor_copy(before[:, 0, :], before[:, NT, :]).then_inc(misc_free, 1)
                    dve.wait_ge(misc_free, n + 1)
                    step.did(v.tensor_tensor(place[:, :, :], place[:, :, :], region_e[:, :].unsqueeze(1).to_broadcast([P, NT, E]), ALU.add))
                    step.settle()
                    step.did(v.tensor_tensor(picked[:, :, :].rearrange("p (t k) e -> p t k e", t=NT),
                                             onehot[:, :, :].rearrange("p (t k) e -> p t k e", t=NT),
                                             place[:, :, :].unsqueeze(2).to_broadcast([P, NT, TOPK, E]), ALU.mult))
                    step.settle()
                    step.did(v.tensor_reduce(slot_f[:, :], picked[:, :, :], AX.X, ALU.add))
                    step.settle()
                    step.did(v.tensor_tensor(slot_f[:, :], slot_f[:, :], dump_rows[:, :], ALU.add))
                    step.settle()
                    v.tensor_copy(slot_i[:, :], slot_f[:, :]).then_inc(slot_ready, 1)

            dve_done = sb("dve_done", [P, 1])

            def dve_body(b, att, prev, nxt):
                jobs = side_jobs(prev, nxt)
                started = not (isinstance(b, int) and b <= 0)
                for s in range(UNITS + 2):
                    u = UNITS * b + s
                    h, t = s // NT, s % NT
                    if s == 0 and prev:
                        dve.wait_ge(probs_ready, UNITS * b)
                        v.reciprocal(inv_rowsum[:, :], rowsum[:, :]).then_inc(inv_ready, 1)
                    if att and s < UNITS:
                        dve.wait_ge(content_ps, u + 1)
                        if t == 0:
                            dve.wait_ge(pos_read[h % 4], 16 * NT * (2 * b + h // 4 + 1))
                        wait(dve, probs_ready, u - 1, dve_gate)
                        v.tensor_tensor_reduce(out=score[:, s % 2, :], in0=bank[s % 2][:, 0:T], in1=pos_in[:, h % 4, t, :],
                                               scale=1.0, scalar=3.0e38, op0=ALU.add, op1=ALU.min,
                                               accum_out=least[:, s % 2:s % 2 + 1]).then_inc(scored, 1)
                    if (att and 1 <= s < UNITS) or (s == 0 and started):
                        hh, tt = (s - 1) // NT % NH, (s - 1) % NT
                        dve.wait_ge(probsT_ps, u)
                        if tt == 0:
                            wait(dve, av_done, (u - 1 - tt) // NT - 1 if isinstance(u, int) else NH * b + hh - 1)
                        v.tensor_copy(probsT[:, hh % 2, :, tt * P:(tt + 1) * P],
                                      bank[4 + (s + 1) % 2][:, 0:TP].rearrange("p (c q) -> p c q", c=NT)).then_inc(probsT_sb, 1)
                    for i, (at, name, j) in enumerate(jobs):
                        if at == s:
                            dve_side(b, i, name)

            PER = 3 + 3 + 3 + 3 + 4 + 4 + 3 - 3 + 0
            dve_body(-1, False, False, True)
            dve_body(0, True, False, True)
            with dve.Fori(1, B - 1) as b:
                step.enter(b - 1, DVE_PER_BATCH)
                dve_body(b, True, True, True)
            step.leave(B - 2, DVE_PER_BATCH)
            dve_body(B - 1, True, True, False)
            dve_body(B, False, True, False)

            def chain(ins):
                step.did(ins)
                step.settle()
            total_e = before[:, 0, :]
            chain(v.tensor_scalar(count_i[:, :], total_e, float(GT - 1), None, ALU.add))
            chain(v.tensor_scalar(count_i[:, :], count_i[:, :], GT.bit_length() - 1, None, ALU.logical_shift_right))
            chain(v.tensor_copy(tiles_f[:, :], count_i[:, :]))
            chain(v.tensor_tensor_scan(tiles_end[:, :], ones[:, 0:E], tiles_f[:, :], 0.0, ALU.mult, ALU.add))
            chain(v.tensor_tensor(tiles_f[:, :], tiles_end[:, :], tiles_f[:, :], ALU.subtract))
            chain(v.scalar_tensor_tensor(out=shift_e[:, :], in0=tiles_f[:, :], scalar=-float(GT), in1=region_e[:, :],
                                         op0=ALU.mult, op1=ALU.add))
            chain(v.tensor_tensor(pad_row[:, :], before[0:1, 0, :], region_e[0:1, :], ALU.add))
            tiles3 = iota_tile[:, :].unsqueeze(2).to_broadcast([1, 64, E])
            chain(v.tensor_tensor(tile_cmp[:, :, :], tiles3, tiles_end[0:1, :].unsqueeze(1).to_broadcast([1, 64, E]), ALU.is_ge))
            chain(v.tensor_reduce(tile_e[:, :], tile_cmp[:, :, :], AX.X, ALU.add))
            chain(v.tensor_scalar(table[:, 0, :], tile_e[:, :], float(E - 1), None, ALU.min))
            chain(v.tensor_tensor(tile_cmp[:, :, :], tile_e[:, :].unsqueeze(2).to_broadcast([1, 64, E]),
                                  iota_e[0:1, :].unsqueeze(1).to_broadcast([1, 64, E]), ALU.is_equal))
            chain(v.tensor_tensor(tile_cmp[:, :, :], tile_cmp[:, :, :], shift_e[0:1, :].unsqueeze(1).to_broadcast([1, 64, E]), ALU.mult))
            chain(v.tensor_reduce(tile_row[:, :], tile_cmp[:, :, :], AX.X, ALU.add))
            chain(v.scalar_tensor_tensor(out=tile_row[:, :], in0=iota_tile[:, :], scalar=float(GT), in1=tile_row[:, :],
                                         op0=ALU.mult, op1=ALU.add))
            chain(v.tensor_scalar(tile_fix[:, :], tile_row[:, :], -1.0, float(ZERO_ROW), ALU.mult, ALU.add))
            chain(v.tensor_scalar(tile_e[:, :], tile_e[:, :], float(E), None, ALU.is_ge))
            chain(v.tensor_tensor(tile_fix[:, :], tile_fix[:, :], tile_e[:, :], ALU.mult))
            v.tensor_tensor(table[:, 1, :], tile_row[:, :], tile_fix[:, :], ALU.add).then_inc(table_ready, 1)

            dve.wait_ge(h2_kept, 4 * B)
            v.tensor_tensor(all_weight[:, :, :], all_top[:, :, :], all_top[:, :, 0:1].to_broadcast([P, NTILES, TOPK]),
                            ALU.subtract).then_inc(dve_step, 1)
            step.n += 1
            step.settle()
            v.tensor_copy(all_top[:, :, :], all_weight[:, :, :]).then_inc(top_shifted, 1)
            dve.wait_ge(top_exp, 1)
            chain(v.tensor_reduce(weight_sum[:, :], all_top[:, :, :], AX.X, ALU.add))
            chain(v.reciprocal(weight_sum[:, :], weight_sum[:, :]))
            chain(v.tensor_tensor(all_weight[:, :, :], all_top[:, :, :], weight_sum[:, :].unsqueeze(2).to_broadcast([P, NTILES, TOPK]), ALU.mult))
            flat_e = all_expert[:, :, :].rearrange("p t k -> p (t k)")
            flat_s = all_slot[:, :, :].rearrange("p t k -> p (t k)")
            for half in range(NTILES * TOPK // (NT * TOPK)):
                part = slice(half * NT * TOPK, (half + 1) * NT * TOPK)
                chain(v.tensor_tensor(picked[:, :, :], flat_e[:, part].unsqueeze(2).to_broadcast([P, NT * TOPK, E]),
                                      iota_e[:, :].unsqueeze(1).to_broadcast([P, NT * TOPK, E]), ALU.is_equal))
                chain(v.tensor_tensor(picked[:, :, :], picked[:, :, :], shift_e[:, :].unsqueeze(1).to_broadcast([P, NT * TOPK, E]), ALU.mult))
                chain(v.tensor_reduce(top_f[:, :, :].rearrange("p t k -> p (t k)"), picked[:, :, :], AX.X, ALU.add))
                chain(v.tensor_tensor(flat_s[:, part], flat_s[:, part], top_f[:, :, :].rearrange("p t k -> p (t k)"), ALU.subtract))
            v.tensor_scalar(y_index[:, :, :].rearrange("p t k -> p (t k)"), flat_s, float(ROUTED * GT - 1), None, ALU.min).then_inc(weights_ready, 1)

            PAIRS = (FC + 1) // 2

            def copy_xT(j, s):
                dve.wait_ge(xe_ps, j + 1)
                wait(dve, y_ps, j - 1)
                v.tensor_copy(xeT[:, s, :], bank[6][:, 0:GT]).then_inc(xe_sb, 1)

            def copy_y(j, s, stored):
                dve.wait_ge(yT_ps, j + 1)
                wait(dve, y_stored[s], stored)
                v.tensor_copy(y_rows[:, s, :, :].rearrange("p t d -> p (t d)"), bank[7][:, 0:GT]).then_inc(y_rows_ready, 1)

            def dve_tile(j, s, nxt, prv, stored):
                for c in range(PAIRS):
                    full = 2 * c + 1 < FC
                    dve.wait_ge(act_ready, PAIRS * j + c + 1)
                    rows, w = (P, 2 * GT) if full else (F_LAST, GT)
                    if c >= 2 or not (isinstance(j, int) and j == 0):
                        wait(dve, up_ps, PAIRS * j + c + 1)
                    if c == 0:
                        wait(dve, y_ps, j)
                    v.tensor_tensor(gated[0:rows, c % 2, 0:w], act_a[0:rows, c % 2, 0:w], bank[2 + c % 2][0:rows, 0:w],
                                    ALU.mult).then_inc(gated_ready, 1)
                    if c == 2 and nxt:
                        copy_xT(j + 1, 1 - s)
                    if c == 3 and prv:
                        copy_y(j - 1, 1 - s, stored)
            copy_xT(0, 0)
            dve_tile(0, 0, True, False, 0)
            dve_tile(1, 1, True, True, 0)
            with dve.Fori(1, (ROUTED + SHARED) // 2 - 1) as i:
                for s in range(2):
                    dve_tile(2 * i + s, s, True, True, 16 * (i - 1 + s))
            N2 = (ROUTED + SHARED) // 2
            dve_tile(2 * N2 - 2, 0, True, True, 16 * (N2 - 2))
            dve_tile(2 * N2 - 1, 1, False, True, 16 * (N2 - 1))
            copy_y(2 * N2 - 1, 1, 16 * (N2 - 1))

            def combine(b, s, n):
                dve.wait_ge(shared_loaded[s], 16 * n)
                dve.wait_ge(gather_done[s], 16 * NT * TOPK * n)
                tot = total[:, bass.ds(b, 1), :].rearrange("p o d -> p (o d)")
                step.did(v.tensor_tensor(shared_in[:, s, :], shared_in[:, s, :], H2[:, bass.ds(b, 1), :].rearrange("p o d -> p (o d)"), ALU.add))
                step.settle()
                for k in range(TOPK):
                    for t in range(NT):
                        dst = shared_in[:, s, t * D:(t + 1) * D]
                        step.did(v.scalar_tensor_tensor(out=dst, in0=gathered[:, s, t * TOPK + k, :],
                                                        scalar=all_weight[:, bass.ds(b * NT + t, 1), k], in1=dst,
                                                        op0=ALU.mult, op1=ALU.add))
                    step.settle()
                v.tensor_copy(tot, shared_in[:, s, :]).then_inc(combined, 1)
            PER = 2 * (1 + NT * TOPK)
            with dve.Fori(0, B // 2) as i:
                step.enter(i, PER)
                for s in range(2):
                    combine(2 * i + s, s, i + 1)
            step.leave(B // 2, PER)


DVE_PER_BATCH = 3 + (3 + 3 + 1 + 1 + 1) + (3 + 1 + 1 + 1 + 1 + 1)


def kernel(**inputs):
    import concourse.bacc as bacc
    from concourse.bass_utils import run_bass_kernel_spmd as run

    nc = bacc.Bacc("TRN2", target_bir_lowering=False, num_devices=1)
    arrays, aps = {}, {}
    for name, value in inputs.items():
        short = name.removeprefix("L0_")
        arrays[f"in_{short}"] = np.ascontiguousarray(value)
        v = arrays[f"in_{short}"]
        aps[short] = nc.dram_tensor(f"in_{short}", v.shape, mybir.dt.from_np(v.dtype), kind="ExternalInput").ap()
    out = nc.dram_tensor("out", (B, T, D), F32, kind="ExternalOutput").ap()
    build(nc, aps, out)
    r = run(nc, [arrays], core_ids=[0])
    return r.results[0]["out"]
```

```python
from contextlib import ExitStack

import numpy as np

import concourse.bass as bass
from concourse import mybir

F32 = mybir.dt.float32
F32R = mybir.dt.float32r
I32 = mybir.dt.int32
U32 = mybir.dt.uint32
ALU = mybir.AluOpType
ACT = mybir.ActivationFunctionType
AX = mybir.AxisListType

P = 128
B = 8
T_IN = 375
T = T_IN - 1
NT = 3
TP = NT * P
T_LAST = T - (NT - 1) * P
X_LAST = T_IN - (NT - 1) * P
D = 128
NH = 8
HD = D // NH
NPAIR = NH // 2
NPOS = 511
POSW = NPOS + 1
E = 16
TOPK = 4
F = 1365
FC = (F + P - 1) // P
F_LAST = F - (FC - 1) * P
EPS = 1e-5
UNITS = NH * NT
NTILES = B * NT

GT = 2 * P
ROUTED = (B * T * TOPK + E * (GT - 1)) // GT
ROUTED += ROUTED % 2
SHARED = NTILES * P // GT
READ, LOW = 4, 1
PAIRS = (FC + 1) // 2
ROW = D + 16
AT_W, AT_E, AT_ID = D, D + TOPK, D + 2 * TOPK
REGION = -(-(B * T + GT) // GT) * GT
ZERO_ROW = E * REGION
DUMP_ROW = ZERO_ROW + GT
XG_ROWS = DUMP_ROW + NT * P * TOPK
F_PAD = -(-F // 8) * 8


def parts_of(piece):
    if piece < 4:
        half = (F + 1) // 2
        return [(P, slice(0, half) if piece % 2 == 0 else slice(half, F))]
    half = (FC + 1) // 2 * D
    if piece == 4:
        return [(P, slice(0, half))]
    return [(P, slice(half, (FC - 1) * D)), (F_LAST, slice((FC - 1) * D, FC * D))]



class Steps:

    def __init__(self, engine, sem, alone=None):
        self.engine, self.sem, self.alone, self.base, self.n = engine, sem, alone, 0, 0

    def did(self, instruction):
        instruction.then_inc(self.sem, 1)
        self.n += 1

    def settle(self, alone=None):
        wait(self.engine, self.sem, self.base + self.n, alone or self.alone)

    def enter(self, i, per_turn):
        self.outer = self.base + self.n
        self.base, self.n = self.outer + i * per_turn, 0

    def leave(self, turns, per_turn):
        assert self.n == per_turn, (self.n, per_turn)
        self.base, self.n = self.outer + turns * per_turn, 0


def wait(engine, sem, value, alone=None):
    if not (isinstance(value, int) and value <= 0):
        engine.wait_ge(sem, value)
        if alone is not None and not isinstance(value, int):
            engine.sem_inc(alone, 1)


POS_TWICE = (10, 13, 16, 19)
POS_AT = {s: [s - 4 + sum(s > t for t in POS_TWICE) + i for i in range(2 if s in POS_TWICE else 1)] for s in range(4, 24)}


def side_jobs(prev, nxt):
    jobs = []
    if nxt:
        jobs += [(0, "q", 0), (1, "k", 0), (2, "v", 0), (3, "sqv", 0), (6, "sk", 0), (7, "squ", 0), (8, "sqv", 1),
                 (10, "sqv", 2), (11, "sk", 1), (13, "squ", 1), (16, "sqv", 3), (17, "sk", 2), (19, "squ", 2),
                 (24, "sk", 3), (25, "squ", 3)]
    if prev:
        jobs += [(4, "rt", 0), (5, "rb", 0), (9, "wo", 0), (12, "x2t", 0), (14, "gate", 0), (18, "count", 0)]
    return sorted(jobs, key=lambda j: j[0])


J_NEXT, J_PREV = len(side_jobs(False, True)), len(side_jobs(True, False))
J_FULL = J_NEXT + J_PREV
LOOP = B - 3


def jobs_before(b):
    if isinstance(b, int) and b <= 0:
        return J_NEXT * (b + 1)
    if isinstance(b, int) and b == B:
        return 2 * J_NEXT + (B - 2) * J_FULL + J_PREV
    return 2 * J_NEXT + (b - 1) * J_FULL


def build(nc, a, out):
    ctx = ExitStack()
    with ctx:
        address = {}

        def sb(name, shape, dt=F32):
            address[name] = -(-nc.sbuf_base // 32) * 32
            return ctx.enter_context(nc.sbuf_tensor(name, shape, dt))

        def sem(name):
            return ctx.enter_context(nc.semaphore(name))

        bank = [ctx.enter_context(nc.psum_tensor(f"bank{i}", [P, 512], F32)) for i in range(8)]

        pos_dram = nc.dram_tensor("pos_scores", (NH, TP * POSW), F32).ap()
        xg_dram = nc.dram_tensor("dispatched_x", (XG_ROWS, ROW), F32).ap()
        xs_dram = nc.dram_tensor("shared_x", (NTILES * P, D), F32).ap()
        sum_dram = nc.dram_tensor("token_sums", (NTILES * P + GT, D), F32).ap()

        ident = sb("ident", [P, P])
        ones = sb("ones", [P, P])
        tri = sb("tri", [P, P])
        head_rows = sb("head_rows", [NH, D])
        template = sb("template", [P, 4, P])
        spread_q_hi = sb("spread_q_hi", [P, NPAIR, P], F32R)
        spread_q_lo = sb("spread_q_lo", [P, NPAIR, P], F32R)
        spread_k_hi = sb("spread_k_hi", [P, NPAIR, P], F32R)
        spread_k_lo = sb("spread_k_lo", [P, NPAIR, P], F32R)
        iota_e = sb("iota_e", [P, E])
        region_e = sb("region_e", [P, E])
        iota_tile = sb("iota_tile", [P, 64])
        valid = sb("valid", [P, NT * TOPK])
        dump_rows = sb("dump_rows", [P, NT * TOPK])
        minus_half = sb("minus_half", [P, NT])
        pad_rows = sb("pad_rows", [P, 2, ROW])
        ids_f = sb("ids_f", [P, NT])
        arena = sb("arena", [P, 4 * F_PAD])
        used = [0]

        def early(shape):
            n = int(np.prod(shape[1:]))
            flat = arena[:, used[0]:used[0] + n]
            used[0] += n
            if len(shape) == 2:
                return flat
            return flat.rearrange("p (a b) -> p a b", a=shape[1])

        gate_raw = early([P, 3, 2 * D])
        att_raw = early([P, 5, D])
        pos_raw = early([P, 4, D])
        wT = sb("wT", [P, 11, P])
        posT = sb("posT", [P, 512])
        cols = sb("cols", [P, 9])
        qbias = sb("qbias", [P, 2])
        bv_row = sb("bv_row", [P, D])
        bo_row = sb("bo_row", [P, D])
        rb_row = sb("rb_row", [P, E])
        gate_w = sb("gate_w", [P, E])
        hnT = sb("hnT", [P, B * TP])
        HX = sb("HX", [P, B, TP])
        H2 = sb("H2", [P, B, TP])
        p_stack = sb("p_stack", [P, NPAIR, 512], F32R)
        x_in = early([P, NT, D])
        xT = early([P, T_IN + 1])
        gates = early([P, 3, T])
        fz = early([P, T])
        cell = early([P, T])
        hT = early([P, TP])
        stats = sb("stats", [P, NT, 6])
        mv = sb("mv", [P, NT, 2])
        vareps = sb("vareps", [P, NT])
        rstd = sb("rstd", [P, NT])
        x1 = sb("x1", [P, NT, D])
        n2 = sb("n2", [P, NT, D])
        hx_part = early([P, TP])
        hnb = sb("hnb", [P, TP])
        t_qu = sb("t_qu", [P, TP])
        t_qv = sb("t_qv", [P, TP])
        t_k = sb("t_k", [P, 512])
        hi_qu, lo_qu = sb("hi_qu", [P, TP], F32R), sb("lo_qu", [P, TP], F32R)
        hi_qv, lo_qv = sb("hi_qv", [P, TP], F32R), sb("lo_qv", [P, TP], F32R)
        hi_k, lo_k = sb("hi_k", [P, 512], F32R), sb("lo_k", [P, 512], F32R)
        qu_stack = sb("qu_stack", [P, NPAIR, TP], F32R)
        qv_stack = sb("qv_stack", [P, NPAIR, TP], F32R)
        k_stack = sb("k_stack", [P, NPAIR, TP], F32R)
        v_rows = sb("v_rows", [P, NT, D])
        v_diag = sb("v_diag", [P, NT, NH, D])
        pos_out = sb("pos_out", [P, 2, NT, POSW])
        pos_in = sb("pos_in", [P, 4, NT, T])
        score = sb("score", [P, 2, T])
        least = sb("least", [P, 2])
        probs = sb("probs", [P, 2, TP])
        rowsum = sb("rowsum", [P, UNITS])
        inv_rowsum = sb("inv_rowsum", [P, UNITS])
        probsT = sb("probsT", [P, 2, NT, TP])
        oT_raw = sb("oT_raw", [P, TP])
        inv_T = sb("inv_T", [NH, TP])
        oT = sb("oT", [P, TP])
        h2 = sb("h2", [P, NT, D])
        x2_row = sb("x2_row", [P, NT, ROW])
        x2 = x2_row[:, :, 0:D]
        x2T = sb("x2T", [P, TP])
        logits = sb("logits", [P, NT, E])
        top_v = sb("top_v", [P, NT, 8])
        top_i = sb("top_i", [P, NT, 8], U32)
        top_f = sb("top_f", [P, NT, TOPK])
        onehot = sb("onehot", [P, NT * TOPK, E])
        picked = sb("picked", [P, NT * TOPK, E])
        chosen = sb("chosen", [P, NT, E])
        before = sb("before", [P, NT + 1, E])
        place = sb("place", [P, NT, E])
        slot_f = sb("slot_f", [P, NT * TOPK])
        slot_i = sb("slot_i", [P, NT * TOPK], I32)
        shifted_v = sb("shifted_v", [P, NT, TOPK])
        exp_v = sb("exp_v", [P, NT, TOPK])
        exp_sum = sb("exp_sum", [P, NT])
        count_i = sb("count_i", [P, E], I32)
        tiles_f = sb("tiles_f", [P, E])
        tiles_end = sb("tiles_end", [P, E])
        shift_e = sb("shift_e", [P, E])
        pad_row = sb("pad_row", [1, E], I32)
        tile_e = sb("tile_e", [P, 64])
        tile_row = sb("tile_row", [1, 64])
        tile_fix = sb("tile_fix", [1, 64])
        table = sb("table", [1, 2, 64], I32)
        tile_expert = sb("tile_expert", [P, 1])
        same = sb("same", [P, 2, TOPK])
        row_weight = sb("row_weight", [P, 2, 2])
        row_id = sb("row_id", [P, 2, 2], I32)
        y_rows = sb("y_rows", [P, 2, 2, D])

        assert used[0] <= 4 * F_PAD

        F3 = FC * D

        def over(host, floats, name, shape, dt=F32):
            return nc.alloc_sbuf_tensor_at(name, shape, dt, offset=address[host] + 4 * floats)

        raw1 = [over("arena", i * F_PAD, f"raw1_{i}", [P, F]) for i in range(2)]
        raw2 = [over("arena", (2 + i) * F_PAD, f"raw2_{i}", [P, F]) for i in range(2)]
        raw3 = [over("v_diag", i * F3, f"raw3_{i}", [P, F3]) for i in range(2)]
        hi1 = [over(n, 0, f"hi1_{n}", [P, F], F32R) for n in ("qu_stack", "k_stack")]
        hi2 = [over(n, 0, f"hi2_{n}", [P, F], F32R) for n in ("qv_stack", "p_stack")]
        hi3 = [over("pos_out", i * F3, f"hi3_{i}", [P, F3], F32R) for i in range(2)]
        lo1 = [over(n, 0, f"lo1_{n}", [P, F], F32R) for n in ("hnT", "HX")]
        lo2 = [over(n, F_PAD, f"lo2_{n}", [P, F], F32R) for n in ("hnT", "HX")]
        lo3 = [over("pos_in", i * F3, f"lo3_{i}", [P, F3], F32R) for i in range(2)]
        act_a = over("pos_in", 2 * F3, "act_a", [P, 2, 2 * GT])
        xe = over("pos_in", 2 * F3 + 4 * GT, "xe", [P, 2, 2, ROW])
        x_hi = over("spread_q_hi", 0, "x_hi", [P, 2, GT], F32R)
        x_lo = over("spread_q_lo", 0, "x_lo", [P, 2, GT], F32R)
        product = over("wT", 0, "product", [P, 2, 2 * GT])
        tile_cmp = over("wT", 0, "tile_cmp", [P, 64, E])
        g_hi = over("probsT", 0, "g_hi", [P, 2, 2 * GT], F32R)
        g_lo = over("probsT", 4 * GT, "g_lo", [P, 2, 2 * GT], F32R)
        yT = over("posT", 0, "yT", [P, 2, GT])
        H2_flat = H2[:, :, :].rearrange("p b d -> p (b d)")

        weights_in = sem("weights_in")
        pool_step, dve_step, act_step = sem("pool_step"), sem("dve_step"), sem("act_step")
        pool_gate, dve_gate, sp_gate = sem("pool_gate"), sem("dve_gate"), sem("sp_gate")
        consts_ready = sem("consts_ready")
        setup_ps, setup_sb = sem("setup_ps"), sem("setup_sb")
        x_loaded = sem("x_loaded")
        xT_ps, xT_sb = sem("xT_ps"), sem("xT_sb")
        conv_ps, conv_sb = sem("conv_ps"), sem("conv_sb")
        hT_ready, h_ps = sem("hT_ready"), sem("h_ps")
        var_ready, rstd_ready = sem("var_ready"), sem("rstd_ready")
        n2_ready, n2_ps, hn_ready = sem("n2_ready"), sem("n2_ps"), sem("hn_ready")
        hx_ready, hx_done = sem("hx_ready"), sem("hx_done")
        misc_ps, misc_free = sem("misc_ps"), sem("misc_free")
        hnb_ready = sem("hnb_ready")
        t_ready, split_ready = sem("t_ready"), sem("split_ready")
        v_diag_ready = sem("v_diag_ready")
        pos_ps, pos_sb = sem("pos_ps"), sem("pos_sb")
        pos_written = [sem(f"pos_written{i}") for i in range(2)]
        pos_read = [sem(f"pos_read{i}") for i in range(4)]
        content_ps, scored, probs_ready = sem("content_ps"), sem("scored"), sem("probs_ready")
        probsT_ps, probsT_sb, av_done = sem("probsT_ps"), sem("probsT_sb"), sem("av_done")
        inv_ready, oT_copied = sem("inv_ready"), sem("oT_copied")
        h2_ready, x2_ready, h2_kept = sem("h2_ready"), sem("x2_ready"), sem("h2_kept")
        x2_stored, chosen_ready = sem("x2_stored"), sem("chosen_ready")
        slot_ready, scattered = sem("slot_ready"), sem("scattered")
        table_ready, pads_written = sem("table_ready"), sem("pads_written")
        shift_ready, exp_ready = sem("shift_ready"), sem("exp_ready")
        zeroed = sem("zeroed")
        w_loaded = [sem(f"w_loaded{i}") for i in range(2)]
        w_hi_ready = sem("w_hi_ready")
        w1_lo_ready = sem("w1_lo_ready")
        w23_lo_ready = sem("w23_lo_ready")
        xe_loaded = [sem(f"xe_loaded{i}") for i in range(2)]
        xe_ps, x_hi_ready, x_ready = sem("xe_ps"), sem("x_hi_ready"), sem("x_ready")
        expert_ready, rows_known = sem("expert_ready"), sem("rows_known")
        a_ps, b_ps, down_ps = sem("a_ps"), sem("b_ps"), sem("down_ps")
        silu_ready, product_ready = sem("silu_ready"), sem("product_ready")
        g_hi_ready, g_lo_ready = sem("g_hi_ready"), sem("g_lo_ready")
        y_sb, yT_ps, y_rows_ready = sem("y_sb"), sem("yT_ps"), sem("y_rows_ready")
        y_stored, y_added, out_stored = sem("y_stored"), sem("y_added"), sem("out_stored")

        pos_rows = pos_dram.rearrange("h (s w) -> s h w", w=POSW)

        def shifted(h, t):
            base = pos_dram[h:h + 1, 0:TP * POSW]
            return bass.AP(base.tensor, base.offset + T + t * P * NPOS, [[NPOS, P], [1, T]])

        block = ctx.enter_context(nc.Block())
        N_SMALL = 3 + 5 + 2 + 9 + 4

        @block.sync
        def _(sp):
            for i, n in enumerate(["tok_W_z", "tok_W_f", "tok_W_o"]):
                sp.dma_start(gate_raw[:, i, :], a[n].rearrange("h d k -> h (d k)")).then_inc(weights_in, 16)
            for i, n in enumerate(["attn_Wq", "attn_Wk", "attn_Wv", "attn_Wo", "attn_Wp"]):
                sp.dma_start(att_raw[:, i, :], a[n]).then_inc(weights_in, 16)
            sp.dma_start(pos_raw[:, 0:3, :], a["attn_pos_emb"][0:3 * P, :].rearrange("(t p) d -> p t d", p=P)).then_inc(weights_in, 16)
            sp.dma_start(pos_raw[0:NPOS - 3 * P, 3, :], a["attn_pos_emb"][3 * P:NPOS, :]).then_inc(weights_in, 16)
            for i, n in enumerate(["tok_b_z", "tok_b_f", "tok_b_o", "attn_bq", "attn_bk", "attn_pos_bias_u",
                                   "attn_pos_bias_v", "attn_ln_w", "attn_ln_b"]):
                sp.dma_start(cols[:, i:i + 1], a[n].rearrange("(p o) -> p o", o=1)).then_inc(weights_in, 16)
            for dst, n in ((bv_row, "attn_bv"), (bo_row, "attn_bo"), (rb_row, "ffn_routing_bias")):
                src = a[n].rearrange("(o n) -> o n", o=1)
                sp.dma_start(dst[:, :], src.to_broadcast([P, src.shape[1]])).then_inc(weights_in, 16)
            sp.dma_start(gate_w[:, :], a["ffn_gate_w"]).then_inc(weights_in, 16)

            sp.wait_ge(consts_ready, 1)
            sp.dma_start(sum_dram[NTILES * P:NTILES * P + GT, :].rearrange("(t p) d -> p t d", p=P), pad_rows[:, :, 0:D]).then_inc(zeroed, 16)

            def load_x(b):
                wait(sp, xT_ps, b)
                sp.dma_start(x_in[:, 0:NT - 1, :], a["x"][bass.ds(b, 1), 0:(NT - 1) * P, :].rearrange(
                    "o (t p) d -> p (o t) d", p=P)).then_inc(x_loaded, 16)
                sp.dma_start(x_in[0:X_LAST, NT - 1, :], a["x"][bass.ds(b, 1), (NT - 1) * P:T_IN, :].rearrange(
                    "o p d -> (o p) d")).then_inc(x_loaded, 16)
            load_x(0)
            with sp.Fori(1, B) as b:
                load_x(b)

            def write_pos(b, h):
                wait(sp, pos_sb, UNITS * b + NT * h + NT, sp_gate)
                wait(sp, pos_read[h % 4], 16 * NT * (2 * b - 1 + h // 4))
                sp.dma_start(pos_rows[:, h, :].rearrange("(t p) w -> p t w", p=P), pos_out[:, h % 2, :, :]).then_inc(
                    pos_written[h % 2], 16)

            def read_pos(b, h):
                wait(sp, scored, UNITS * b + NT * (h - 3))
                wait(sp, pos_written[h % 2], 16 * (4 * b + h // 2 + 1))
                for t in range(NT):
                    sp.dma_start(pos_in[:, h % 4, t, :], shifted(h, t)).then_inc(pos_read[h % 4], 16)

            def sp_body(b, att, prev, nxt):
                order = []
                if nxt:
                    done = {m: s for s, ms in POS_AT.items() for m in ms}
                    order += [(done[NT * h + NT - 1] + 0.5, write_pos, b + 1, h) for h in range(NH)]
                if att:
                    order += [(NT * h + 2.2, read_pos, b, h + 4) for h in range(4)]
                if nxt:
                    order += [(NT * h + 2.2 if att else 23.6 + h, read_pos, b + 1, h - 4) for h in range(4, NH)]
                if prev:
                    order += [(12.1, None, b, 0)]
                for _, what, bb, h in sorted(order, key=lambda o: o[0]):
                    if what is not None:
                        what(bb, h)
                        continue
                    wait(sp, x2_ready, bb)
                    sp.dma_start(xs_dram[bass.ds((bb - 1) * TP, TP), :].rearrange("(t p) d -> p t d", p=P),
                                 x2).then_inc(x2_stored, 16)

            sp_body(-1, False, False, True)
            sp_body(0, True, False, True)
            with sp.Fori(1, 1 + LOOP) as b:
                sp_body(b, True, True, True)
            sp_body(B - 2, True, True, True)
            sp_body(B - 1, True, True, False)

            def load_weights(w, s, w1, w2, w3a, w3b):
                wait(sp, w1_lo_ready, 2 * (w - 1))
                sp.dma_start(raw1[s][:, :], w1).then_inc(w_loaded[s], 16)
                wait(sp, w23_lo_ready, 4 * (w - 2) + 2)
                sp.dma_start(raw2[s][:, :], w2).then_inc(w_loaded[s], 16)
                wait(sp, w23_lo_ready, 4 * (w - 1))
                sp.dma_start(raw3[s][:, 0:F3 - D].rearrange("p (c d) -> p c d", d=D), w3a).then_inc(w_loaded[s], 16)
                sp.dma_start(raw3[s][0:F_LAST, F3 - D:F3], w3b).then_inc(w_loaded[s], 16)

            def load_routed_weights(w, s):
                e = sp.value_load(table[0:1, 0, bass.ds(w - 1, 1)], min_val=0, max_val=E - 1)
                load_weights(w, s, a["ffn_w1"][bass.ds(e, 1), :, :].rearrange("o d f -> (o d) f"),
                             a["ffn_w2"][bass.ds(e, 1), :, :].rearrange("o d f -> (o d) f"),
                             a["ffn_w3"][bass.ds(e, 1), 0:(FC - 1) * P, :].rearrange("o (c p) d -> p (o c) d", p=P),
                             a["ffn_w3"][bass.ds(e, 1), (FC - 1) * P:F, :].rearrange("o p d -> (o p) d"))

            def load_shared_x(j, s):
                wait(sp, xe_ps, j - 1)
                sp.dma_start(xe[:, s, :, 0:D], xs_dram[bass.ds(j * GT, GT), :].rearrange("(t p) d -> p t d", p=P)).then_inc(xe_loaded[s], 16)

            def load_routed_x(r, s):
                wait(sp, xe_ps, r + SHARED - 1, sp_gate)
                wait(sp, rows_known, r - 1, sp_gate)
                row = sp.value_load(table[0:1, 1, bass.ds(r, 1)], min_val=0, max_val=ZERO_ROW)
                sp.dma_start(xe[:, s, :, :], xg_dram[bass.ds(row, GT), :].rearrange("(t p) d -> p t d", p=P)).then_inc(xe_loaded[s], 16)

            def store_y(j, s):
                sp.wait_ge(y_rows_ready, j + 1)
                sp.dma_start(sum_dram[bass.ds(j * GT, GT), :].rearrange("(t p) d -> p t d", p=P), y_rows[:, s, :, :]).then_inc(y_stored, 16)

            sp.wait_ge(hx_done, B)
            sp.wait_ge(av_done, NH * B)
            load_weights(0, 0, a["ffn_sw1"], a["ffn_sw2"],
                         a["ffn_sw3"][0:(FC - 1) * P, :].rearrange("(c p) d -> p c d", p=P), a["ffn_sw3"][(FC - 1) * P:F, :])
            sp_body(B, False, True, False)
            sp.wait_ge(x2_stored, 16 * B)
            load_shared_x(0, 0)
            load_shared_x(1, 1)
            load_shared_x(2, 0)
            load_shared_x(3, 1)
            store_y(0, 0)
            sp.wait_ge(table_ready, 1)
            sp.wait_ge(scattered, 16 * B * NT * TOPK)
            for e in range(E):
                row = sp.value_load(pad_row[0:1, e:e + 1], min_val=0, max_val=ZERO_ROW - GT)
                sp.dma_start(xg_dram[bass.ds(row, GT), :].rearrange("(t p) d -> p t d", p=P), pad_rows[:, :, :]).then_inc(pads_written, 16)
            sp.dma_start(xg_dram[ZERO_ROW:ZERO_ROW + GT, :].rearrange("(t p) d -> p t d", p=P), pad_rows[:, :, :]).then_inc(pads_written, 16)
            with sp.Fori(1, SHARED // 2 - 1) as i:
                for s in range(2):
                    load_shared_x(2 * i + s + 2, s)
                    store_y(2 * i + s - 1, 1 - s)
            sp.wait_ge(pads_written, 16 * (E + 1))
            for j in range(SHARED - 2, SHARED + 2):
                load_routed_weights(j - SHARED + 3, (j + 1) % 2)
                load_routed_x(j + 2 - SHARED, j % 2)
                if j <= SHARED:
                    store_y(j - 1, (j - 1) % 2)
            with sp.Fori(1, ROUTED // 2 - 1) as i:
                for s in range(2):
                    load_routed_weights(2 * i + s + 3, 1 - s)
                    load_routed_x(2 * i + s + 2, s)

            sp.wait_ge(y_added, 32 * ROUTED)
            for b in range(B):
                sp.dma_start(out[b, :, :], sum_dram[b * TP:b * TP + T, :]).then_inc(out_stored, 16)
            sp.wait_ge(out_stored, 16 * B)

        @block.gpsimd
        def _(pool):
            g = nc.gpsimd
            step = Steps(pool, pool_step, pool_gate)

            def pw(sem_, value):
                wait(pool, sem_, value, pool_gate)

            step.did(g.memset(ones[:], 1.0))
            step.did(g.memset(template[:], 0.0))
            step.did(g.memset(pad_rows[:, :, :], 0.0))
            step.did(g.memset(x2_row[:, :, :], 0.0))
            step.did(g.memset(v_diag[:, :, :, :], 0.0))
            step.settle()
            step.did(g.affine_select(out=ident[:], in_=ones[:], compare_op=ALU.is_equal, fill=0.0, base=0,
                                     pattern=[[-1, P]], channel_multiplier=1))
            step.did(g.affine_select(out=tri[:], in_=ones[:], compare_op=ALU.is_gt, fill=0.0, base=0,
                                     pattern=[[1, P]], channel_multiplier=-1))
            step.did(g.affine_select(out=head_rows[:], in_=ones[0:NH, :], compare_op=ALU.is_ge, fill=0.0, base=0,
                                     pattern=[[1, D]], channel_multiplier=-HD))
            for n, copies in enumerate(((0, 2), (1, 3), (0, 1), (2, 3))):
                tv = template[:, n, :].rearrange("p (i c f) -> p i c f", i=2, c=4)
                for c in copies:
                    step.did(g.memset(tv[:, :, c, :], 1.0))
            step.settle()
            step.did(g.affine_select(out=head_rows[:], in_=head_rows[:], compare_op=ALU.is_ge, fill=0.0, base=HD - 1,
                                     pattern=[[-1, D]], channel_multiplier=HD))
            for n, spread in enumerate((spread_q_hi, spread_q_lo, spread_k_hi, spread_k_lo)):
                for j in range(NPAIR):
                    step.did(g.affine_select(out=spread[:, j, :], in_=template[:, n, :], compare_op=ALU.is_equal, fill=0.0,
                                             base=-2 * HD * j, pattern=[[-HD, 2], [0, 4], [-1, HD]], channel_multiplier=1))
            step.did(g.iota(iota_e[:], pattern=[[1, E]], base=0, channel_multiplier=0, allow_small_or_imprecise_dtypes=True))
            step.did(g.iota(region_e[:], pattern=[[REGION, E]], base=0, channel_multiplier=0, allow_small_or_imprecise_dtypes=True))
            step.did(g.iota(iota_tile[:], pattern=[[1, 64]], base=0, channel_multiplier=0, allow_small_or_imprecise_dtypes=True))
            step.did(g.iota(dump_rows[:], pattern=[[P * TOPK, NT], [1, TOPK]], base=DUMP_ROW, channel_multiplier=TOPK,
                            allow_small_or_imprecise_dtypes=True))
            for t in range(2):
                step.did(g.iota(pad_rows[:, t, AT_ID:AT_ID + 1], pattern=[[1, 1]], base=NTILES * P + t * P, channel_multiplier=1,
                                allow_small_or_imprecise_dtypes=True))
            step.did(g.iota(ids_f[:], pattern=[[P, NT]], base=0, channel_multiplier=1, allow_small_or_imprecise_dtypes=True))
            step.did(g.memset(minus_half[:], -0.5))
            step.did(g.memset(before[:], 0.0))
            step.did(g.memset(hT[:, T:TP], 0.0))
            step.did(g.memset(probs[:, :, T:TP], 0.0))
            step.did(g.memset(pos_out[:, :, :, 0:1], 0.0))
            step.did(g.memset(posT[:, NPOS:512], 0.0))
            step.settle()
            step.did(g.affine_select(out=valid[:], in_=ones[:, 0:NT * TOPK], compare_op=ALU.is_gt, fill=0.0, base=T,
                                     pattern=[[-P, NT], [0, TOPK]], channel_multiplier=-1))
            step.did(g.affine_select(out=dump_rows[:], in_=dump_rows[:], compare_op=ALU.is_ge, fill=0.0, base=-T,
                                     pattern=[[P, NT], [0, TOPK]], channel_multiplier=1))
            step.settle()
            g.memset(vareps[:], 1.0).then_inc(consts_ready, 1)

            def inverse_root(n):
                pw(var_ready, n + 1)
                step.did(g.tensor_scalar_add(vareps[:], mv[:, :, 1], EPS))
                step.settle()
                g.tensor_tensor(rstd[:], vareps[:], minus_half[:], ALU.pow).then_inc(rstd_ready, 1)

            def pool_mixer(b):
                inverse_root(2 * b)
                inverse_root(2 * b + 1)
                pw(hx_ready, b + 1)
                g.tensor_tensor(HX[:, bass.ds(b, 1), :].rearrange("p o (t d) -> p (o t) d", d=D),
                                hx_part[:].rearrange("p (t d) -> p t d", d=D),
                                bo_row[:, :].unsqueeze(1).to_broadcast([P, NT, D]), ALU.add).then_inc(hx_done, 1)
            def split(sem_, n, t, hi, lo, w):
                pw(sem_, n)
                g.tensor_tensor(lo[:, 0:w], t[:, 0:w], hi[:, 0:w].bitcast(F32), ALU.subtract).then_inc(split_ready, 1)

            pw(weights_in, 16 * N_SMALL)
            split(t_ready, 1, t_k, hi_k, lo_k, 512)
            PER = 2
            with pool.Fori(0, B) as b:
                step.enter(b, PER)
                pool_mixer(b)
            step.leave(B, PER)

            def diag(b, h):
                pw(av_done, NH * (b - 1) + h + 1)
                g.tensor_copy(v_diag[:, :, h, h * HD:(h + 1) * HD], v_rows[:, :, h * HD:(h + 1) * HD]).then_inc(v_diag_ready, 1)

            def copy_hn(b):
                pw(misc_ps, jobs_before(b - 2) + 3) if not isinstance(b, int) or b >= 1 else None
                pw(hn_ready, b + 1)
                g.tensor_copy(hnb[:, :], hnT[:, bass.ds(b * TP, TP)]).then_inc(hnb_ready, 1)

            def split_low(w, s, piece):
                pw(w_hi_ready, 6 * w + piece + 1)
                raw, hi, lo = (raw2, hi2, lo2) if piece < 4 else (raw3, hi3, lo3)
                for rows, part in parts_of(piece):
                    ins = g.tensor_tensor(lo[s][0:rows, part], raw[s][0:rows, part], hi[s][0:rows, part].bitcast(F32), ALU.subtract)
                ins.then_inc(w23_lo_ready, 1)

            def pool_body(b, att, prev, nxt):
                started = not (isinstance(b, int) and b <= 0)
                if nxt:
                    pw(misc_ps, jobs_before(b) + 1)
                    split(t_ready, b + 3, t_qv, hi_qv, lo_qv, TP)
                    split(misc_free, jobs_before(b) + 1, t_qu, hi_qu, lo_qu, TP)
                    split(misc_free, jobs_before(b) + 2, t_k, hi_k, lo_k, TP)
                if att and started:
                    for h in range(NH - 3, NH):
                        diag(b, h)
                if prev:
                    inverse_root(2 * B + b - 1)
                if nxt and not (isinstance(b, int) and b >= B - 2):
                    copy_hn(b + 2)
                heads = list(range(NH - 3 if att else NH)) if nxt else []
                if nxt:
                    pw(misc_free, jobs_before(b) + 3)
                for h in heads[:3]:
                    diag(b + 1, h)
                if not att and prev:
                    for piece in range(2, 6):
                        split_low(0, 0, piece)
                if prev:
                    pw(slot_ready, b)
                    g.tensor_copy(H2[:, bass.ds(b - 1, 1), :].rearrange("p o (t d) -> p (o t) d", d=D), h2[:, :, :]).then_inc(h2_kept, 1)
                    for t in range(NT):
                        for k in range(TOPK):
                            c = t * TOPK + k
                            pool.indirect_dma_start(xg_dram[:, :], bass.IndirectOffsetOnAxis(slot_i[:, c:c + 1], 0),
                                                    x2_row[:, t, :], None).then_inc(scattered, 16)
                for h in heads[3:]:
                    diag(b + 1, h)

            PER = 1
            copy_hn(0)
            pool_body(-1, False, False, True)
            pool_body(0, True, False, True)
            with pool.Fori(1, 1 + LOOP) as b:
                step.enter(b - 1, PER)
                pool_body(b, True, True, True)
            step.leave(LOOP, PER)
            pool_body(B - 2, True, True, True)
            pool_body(B - 1, True, True, False)
            pool_body(B, False, True, False)

            def add_rows(r, s):
                pw(y_rows_ready, SHARED + r + 1)
                pw(y_added, 32 * r)
                for t in range(2):
                    pool.indirect_dma_start(sum_dram[:, :], bass.IndirectOffsetOnAxis(row_id[:, s, t:t + 1], 0),
                                            y_rows[:, s, t, :], None, compute_op=ALU.add).then_inc(y_added, 16)

            def pool_tile(r, s, split, add):
                for piece in (2, 3):
                    if split:
                        split_low(r + 2, s, piece)
                if split:
                    split_low(r + 2, s, 4)
                if add:
                    add_rows(r - 1, 1 - s)
                if split:
                    split_low(r + 2, s, 5)
            for piece in range(2, 6):
                split_low(1, 1, piece)
            pool_tile(0, 0, True, False)
            pw(y_stored, 16 * SHARED)
            pw(zeroed, 16)
            pool_tile(1, 1, True, True)
            with pool.Fori(1, ROUTED // 2 - 1) as i:
                for s in range(2):
                    pool_tile(2 * i + s, s, True, True)
            pool_tile(ROUTED - 2, 0, True, True)
            pool_tile(ROUTED - 1, 1, False, True)
            add_rows(ROUTED - 1, 1)

        @block.tensor
        def _(pe):
            mm, tr = nc.tensor.matmul, nc.tensor.transpose
            pe.wait_ge(weights_in, 16 * N_SMALL)
            pe.wait_ge(consts_ready, 1)
            raws = [gate_raw[:, i, :].rearrange("h (d k) -> h k d", k=2)[:, k, :] for i in range(3) for k in range(2)]
            raws += [att_raw[:, i, :] for i in range(5)]
            for n, raw in enumerate(raws):
                ins = tr(bank[n // 4][:, (n % 4) * P:(n % 4 + 1) * P], raw, ident[:])
                if n % 4 == 3 or n == len(raws) - 1:
                    ins.then_inc(setup_ps, 1)
            for t in range(4):
                rows = P if t < 3 else NPOS - 3 * P
                ins = tr(bank[3][:, t * P:t * P + rows], pos_raw[0:rows, t, :], ident[0:rows, 0:rows])
            ins.then_inc(setup_ps, 1)
            pe.wait_ge(setup_sb, 5)
            mm(bank[4][:, :], wT[:, 10, :], posT[:, :], start=True, stop=True).then_inc(setup_ps, 1)
            pe.wait_ge(split_ready, 1)
            for j in range(NPAIR):
                wait(pe, setup_sb, 5 + j)
                mm(bank[5][:, :], spread_k_hi[:, j, :], hi_k[:, :], start=True, stop=False)
                mm(bank[5][:, :], spread_k_lo[:, j, :], lo_k[:, :], start=False, stop=True).then_inc(setup_ps, 1)

            def pe_mixer(b):
                pe.wait_ge(x_loaded, 32 * b + 32)
                for t in range(NT):
                    rows = P if t < NT - 1 else X_LAST
                    ins = tr(bank[0][:, t * P:t * P + rows], x_in[0:rows, t, :], ident[0:rows, 0:rows])
                ins.then_inc(xT_ps, 1)
                pe.wait_ge(xT_sb, b + 1)
                for i in range(3):
                    mm(bank[1 + i][:, 0:T], wT[:, 2 * i, :], xT[:, 0:T], start=True, stop=False)
                    mm(bank[1 + i][:, 0:T], wT[:, 2 * i + 1, :], xT[:, 1:T_IN], start=False, stop=True).then_inc(conv_ps, 1)
                pe.wait_ge(hT_ready, b + 1)
                for t in range(NT):
                    ins = tr(bank[4][:, t * P:(t + 1) * P], hT[:, t * P:(t + 1) * P], ident[:])
                ins.then_inc(h_ps, 1)
                pe.wait_ge(n2_ready, b + 1)
                for t in range(NT):
                    ins = tr(bank[5][:, t * P:(t + 1) * P], n2[:, t, :], ident[:])
                ins.then_inc(n2_ps, 1)
            pe.wait_ge(setup_sb, 9)
            with pe.Fori(0, B) as b:
                pe_mixer(b)
            pe.wait_ge(hn_ready, B)

            mi = bank[7]

            def side(b, pos_in_list, name, j):
                index = jobs_before(b) + pos_in_list
                wait(pe, misc_free, index)
                if name == "q":
                    pe.wait_ge(hnb_ready, b + 2)
                    ins = mm(mi[:, 0:TP], wT[:, 6, :], hnb[:, :], start=True, stop=True)
                elif name == "k":
                    ins = mm(mi[:, 0:TP], wT[:, 7, :], hnb[:, :], start=True, stop=True)
                elif name == "v":
                    for t in range(NT):
                        ins = mm(mi[:, t * P:(t + 1) * P], hnb[:, t * P:(t + 1) * P], wT[:, 8, :], start=True, stop=True)
                elif name in ("sqv", "squ", "sk"):
                    hi, lo, sh, sl = {"sqv": (hi_qv, lo_qv, spread_q_hi, spread_q_lo),
                                      "squ": (hi_qu, lo_qu, spread_q_hi, spread_q_lo),
                                      "sk": (hi_k, lo_k, spread_k_hi, spread_k_lo)}[name]
                    if j == 0:
                        pe.wait_ge(split_ready, 3 * b + {"sqv": 5, "squ": 6, "sk": 7}[name])
                    mm(mi[:, 0:TP], sh[:, j, :], hi[:, 0:TP], start=True, stop=False)
                    ins = mm(mi[:, 0:TP], sl[:, j, :], lo[:, 0:TP], start=False, stop=True)
                elif name == "rt":
                    pe.wait_ge(inv_ready, b)
                    for t in range(NT):
                        ins = tr(mi[0:NH, t * P:(t + 1) * P], inv_rowsum[:].rearrange("p (h t) -> p t h", t=NT)[:, t, :], ident[:])
                elif name == "rb":
                    ins = mm(mi[:, 0:TP], head_rows[:, :], inv_T[:, :], start=True, stop=True)
                elif name == "wo":
                    for t in range(NT):
                        ins = mm(mi[:, t * P:(t + 1) * P], oT[:, t * P:(t + 1) * P], wT[:, 9, :], start=True, stop=True)
                elif name == "x2t":
                    pe.wait_ge(x2_ready, b)
                    for t in range(NT):
                        ins = tr(mi[:, t * P:(t + 1) * P], x2[:, t, :], ident[:])
                elif name == "gate":
                    for t in range(NT):
                        ins = mm(mi[:, t * E:(t + 1) * E], x2T[:, t * P:(t + 1) * P], gate_w[:, :], start=True, stop=True)
                elif name == "count":
                    pe.wait_ge(chosen_ready, b)
                    flat = chosen[:, :, :].rearrange("p t e -> p (t e)")
                    mm(mi[:, 0:NT * E], tri[:, :], flat, start=True, stop=True)
                    ins = mm(mi[:, NT * E:2 * NT * E], ones[:, :], flat, start=True, stop=True)
                ins.then_inc(misc_ps, 1)

            def pe_body(b, att, prev, nxt):
                jobs = side_jobs(prev, nxt)
                where = {(name, j): i for i, (_, name, j) in enumerate(jobs)}
                started = not (isinstance(b, int) and b <= 0)
                for s in range(UNITS + 2):
                    u = UNITS * b + s
                    for i, (at, name, j) in enumerate(jobs):
                        if at == s:
                            side(b, i, name, j)
                    if (att and s < UNITS - 1) or (nxt and s == UNITS - 1):
                        h, t = (s + 1) // NT % NH, (s + 1) % NT
                        pair, half = h // 2, 64 * (h % 2)
                        wait(pe, scored, u)
                        if h % 2 == 0 and t == 0 and s == UNITS - 1:
                            pe.wait_ge(misc_free, jobs_before(b) + where["squ", 0] + 1)
                        elif pair == NPAIR - 1 and h % 2 == 0 and t == 0:
                            pe.wait_ge(misc_free, jobs_before(b))
                        mm(bank[(s + 1) % 2][:, 0:T], qu_stack[half:half + 64, pair, t * P:(t + 1) * P],
                           k_stack[half:half + 64, pair, 0:T], start=True, stop=True).then_inc(content_ps, 1)
                    if nxt:
                        for m in POS_AT.get(s, []):
                            h1, t1 = m // NT, m % NT
                            pair, half = h1 // 2, 64 * (h1 % 2)
                            if m % (2 * NT) == 0:
                                pe.wait_ge(misc_free, jobs_before(b) + where["sqv", pair] + 1)
                            wait(pe, pos_sb, UNITS * (b + 1) + m - 1)
                            mm(bank[2 + m % 2][:, :], qv_stack[half:half + 64, pair, t1 * P:(t1 + 1) * P],
                               p_stack[half:half + 64, pair, :], start=True, stop=True).then_inc(pos_ps, 1)
                    if (att and 1 <= s < UNITS) or (s == 0 and started):
                        wait(pe, probs_ready, u)
                        wait(pe, probsT_sb, u - 2)
                        for c in range(NT):
                            ins = tr(bank[4 + (s + 1) % 2][:, c * P:(c + 1) * P], probs[:, (s + 1) % 2, c * P:(c + 1) * P], ident[:])
                        ins.then_inc(probsT_ps, 1)
                    if (att and s >= 5 and s % NT == 2 and s < UNITS) or (s == 2 and started):
                        gh = NH * b + (s - 5) // NT
                        hh = (s - 5) // NT % NH
                        wait(pe, probsT_sb, NT * gh + NT)
                        pe.wait_ge(v_diag_ready, gh + 1)
                        if hh == 0:
                            wait(pe, oT_copied, b)
                        for c in range(NT):
                            rows = P if c < NT - 1 else T_LAST
                            ins = mm(bank[6][:, 0:TP], v_diag[0:rows, c, hh, :], probsT[0:rows, hh % 2, c, :],
                                     start=hh == 0 and c == 0, stop=hh == NH - 1 and c == NT - 1)
                        ins.then_inc(av_done, 1)

            pe_body(-1, False, False, True)
            pe_body(0, True, False, True)
            with pe.Fori(1, 1 + LOOP) as b:
                pe_body(b, True, True, True)
            pe_body(B - 2, True, True, True)
            pe_body(B - 1, True, True, False)
            pe_body(B, False, True, False)

            def chunks(c):
                return [k for k in (2 * c, 2 * c + 1) if k < FC]

            def width(k):
                return P if k < FC - 1 else F_LAST

            def transposes(j, s, n):
                pe.wait_ge(xe_loaded[s], 16 * n)
                wait(pe, x_ready, j)
                for t in range(2):
                    ins = tr(bank[6][:, t * P:(t + 1) * P], xe[:, s, t, 0:D], ident[:])
                ins.then_inc(xe_ps, 1)

            def y_transposes(j, s):
                wait(pe, y_sb, j + 1)
                wait(pe, y_rows_ready, j)
                for t in range(2):
                    ins = tr(bank[7][:, t * P:(t + 1) * P], yT[:, s, t * P:(t + 1) * P], ident[:])
                ins.then_inc(yT_ps, 1)

            def up(s, c, first_bank, hi, lo, sem_):
                for i, k in enumerate(chunks(c)):
                    dst = bank[first_bank + c % 2][0:width(k), i * GT:(i + 1) * GT]
                    cols_ = slice(k * P, k * P + width(k))
                    mm(dst, hi[:, cols_], x_hi[:, s, :], start=True, stop=False)
                    mm(dst, hi[:, cols_], x_lo[:, s, :], start=False, stop=False)
                    ins = mm(dst, lo[:, cols_], x_hi[:, s, :], start=False, stop=True)
                ins.then_inc(sem_, 1)

            def down(j, s, ws, w, c):
                if c == 0:
                    wait(pe, y_sb, j - 1)
                    if w is not None:
                        wait(pe, w23_lo_ready, 4 * w + 3)
                if c == (FC + 1) // 4 and w is not None:
                    wait(pe, w23_lo_ready, 4 * w + 4)
                pe.wait_ge(g_lo_ready, PAIRS * j + c + 1)
                for i, k in enumerate(chunks(c)):
                    dst, rows = bank[4 + s][:, 0:GT], width(k)
                    wh, wl = hi3[ws][0:rows, k * D:(k + 1) * D], lo3[ws][0:rows, k * D:(k + 1) * D]
                    gh, gl = (x_[0:rows, c % 2, i * GT:(i + 1) * GT] for x_ in (g_hi, g_lo))
                    mm(dst, wh, gh, start=k == 0, stop=False)
                    mm(dst, wh, gl, start=False, stop=False)
                    ins = mm(dst, wl, gh, start=False, stop=k == FC - 1)
                ins.then_inc(down_ps, 1)

            def tile(j, s, ws, w, prev_ws, after):
                first = isinstance(j, int) and j == 0
                wait(pe, x_ready, j + 1)
                for c in range(PAIRS):
                    if w is not None and c == 0:
                        pe.wait_ge(w1_lo_ready, 2 * w + 2)
                    wait(pe, silu_ready, PAIRS * j + c - 1)
                    up(s, c, 0, hi1[ws], lo1[ws], a_ps)
                    if w is not None and c == 0:
                        pe.wait_ge(w23_lo_ready, 4 * w + 2)
                    wait(pe, product_ready, PAIRS * j + c - 1)
                    up(s, c, 2, hi2[ws], lo2[ws], b_ps)
                    if c >= 2:
                        down(j, s, ws, w, c - 2)
                    elif not first:
                        down(j - 1, 1 - s, prev_ws, None, PAIRS - 2 + c)
                    if c == 1 and after is not None:
                        transposes(j + 1, 1 - s, after)
                    if c == 3 and not first:
                        y_transposes(j - 1, 1 - s)

            pe.wait_ge(scored, UNITS * B)
            pe.wait_ge(pos_sb, UNITS * B)
            pe.wait_ge(probsT_sb, UNITS * B)
            pe.wait_ge(oT_copied, B)
            pe.wait_ge(misc_free, jobs_before(B))
            transposes(0, 0, 1)
            tile(0, 0, 0, 0, 0, 1)
            tile(1, 1, 0, None, 0, 2)
            with pe.Fori(1, SHARED // 2) as i:
                for s in range(2):
                    tile(2 * i + s, s, 0, None, 0, i + 1 + s)
            tile(SHARED, 0, 1, 1, 0, SHARED // 2 + 1)
            tile(SHARED + 1, 1, 0, 2, 1, SHARED // 2 + 2)
            HALF = (SHARED + ROUTED) // 2
            with pe.Fori(SHARED // 2 + 1, HALF - 1) as i:
                for s in range(2):
                    tile(2 * i + s, s, 1 - s, 2 * i + s - SHARED + 1, s, i + 1 + s)
            tile(2 * HALF - 2, 0, 1, ROUTED - 1, 0, HALF)
            tile(2 * HALF - 1, 1, 0, ROUTED, 1, None)
            down(2 * HALF - 1, 1, 0, None, PAIRS - 2)
            down(2 * HALF - 1, 1, 0, None, PAIRS - 1)
            y_transposes(2 * HALF - 1, 1)

        @block.scalar
        def _(act):
            f = nc.scalar.activation
            step = Steps(act, act_step)
            pe_ready = setup_ps
            for n in range(3):
                act.wait_ge(pe_ready, n + 1)
                w = 4 if n < 2 else 3
                nc.scalar.copy(wT[:, 4 * n:4 * n + w, :].rearrange("p a b -> p (a b)"), bank[n][:, 0:w * P]).then_inc(setup_sb, 1)
            act.wait_ge(pe_ready, 4)
            act.wait_ge(consts_ready, 1)
            nc.scalar.copy(posT[:, 0:NPOS], bank[3][:, 0:NPOS]).then_inc(setup_sb, 1)
            act.wait_ge(weights_in, 16 * N_SMALL)
            step.did(nc.scalar.mul(qbias[:, :], cols[:, 5:7], -0.25))
            step.did(nc.scalar.mul(fz[:, 0:1], cols[:, 3:4], -0.25))
            step.settle()
            f(qbias[:, :], qbias[:, :], ACT.Identity, bias=fz[:, 0:1]).then_inc(setup_sb, 1)
            act.wait_ge(pe_ready, 5)
            nc.scalar.copy(hi_k[:, :], bank[4][:, :])
            nc.scalar.copy(t_k[:, :], bank[4][:, :]).then_inc(t_ready, 1)
            for j in range(NPAIR):
                act.wait_ge(pe_ready, 6 + j)
                nc.scalar.copy(p_stack[:, j, :], bank[5][:, :]).then_inc(setup_sb, 1)

            def act_mixer(b):
                act.wait_ge(xT_ps, b + 1)
                nc.scalar.copy(xT[:, 0:T_IN], bank[0][:, 0:T_IN]).then_inc(xT_sb, 1)
                for i, fn in enumerate((ACT.Tanh, ACT.Sigmoid, ACT.Sigmoid)):
                    act.wait_ge(conv_ps, 3 * b + i + 1)
                    if i == 0:
                        wait(act, hT_ready, b)
                    f(gates[:, i, :], bank[1 + i][:, 0:T], fn, bias=cols[:, i:i + 1]).then_inc(conv_sb, 1)
                act.wait_ge(n2_ps, b + 1)
                f(hnT[:, bass.ds(b * TP, TP)], bank[5][:, 0:TP], ACT.Identity, bias=cols[:, 8:9],
                  scale=cols[:, 7:8]).then_inc(hn_ready, 1)
            act_mixer(0)
            with act.Fori(1, B) as b:
                act_mixer(b)

            mi = bank[7]

            def act_side(b, i, name, j):
                n = jobs_before(b) + i
                if name == "q":
                    act.wait_ge(misc_ps, n + 1)
                    wait(act, split_ready, 3 * b + 4)
                    f(hi_qv[:, :], mi[:, 0:TP], ACT.Identity, bias=qbias[:, 1:2], scale=-0.25)
                    f(t_qv[:, :], mi[:, 0:TP], ACT.Identity, bias=qbias[:, 1:2], scale=-0.25).then_inc(t_ready, 1)
                    f(hi_qu[:, :], mi[:, 0:TP], ACT.Identity, bias=qbias[:, 0:1], scale=-0.25)
                    f(t_qu[:, :], mi[:, 0:TP], ACT.Identity, bias=qbias[:, 0:1], scale=-0.25).then_inc(misc_free, 1)
                elif name == "k":
                    act.wait_ge(misc_ps, n + 1)
                    f(hi_k[:, 0:TP], mi[:, 0:TP], ACT.Identity, bias=cols[:, 4:5])
                    f(t_k[:, 0:TP], mi[:, 0:TP], ACT.Identity, bias=cols[:, 4:5]).then_inc(misc_free, 1)
                elif name in ("sqv", "squ", "sk"):
                    act.wait_ge(misc_ps, n + 1)
                    dst = {"sqv": qv_stack, "squ": qu_stack, "sk": k_stack}[name]
                    nc.scalar.copy(dst[:, j, :], mi[:, 0:TP]).then_inc(misc_free, 1)
                elif name == "x2t":
                    act.wait_ge(misc_ps, n + 1)
                    nc.scalar.copy(x2T[:, :], mi[:, 0:TP]).then_inc(misc_free, 1)

            def act_body(b, att, prev, nxt):
                jobs = side_jobs(prev, nxt)
                for s in range(UNITS + 2):
                    u = UNITS * b + s
                    if nxt:
                        for m in POS_AT.get(s - 1, []):
                            h1, t1 = m // NT, m % NT
                            act.wait_ge(pos_ps, UNITS * (b + 1) + m + 1)
                            if t1 == 0:
                                wait(act, pos_written[h1 % 2], 16 * (4 * (b + 1) + h1 // 2))
                            nc.scalar.copy(pos_out[:, h1 % 2, t1, 1:POSW], bank[2 + m % 2][:, 0:NPOS]).then_inc(pos_sb, 1)
                    for i, (at, name, j) in enumerate(jobs):
                        if at == s:
                            act_side(b, i, name, j)
                    if att and s < UNITS:
                        act.wait_ge(scored, u + 1)
                        wait(act, probsT_ps, u - 1)
                        if s == 0:
                            wait(act, inv_ready, b)
                        f(probs[:, s % 2, 0:T], score[:, s % 2, :], ACT.Exp, bias=least[:, s % 2:s % 2 + 1], scale=-1.0,
                          accum_out=rowsum[:, s:s + 1]).then_inc(probs_ready, 1)
                    if s == 3 and prev:
                        act.wait_ge(av_done, NH * b)
                        nc.scalar.copy(oT_raw[:, :], bank[6][:, 0:TP]).then_inc(oT_copied, 1)
                    if s == 16 and prev:
                        act.wait_ge(shift_ready, b)
                        f(exp_v[:, :, :], shifted_v[:, :, :], ACT.Exp).then_inc(exp_ready, 1)

            act_body(-1, False, False, True)
            act_body(0, True, False, True)
            with act.Fori(1, 1 + LOOP) as b:
                act_body(b, True, True, True)
            act_body(B - 2, True, True, True)
            act_body(B - 1, True, True, False)
            act_body(B, False, True, False)

            def split_high(w, s, piece, loads):
                if piece == 0:
                    act.wait_ge(w_loaded[s], 64 * loads)
                raw, hi = ((raw1, hi1), (raw2, hi2), (raw3, hi3))[piece // 2]
                for rows, part in parts_of(piece):
                    ins = nc.scalar.copy(hi[s][0:rows, part], raw[s][0:rows, part])
                ins.then_inc(w_hi_ready, 1)

            def g_high(j, s, c):
                act.wait_ge(product_ready, PAIRS * j + c + 1)
                wait(act, down_ps, PAIRS * j + c - 1)
                rows, w = (P, 2 * GT) if 2 * c + 1 < FC else (F_LAST, GT)
                nc.scalar.copy(g_hi[0:rows, c % 2, 0:w], product[0:rows, c % 2, 0:w]).then_inc(g_hi_ready, 1)

            def x_high(j, s):
                act.wait_ge(xe_ps, j + 1)
                wait(act, b_ps, PAIRS * (j - 1))
                nc.scalar.copy(x_hi[:, s, :], bank[6][:, 0:GT]).then_inc(x_hi_ready, 1)

            def copy_yT(j, s):
                act.wait_ge(down_ps, PAIRS * (j + 1))
                wait(act, yT_ps, j - 1)
                nc.scalar.copy(yT[:, s, :], bank[4 + s][:, 0:GT]).then_inc(y_sb, 1)

            def act_tile(j, s, split, loads, nxt):
                first = isinstance(j, int) and j == 0
                for c in range(PAIRS):
                    rows, w = (P, 2 * GT) if 2 * c + 1 < FC else (F_LAST, GT)
                    act.wait_ge(a_ps, PAIRS * j + c + 1)
                    wait(act, product_ready, PAIRS * j + c - 1)
                    f(act_a[0:rows, c % 2, 0:w], bank[c % 2][0:rows, 0:w], ACT.Silu).then_inc(silu_ready, 1)
                    if c > 0:
                        g_high(j, s, c - 1)
                    elif not first:
                        g_high(j - 1, 1 - s, PAIRS - 1)
                    if c == 2 and not first:
                        copy_yT(j - 1, 1 - s)
                    if c == 2 and nxt:
                        x_high(j + 1, 1 - s)
                    if split is not None:
                        split_high(split, s, c, loads)

            for i in range(2):
                act.wait_ge(pos_written[i], 16 * NH * B // 2)
            for piece in range(6):
                split_high(0, 0, piece, 1)
            x_high(0, 0)
            act_tile(0, 0, None, None, True)
            act_tile(1, 1, None, None, True)
            with act.Fori(1, SHARED // 2 - 1) as i:
                for s in range(2):
                    act_tile(2 * i + s, s, None, None, True)
            act_tile(SHARED - 2, 0, None, None, True)
            act_tile(SHARED - 1, 1, 1, 1, True)
            HALF = (SHARED + ROUTED) // 2
            with act.Fori(SHARED // 2, HALF - 1) as i:
                for s in range(2):
                    act_tile(2 * i + s, s, 2 * i + s - SHARED + 2, i - SHARED // 2 + 2, True)
            act_tile(2 * HALF - 2, 0, ROUTED, ROUTED // 2 + 1, True)
            act_tile(2 * HALF - 1, 1, None, None, False)
            g_high(2 * HALF - 1, 1, PAIRS - 1)
            copy_yT(2 * HALF - 1, 1)

        @block.vector
        def _(dve):
            v = nc.vector
            step = Steps(dve, dve_step)

            def norm_stats(srcs):
                for t, src in enumerate(srcs):
                    step.did(v.bn_stats(stats[:, t, :], src))
                step.settle(dve_gate)
                for t in range(NT):
                    ins = v.bn_aggr(mv[:, t, :], stats[:, t, :])
                    if t == NT - 1:
                        ins.then_inc(var_ready, 1)

            def normalise(dst, srcs, n, sem_):
                dve.wait_ge(rstd_ready, n + 1)
                for t, src in enumerate(srcs):
                    ins = v.tensor_scalar(dst[:, t, :], src, mv[:, t, 0:1], rstd[:, t:t + 1], ALU.subtract, ALU.mult)
                    if sem_ is None:
                        step.did(ins)
                if sem_ is not None:
                    ins.then_inc(sem_, 1)

            def dve_mixer(b):
                dve.wait_ge(conv_sb, 3 * b + 2)
                step.did(v.scalar_tensor_tensor(out=fz[:, :], in0=gates[:, 1, :], scalar=1.0, in1=gates[:, 0, :],
                                                op0=ALU.subtract, op1=ALU.mult))
                step.settle()
                step.did(v.tensor_tensor_scan(cell[:, :], gates[:, 1, :], fz[:, :], 0.0, ALU.mult, ALU.subtract))
                step.settle()
                dve.wait_ge(conv_sb, 3 * b + 3)
                v.tensor_tensor(hT[:, 0:T], cell[:, :], gates[:, 2, :], ALU.mult).then_inc(hT_ready, 1)
                dve.wait_ge(h_ps, b + 1)
                h_rows = [bank[4][:, t * P:(t + 1) * P] for t in range(NT)]
                x1_rows = [x1[:, t, :] for t in range(NT)]
                norm_stats(h_rows)
                normalise(x1, h_rows, 2 * b, None)
                step.settle()
                norm_stats(x1_rows)
                wait(dve, hx_done, b)
                v.tensor_tensor(hx_part[:, :], bank[4][:, 0:TP], x1[:, :, :].rearrange("p t d -> p (t d)"), ALU.add).then_inc(hx_ready, 1)
                wait(dve, n2_ps, b)
                normalise(n2, x1_rows, 2 * b + 1, n2_ready)
            dve.wait_ge(consts_ready, 1)
            dve.wait_ge(setup_sb, 9)
            PER = 2 + 3 + 3 + 3
            with dve.Fori(0, B) as b:
                step.enter(b, PER)
                dve_mixer(b)
            step.leave(B, PER)

            mi = bank[7]

            def dve_side(b, i, name, part):
                n = jobs_before(b) + i
                if name not in ("v", "rt", "rb", "wo", "gate", "count"):
                    return
                if part == 0:
                    dve.wait_ge(misc_ps, n + 1)
                if (name, part) == ("v", 0):
                    wait(dve, v_diag_ready, NH * (b + 1))
                    v.tensor_tensor(v_rows[:, :, :], mi[:, 0:TP].rearrange("p (t d) -> p t d", t=NT),
                                    bv_row[:, :].unsqueeze(1).to_broadcast([P, NT, D]), ALU.add).then_inc(misc_free, 1)
                elif (name, part) == ("rt", 0):
                    v.tensor_copy(inv_T[:, :], mi[0:NH, 0:TP]).then_inc(misc_free, 1)
                elif (name, part) == ("rb", 0):
                    dve.wait_ge(oT_copied, b)
                    v.tensor_tensor(oT[:, :], oT_raw[:, :], mi[:, 0:TP], ALU.mult).then_inc(misc_free, 1)
                elif (name, part) == ("wo", 0):
                    wait(dve, h2_kept, b - 1)
                    wait(dve, x2_stored, 16 * (b - 1))
                    wait(dve, scattered, 16 * NT * TOPK * (b - 1))
                    v.tensor_tensor(h2[:, :, :].rearrange("p t d -> p (t d)"), mi[:, 0:TP],
                                    HX[:, bass.ds(b - 1, 1), :].rearrange("p o d -> p (o d)"), ALU.add).then_inc(misc_free, 1)
                    dve.wait_ge(misc_free, n + 1)
                    norm_stats([h2[:, t, :] for t in range(NT)])
                elif (name, part) == ("wo", 1):
                    normalise(x2, [h2[:, t, :] for t in range(NT)], 2 * B + b - 1, x2_ready)
                elif (name, part) == ("gate", 0):
                    v.tensor_tensor(logits[:, :, :], mi[:, 0:NT * E].rearrange("p (t e) -> p t e", t=NT),
                                    rb_row[:, :].unsqueeze(1).to_broadcast([P, NT, E]), ALU.add).then_inc(misc_free, 1)
                    wait(dve, misc_free, n + 1, dve_gate)
                    for t in range(NT):
                        step.did(v.max(top_v[:, t, :], logits[:, t, :]))
                    step.settle(dve_gate)
                    for t in range(NT):
                        step.did(v.max_index(top_i[:, t, :], top_v[:, t, :], logits[:, t, :]))
                elif (name, part) == ("gate", 1):
                    step.settle()
                    wait(dve, exp_ready, b - 1)
                    v.tensor_tensor(shifted_v[:, :, :], top_v[:, :, 0:TOPK], top_v[:, :, 0:1].to_broadcast([P, NT, TOPK]),
                                    ALU.subtract).then_inc(shift_ready, 1)
                    step.did(v.tensor_copy(top_f[:, :, :], top_i[:, :, 0:TOPK]))
                    step.settle()
                    ranks = top_f[:, :, :].rearrange("p t k -> p (t k)")
                    step.did(v.tensor_tensor(onehot[:, :, :], ranks.unsqueeze(2).to_broadcast([P, NT * TOPK, E]),
                                             iota_e[:, :].unsqueeze(1).to_broadcast([P, NT * TOPK, E]), ALU.is_equal))
                elif (name, part) == ("gate", 2):
                    step.settle()
                    step.did(v.tensor_tensor(onehot[:, :, :], onehot[:, :, :],
                                             valid[:, :].unsqueeze(2).to_broadcast([P, NT * TOPK, E]), ALU.mult))
                    step.settle()
                    v.tensor_reduce(chosen[:, :, :], onehot[:, :, :].rearrange("p (t k) e -> p t e k", t=NT), AX.X,
                                    ALU.add).then_inc(chosen_ready, 1)
                elif (name, part) == ("count", 0):
                    for t in range(NT):
                        step.did(v.tensor_tensor(before[:, t + 1, :], before[:, t, :], mi[:, (NT + t) * E:(NT + t + 1) * E], ALU.add))
                        step.settle()
                    step.did(v.tensor_tensor(place[:, :, :], before[:, 0:NT, :], mi[:, 0:NT * E].rearrange("p (t e) -> p t e", t=NT), ALU.add))
                    step.settle()
                    v.tensor_copy(before[:, 0, :], before[:, NT, :]).then_inc(misc_free, 1)
                elif (name, part) == ("count", 1):
                    dve.wait_ge(misc_free, n + 1)
                    step.did(v.tensor_tensor(place[:, :, :], place[:, :, :], region_e[:, :].unsqueeze(1).to_broadcast([P, NT, E]), ALU.add))
                    step.settle()
                    step.did(v.tensor_tensor(picked[:, :, :].rearrange("p (t k) e -> p t k e", t=NT),
                                             onehot[:, :, :].rearrange("p (t k) e -> p t k e", t=NT),
                                             place[:, :, :].unsqueeze(2).to_broadcast([P, NT, TOPK, E]), ALU.mult))
                    step.settle()
                    step.did(v.tensor_reduce(slot_f[:, :], picked[:, :, :], AX.X, ALU.add))
                elif (name, part) == ("count", 2):
                    step.settle()
                    step.did(v.tensor_tensor(slot_f[:, :], slot_f[:, :], dump_rows[:, :], ALU.add))
                    dve.wait_ge(exp_ready, b)
                    step.did(v.tensor_reduce(exp_sum[:, :], exp_v[:, :, :], AX.X, ALU.add))
                    step.settle()
                    step.did(v.reciprocal(exp_sum[:, :], exp_sum[:, :]))
                    step.did(v.tensor_copy(x2_row[:, :, AT_E:AT_E + TOPK], top_f[:, :, :]))
                    step.did(v.tensor_copy(x2_row[:, :, AT_ID:AT_ID + 1], ids_f[:, :].unsqueeze(2)))
                    step.did(v.tensor_scalar(ids_f[:, :], ids_f[:, :], float(TP), None, ALU.add))
                    step.settle()
                    step.did(v.tensor_tensor(x2_row[:, :, AT_W:AT_W + TOPK], exp_v[:, :, :],
                                             exp_sum[:, :].unsqueeze(2).to_broadcast([P, NT, TOPK]), ALU.mult))
                    v.tensor_copy(slot_i[:, :], slot_f[:, :]).then_inc(slot_ready, 1)

            def dve_body(b, att, prev, nxt):
                jobs = side_jobs(prev, nxt)
                started = not (isinstance(b, int) and b <= 0)
                for s in range(UNITS + 2):
                    u = UNITS * b + s
                    h, t = s // NT, s % NT
                    if s == 0 and prev:
                        dve.wait_ge(probs_ready, UNITS * b)
                        v.reciprocal(inv_rowsum[:, :], rowsum[:, :]).then_inc(inv_ready, 1)
                    if att and s < UNITS:
                        dve.wait_ge(content_ps, u + 1)
                        if t == 0:
                            dve.wait_ge(pos_read[h % 4], 16 * NT * (2 * b + h // 4 + 1))
                        wait(dve, probs_ready, u - 1, dve_gate)
                        v.tensor_tensor_reduce(out=score[:, s % 2, :], in0=bank[s % 2][:, 0:T], in1=pos_in[:, h % 4, t, :],
                                               scale=1.0, scalar=3.0e38, op0=ALU.add, op1=ALU.min,
                                               accum_out=least[:, s % 2:s % 2 + 1]).then_inc(scored, 1)
                    if (att and 2 <= s < UNITS) or (s < 2 and started):
                        hh, tt = (s - 2) // NT % NH, (s - 2) % NT
                        dve.wait_ge(probsT_ps, u - 1)
                        if tt == 0:
                            wait(dve, av_done, NH * b + hh - 1)
                        v.tensor_copy(probsT[:, hh % 2, :, tt * P:(tt + 1) * P],
                                      bank[4 + s % 2][:, 0:TP].rearrange("p (c q) -> p c q", c=NT)).then_inc(probsT_sb, 1)
                    for part in (2, 1, 0):
                        for i, (at, name, j) in enumerate(jobs):
                            if at == s - part:
                                dve_side(b, i, name, part)

            dve_body(-1, False, False, True)
            dve_body(0, True, False, True)
            with dve.Fori(1, 1 + LOOP) as b:
                step.enter(b - 1, DVE_PER_BATCH)
                dve_body(b, True, True, True)
            step.leave(LOOP, DVE_PER_BATCH)
            dve_body(B - 2, True, True, True)
            dve_body(B - 1, True, True, False)
            dve_body(B, False, True, False)

            def split_low(w, s, piece):
                dve.wait_ge(w_hi_ready, 6 * w + piece + 1)
                for rows, part in parts_of(piece):
                    v.tensor_tensor(lo1[s][:, part], raw1[s][:, part], hi1[s][:, part].bitcast(F32), ALU.subtract).then_inc(w1_lo_ready, 1)

            def x_low(j, s):
                dve.wait_ge(x_hi_ready, j + 1)
                v.tensor_tensor(x_lo[:, s, :], bank[6][:, 0:GT], x_hi[:, s, :].bitcast(F32), ALU.subtract).then_inc(x_ready, 1)

            dve.wait_ge(hnb_ready, B)
            split_low(0, 0, 0)
            split_low(0, 0, 1)
            x_low(0, 0)

            def chain(ins):
                step.did(ins)
                step.settle()
            total_e = before[:, 0, :]
            chain(v.tensor_scalar(count_i[:, :], total_e, float(GT - 1), None, ALU.add))
            chain(v.tensor_scalar(count_i[:, :], count_i[:, :], GT.bit_length() - 1, None, ALU.logical_shift_right))
            chain(v.tensor_copy(tiles_f[:, :], count_i[:, :]))
            chain(v.tensor_tensor_scan(tiles_end[:, :], ones[:, 0:E], tiles_f[:, :], 0.0, ALU.mult, ALU.add))
            chain(v.tensor_tensor(tiles_f[:, :], tiles_end[:, :], tiles_f[:, :], ALU.subtract))
            chain(v.scalar_tensor_tensor(out=shift_e[:, :], in0=tiles_f[:, :], scalar=-float(GT), in1=region_e[:, :],
                                         op0=ALU.mult, op1=ALU.add))
            chain(v.tensor_tensor(pad_row[:, :], before[0:1, 0, :], region_e[0:1, :], ALU.add))
            each = [P, 64, E]
            chain(v.tensor_tensor(tile_cmp[:, :, :], iota_tile[:, :].unsqueeze(2).to_broadcast(each),
                                  tiles_end[:, :].unsqueeze(1).to_broadcast(each), ALU.is_ge))
            chain(v.tensor_reduce(tile_e[:, :], tile_cmp[:, :, :], AX.X, ALU.add))
            chain(v.tensor_scalar(table[:, 0, :], tile_e[0:1, :], float(E - 1), None, ALU.min))
            each = [1, 64, E]
            chain(v.tensor_tensor(tile_cmp[0:1, :, :], tile_e[0:1, :].unsqueeze(2).to_broadcast(each),
                                  iota_e[0:1, :].unsqueeze(1).to_broadcast(each), ALU.is_equal))
            chain(v.tensor_tensor(tile_cmp[0:1, :, :], tile_cmp[0:1, :, :], shift_e[0:1, :].unsqueeze(1).to_broadcast(each), ALU.mult))
            chain(v.tensor_reduce(tile_row[:, :], tile_cmp[0:1, :, :], AX.X, ALU.add))
            chain(v.scalar_tensor_tensor(out=tile_row[:, :], in0=iota_tile[0:1, :], scalar=float(GT), in1=tile_row[:, :],
                                         op0=ALU.mult, op1=ALU.add))
            chain(v.tensor_scalar(tile_fix[:, :], tile_row[:, :], -1.0, float(ZERO_ROW), ALU.mult, ALU.add))
            chain(v.tensor_scalar(tile_cmp[0:1, :, 0], tile_e[0:1, :], float(E), None, ALU.is_ge))
            chain(v.tensor_tensor(tile_fix[:, :], tile_fix[:, :], tile_cmp[0:1, :, 0], ALU.mult))
            v.tensor_tensor(table[:, 1, :], tile_row[:, :], tile_fix[:, :], ALU.add).then_inc(table_ready, 1)

            def g_low(j, s, c):
                dve.wait_ge(g_hi_ready, PAIRS * j + c + 1)
                rows, w = (P, 2 * GT) if 2 * c + 1 < FC else (F_LAST, GT)
                v.tensor_tensor(g_lo[0:rows, c % 2, 0:w], product[0:rows, c % 2, 0:w], g_hi[0:rows, c % 2, 0:w].bitcast(F32),
                                ALU.subtract).then_inc(g_lo_ready, 1)

            def read_rows(r, s):
                dve.wait_ge(x_ready, SHARED + r + 1)
                wait(dve, y_added, 32 * (r - 1))
                v.tensor_copy(tile_expert[:, :], tile_e[:, bass.ds(r, 1)]).then_inc(expert_ready, 1)
                dve.wait_ge(expert_ready, r + 1)
                for t in range(2):
                    v.tensor_copy(row_id[:, s, t:t + 1], xe[:, s, t, AT_ID:AT_ID + 1])
                for t in range(2):
                    ins = v.scalar_tensor_tensor(out=same[:, t, :], in0=xe[:, s, t, AT_E:AT_E + TOPK], scalar=tile_expert[:, 0:1],
                                                 in1=xe[:, s, t, AT_W:AT_W + TOPK], op0=ALU.is_equal, op1=ALU.mult,
                                                 accum_out=row_weight[:, s, t:t + 1])
                ins.then_inc(rows_known, 1)

            def shared_rows(j, s):
                wait(dve, y_stored, 16 * (j - 1))
                dve.wait_ge(yT_ps, j + 1)
                v.tensor_tensor(y_rows[:, s, :, :].rearrange("p t d -> p (t d)"), bank[7][:, 0:GT],
                                H2_flat[:, bass.ds(j * GT, GT)], ALU.add).then_inc(y_rows_ready, 1)

            def routed_rows(j, s):
                wait(dve, y_added, 32 * (j - SHARED - 1))
                wait(dve, rows_known, j - SHARED + 1)
                dve.wait_ge(yT_ps, j + 1)
                for t in range(2):
                    ins = v.tensor_scalar(y_rows[:, s, t, :], bank[7][:, t * P:(t + 1) * P], row_weight[:, s, t:t + 1], None, ALU.mult)
                ins.then_inc(y_rows_ready, 1)

            def dve_tile(j, s, split, routed, prev, nxt):
                first = isinstance(j, int) and j == 0
                for c in range(PAIRS):
                    rows, w = (P, 2 * GT) if 2 * c + 1 < FC else (F_LAST, GT)
                    dve.wait_ge(silu_ready, PAIRS * j + c + 1)
                    dve.wait_ge(b_ps, PAIRS * j + c + 1)
                    wait(dve, g_lo_ready, PAIRS * j + c - 1)
                    v.tensor_tensor(product[0:rows, c % 2, 0:w], act_a[0:rows, c % 2, 0:w], bank[2 + c % 2][0:rows, 0:w],
                                    ALU.mult).then_inc(product_ready, 1)
                    if c > 0:
                        g_low(j, s, c - 1)
                    elif not first:
                        g_low(j - 1, 1 - s, PAIRS - 1)
                    if c == READ and routed:
                        read_rows(j - SHARED, s)
                    if c in (LOW, LOW + 1) and split is not None:
                        split_low(split, s, c - LOW)
                    if c == 4 and prev is not None:
                        prev(j - 1, 1 - s)
                    if c == 3 and nxt:
                        x_low(j + 1, 1 - s)

            dve.wait_ge(h2_kept, B)
            dve_tile(0, 0, None, False, None, True)
            dve_tile(1, 1, None, False, shared_rows, True)
            with dve.Fori(1, SHARED // 2 - 1) as i:
                for s in range(2):
                    dve_tile(2 * i + s, s, None, False, shared_rows, True)
            dve_tile(SHARED - 2, 0, None, False, shared_rows, True)
            dve_tile(SHARED - 1, 1, 1, False, shared_rows, True)
            dve_tile(SHARED, 0, 2, True, shared_rows, True)
            dve_tile(SHARED + 1, 1, 3, True, routed_rows, True)
            HALF = (SHARED + ROUTED) // 2
            with dve.Fori(SHARED // 2 + 1, HALF - 1) as i:
                for s in range(2):
                    dve_tile(2 * i + s, s, 2 * i + s - SHARED + 2, True, routed_rows, True)
            dve_tile(2 * HALF - 2, 0, ROUTED, True, routed_rows, True)
            dve_tile(2 * HALF - 1, 1, None, True, routed_rows, False)
            g_low(2 * HALF - 1, 1, PAIRS - 1)
            routed_rows(2 * HALF - 1, 1)


DVE_PER_BATCH = 26


def kernel(**inputs):
    import concourse.bacc as bacc
    from concourse.bass_utils import run_bass_kernel_spmd as run

    nc = bacc.Bacc("TRN2", target_bir_lowering=False, num_devices=1)
    arrays, aps = {}, {}
    for name, value in inputs.items():
        short = name.removeprefix("L0_")
        arrays[f"in_{short}"] = np.ascontiguousarray(value)
        v = arrays[f"in_{short}"]
        aps[short] = nc.dram_tensor(f"in_{short}", v.shape, mybir.dt.from_np(v.dtype), kind="ExternalInput").ap()
    out = nc.dram_tensor("out", (B, T, D), F32, kind="ExternalOutput").ap()
    build(nc, aps, out)
    r = run(nc, [arrays], core_ids=[0])
    return r.results[0]["out"]
```

```python
from contextlib import ExitStack

import numpy as np

import concourse.bass as bass
from concourse import mybir

F32 = mybir.dt.float32
F32R = mybir.dt.float32r
I32 = mybir.dt.int32
U32 = mybir.dt.uint32
ALU = mybir.AluOpType
ACT = mybir.ActivationFunctionType
AX = mybir.AxisListType

P = 128
B = 8
T_IN = 375
T = T_IN - 1
NT = 3
TP = NT * P
T_LAST = T - (NT - 1) * P
X_LAST = T_IN - (NT - 1) * P
D = 128
NH = 8
HD = D // NH
NPAIR = NH // 2
NPOS = 511
POSW = NPOS + 1
E = 16
TOPK = 4
F = 1365
FC = (F + P - 1) // P
F_LAST = F - (FC - 1) * P
EPS = 1e-5
UNITS = NH * NT
NTILES = B * NT

GT = 2 * P
ROUTED = (B * T * TOPK + E * (GT - 1)) // GT
ROUTED += ROUTED % 2
SHARED = NTILES * P // GT
PAIRS = (FC + 1) // 2
ROW = D + 16
AT_W, AT_E, AT_ID = D, D + TOPK, D + 2 * TOPK
REGION = -(-(B * T + GT) // GT) * GT
ZERO_ROW = E * REGION
DUMP_ROW = ZERO_ROW + GT
XG_ROWS = DUMP_ROW + NT * P * TOPK
F_PAD = -(-F // 8) * 8


def parts_of(piece):
    if piece < 4:
        half = (F + 1) // 2 if piece < 2 else 3 * P
        return [(P, slice(0, half) if piece % 2 == 0 else slice(half, F))]
    half = (FC + 1) // 2 * D
    if piece == 4:
        return [(P, slice(0, half))]
    return [(P, slice(half, (FC - 1) * D)), (F_LAST, slice((FC - 1) * D, FC * D))]


class Steps:

    def __init__(self, engine, sem, alone=None):
        self.engine, self.sem, self.alone, self.base, self.n = engine, sem, alone, 0, 0

    def did(self, instruction):
        instruction.then_inc(self.sem, 1)
        self.n += 1

    def settle(self, alone=None):
        wait(self.engine, self.sem, self.base + self.n, alone or self.alone)

    def enter(self, i, per_turn):
        self.outer = self.base + self.n
        self.base, self.n = self.outer + i * per_turn, 0

    def leave(self, turns, per_turn):
        assert self.n == per_turn, (self.n, per_turn)
        self.base, self.n = self.outer + turns * per_turn, 0


def wait(engine, sem, value, alone=None):
    if not (isinstance(value, int) and value <= 0):
        engine.wait_ge(sem, value)
        if alone is not None and not isinstance(value, int):
            engine.sem_inc(alone, 1)


POS_TWICE = (11, 14, 17, 20)
POS_AT = {s: [s - 4 + sum(s > t for t in POS_TWICE) + i for i in range(2 if s in POS_TWICE else 1)] for s in range(4, 24)}

ATTENTION_END = range(5)
FIRST, AFTER_FIRST = range(2), range(2, UNITS + 2)
SHARED_SPLITS = (4, 6, 8, 10, 12, 14)
SLOT_IN_TILE = {(0, 0): 6, (0, 1): 7, (0, 2): 8, (0, 3): 10, (0, 4): 12, (0, 5): 13, (1, 0): 14, (1, 1): 16, (1, 2): 17,
                (1, 3): 18}


def side_jobs(prev, nxt):
    jobs = []
    if nxt:
        jobs += [(0, "q", 0), (1, "k", 0), (3, "sqv", 0), (5, "sk", 0), (8, "v", 0), (9, "sqv", 1), (11, "squ", 0),
                 (13, "sqv", 2), (14, "sk", 1), (15, "squ", 1), (17, "sk", 2), (18, "sqv", 3), (20, "squ", 2),
                 (24, "sk", 3), (25, "squ", 3)]
    if prev:
        jobs += [(4, "rt", 0), (6, "rb", 0), (7, "wo", 0), (10, "x2t", 0), (12, "gate", 0), (16, "count", 0)]
    return sorted(jobs, key=lambda j: j[0])


J_NEXT, J_PREV = len(side_jobs(False, True)), len(side_jobs(True, False))
J_FULL = J_NEXT + J_PREV
LOOP = B - 3
DVE_PER_BATCH = 26


def jobs_before(b):
    if isinstance(b, int) and b <= 0:
        return J_NEXT * (b + 1)
    if isinstance(b, int) and b == B:
        return 2 * J_NEXT + (B - 2) * J_FULL + J_PREV
    return 2 * J_NEXT + (b - 1) * J_FULL


def build(nc, a, out):
    ctx = ExitStack()
    with ctx:
        address = {}

        def sb(name, shape, dt=F32):
            address[name] = -(-nc.sbuf_base // 32) * 32
            return ctx.enter_context(nc.sbuf_tensor(name, shape, dt))

        def sem(name):
            return ctx.enter_context(nc.semaphore(name))

        bank = [ctx.enter_context(nc.psum_tensor(f"bank{i}", [P, 512], F32)) for i in range(8)]

        pos_dram = nc.dram_tensor("pos_scores", (NH, TP * POSW), F32).ap()
        xg_dram = nc.dram_tensor("dispatched_x", (XG_ROWS, ROW), F32).ap()
        xs_dram = nc.dram_tensor("shared_x", (NTILES * P, D), F32).ap()
        sum_dram = nc.dram_tensor("token_sums", (NTILES * P + GT, D), F32).ap()

        ident = sb("ident", [P, P])
        ones = sb("ones", [P, P])
        tri = sb("tri", [P, P])
        head_rows = sb("head_rows", [NH, D])
        template = sb("template", [P, 4, P])
        spread_q_hi = sb("spread_q_hi", [P, NPAIR, P], F32R)
        spread_q_lo = sb("spread_q_lo", [P, NPAIR, P], F32R)
        spread_k_hi = sb("spread_k_hi", [P, NPAIR, P], F32R)
        spread_k_lo = sb("spread_k_lo", [P, NPAIR, P], F32R)
        iota_e = sb("iota_e", [P, E])
        region_e = sb("region_e", [P, E])
        iota_tile = sb("iota_tile", [P, 64])
        valid = sb("valid", [P, NT * TOPK])
        dump_rows = sb("dump_rows", [P, NT * TOPK])
        minus_half = sb("minus_half", [P, NT])
        pad_rows = sb("pad_rows", [P, 2, ROW])
        ids_f = sb("ids_f", [P, NT])
        arena = sb("arena", [P, 4 * F_PAD])
        used = [0]

        def early(shape):
            n = int(np.prod(shape[1:]))
            flat = arena[:, used[0]:used[0] + n]
            used[0] += n
            if len(shape) == 2:
                return flat
            return flat.rearrange("p (a b) -> p a b", a=shape[1])

        gate_raw = early([P, 3, 2 * D])
        att_raw = early([P, 5, D])
        pos_raw = early([P, 4, D])
        wT = sb("wT", [P, 11, P])
        posT = sb("posT", [P, 512])
        cols = sb("cols", [P, 9])
        quarter_bq = sb("quarter_bq", [P, 1])
        qbias = sb("qbias", [P, 2])
        bv_row = sb("bv_row", [P, D])
        bo_row = sb("bo_row", [P, D])
        rb_row = sb("rb_row", [P, E])
        gate_w = sb("gate_w", [P, E])
        hnT = sb("hnT", [P, B * TP])
        HX = sb("HX", [P, B, TP])
        H2 = sb("H2", [P, B, TP])
        p_stack = sb("p_stack", [P, NPAIR, 512], F32R)
        x_in = early([P, NT, D])
        xT = early([P, T_IN + 1])
        gates = early([P, 3, T])
        fz = early([P, T])
        cell = early([P, T])
        hT = early([P, TP])
        stats = sb("stats", [P, NT, 6])
        mv = sb("mv", [P, NT, 2])
        vareps = sb("vareps", [P, NT])
        rstd = sb("rstd", [P, NT])
        x1 = sb("x1", [P, NT, D])
        n2 = sb("n2", [P, NT, D])
        hx_part = early([P, TP])
        hnb = sb("hnb", [P, TP])
        t_qu = sb("t_qu", [P, TP])
        t_qv = sb("t_qv", [P, TP])
        t_k = sb("t_k", [P, 512])
        hi_qu, lo_qu = sb("hi_qu", [P, TP], F32R), sb("lo_qu", [P, TP], F32R)
        hi_qv, lo_qv = sb("hi_qv", [P, TP], F32R), sb("lo_qv", [P, TP], F32R)
        hi_k, lo_k = sb("hi_k", [P, 512], F32R), sb("lo_k", [P, 512], F32R)
        qu_stack = sb("qu_stack", [P, NPAIR, TP], F32R)
        qv_stack = sb("qv_stack", [P, NPAIR, TP], F32R)
        k_stack = sb("k_stack", [P, NPAIR, TP], F32R)
        v_rows = sb("v_rows", [P, NT, D])
        v_diag = sb("v_diag", [P, NT, NH, D])
        pos_out = sb("pos_out", [P, 2, NT, POSW])
        pos_in = sb("pos_in", [P, 4, NT, T])
        score = sb("score", [P, 2, T])
        least = sb("least", [P, 2])
        probs = sb("probs", [P, 2, TP])
        rowsum = sb("rowsum", [P, UNITS])
        inv_rowsum = sb("inv_rowsum", [P, UNITS])
        probsT = sb("probsT", [P, 2, NT, TP])
        oT_raw = sb("oT_raw", [P, TP])
        inv_T = sb("inv_T", [NH, TP])
        oT = sb("oT", [P, TP])
        h2 = sb("h2", [P, NT, D])
        x2_row = sb("x2_row", [P, NT, ROW])
        x2 = x2_row[:, :, 0:D]
        x2T = sb("x2T", [P, TP])
        logits = sb("logits", [P, NT, E])
        top_v = sb("top_v", [P, NT, 8])
        top_i = sb("top_i", [P, NT, 8], U32)
        top_f = sb("top_f", [P, NT, TOPK])
        onehot = sb("onehot", [P, NT * TOPK, E])
        picked = sb("picked", [P, NT * TOPK, E])
        chosen = sb("chosen", [P, NT, E])
        before = sb("before", [P, NT + 1, E])
        place = sb("place", [P, NT, E])
        slot_f = sb("slot_f", [P, NT * TOPK])
        slot_i = sb("slot_i", [P, NT * TOPK], I32)
        shifted_v = sb("shifted_v", [P, NT, TOPK])
        exp_v = sb("exp_v", [P, NT, TOPK])
        exp_sum = sb("exp_sum", [P, NT])
        count_i = sb("count_i", [P, E], I32)
        tiles_f = sb("tiles_f", [P, E])
        tiles_end = sb("tiles_end", [P, E])
        shift_e = sb("shift_e", [P, E])
        pad_row = sb("pad_row", [1, E], I32)
        tile_e = sb("tile_e", [P, 64])
        tile_row = sb("tile_row", [1, 64])
        tile_fix = sb("tile_fix", [1, 64])
        table = sb("table", [1, 2, 64], I32)
        tile_expert = sb("tile_expert", [P, 1])
        same = sb("same", [P, 2, TOPK])
        row_weight = sb("row_weight", [P, 2, 2])
        row_id = sb("row_id", [P, 2, 2], I32)
        y_rows = sb("y_rows", [P, 2, 2, D])

        assert used[0] <= 4 * F_PAD

        F3 = FC * D

        def over(host, floats, name, shape, dt=F32):
            return nc.alloc_sbuf_tensor_at(name, shape, dt, offset=address[host] + 4 * floats)

        raw1 = [over("arena", i * F_PAD, f"raw1_{i}", [P, F]) for i in range(2)]
        raw2 = [over("arena", (2 + i) * F_PAD, f"raw2_{i}", [P, F]) for i in range(2)]
        raw3 = [sb("raw3_0", [P, F3]), over("v_diag", 0, "raw3_1", [P, F3])]
        hi1 = [over(n, 0, f"hi1_{n}", [P, F], F32R) for n in ("qv_stack", "qu_stack")]
        hi2 = [over(n, 0, f"hi2_{n}", [P, F], F32R) for n in ("p_stack", "k_stack")]
        hi3 = [over("pos_out", i * F3, f"hi3_{i}", [P, F3], F32R) for i in range(2)]
        lo1 = [over(n, 0, f"lo1_{n}", [P, F], F32R) for n in ("hnT", "HX")]
        lo2 = [over(n, F_PAD, f"lo2_{n}", [P, F], F32R) for n in ("hnT", "HX")]
        lo3 = [over("hnb", 0, "lo3_0", [P, F3], F32R), over("pos_in", 0, "lo3_1", [P, F3], F32R)]
        act_a = over("pos_in", F3, "act_a", [P, 2, 2 * GT])
        xe = over("pos_in", F3 + 4 * GT, "xe", [P, 2, 2, ROW])
        x_hi = over("spread_q_hi", 0, "x_hi", [P, 2, GT], F32R)
        x_lo = over("spread_q_lo", 0, "x_lo", [P, 2, GT], F32R)
        product = over("wT", 0, "product", [P, 2, 2 * GT])
        tile_cmp = over("arena", F_PAD, "tile_cmp", [P, 64, E])
        g_hi = over("probsT", 0, "g_hi", [P, 2, 2 * GT], F32R)
        g_lo = over("probsT", 4 * GT, "g_lo", [P, 2, 2 * GT], F32R)
        yT = over("posT", 0, "yT", [P, 2, GT])
        H2_flat = H2[:, :, :].rearrange("p b d -> p (b d)")

        gates_in, weights_in = sem("gates_in"), sem("weights_in")
        ident_ready = sem("ident_ready")
        pool_step, dve_step, act_step = sem("pool_step"), sem("dve_step"), sem("act_step")
        pool_gate, dve_gate, sp_gate = sem("pool_gate"), sem("dve_gate"), sem("sp_gate")
        consts_ready = sem("consts_ready")
        setup_ps, setup_sb = sem("setup_ps"), sem("setup_sb")
        x_loaded = sem("x_loaded")
        xT_ps, xT_sb = sem("xT_ps"), sem("xT_sb")
        conv_ps, conv_sb = sem("conv_ps"), sem("conv_sb")
        hT_ready, h_ps = sem("hT_ready"), sem("h_ps")
        var_ready, rstd_ready = sem("var_ready"), sem("rstd_ready")
        n2_ready, n2_ps, hn_ready = sem("n2_ready"), sem("n2_ps"), sem("hn_ready")
        hx_ready, hx_done = sem("hx_ready"), sem("hx_done")
        misc_ps, misc_free = sem("misc_ps"), sem("misc_free")
        hnb_ready = sem("hnb_ready")
        t_ready, hi_ready, split_ready = sem("t_ready"), sem("hi_ready"), sem("split_ready")
        v_diag_ready = sem("v_diag_ready")
        pos_ps, pos_sb = sem("pos_ps"), sem("pos_sb")
        pos_written = [sem(f"pos_written{i}") for i in range(2)]
        pos_read = [sem(f"pos_read{i}") for i in range(4)]
        content_ps, scored, probs_ready = sem("content_ps"), sem("scored"), sem("probs_ready")
        probsT_ps, probsT_sb, av_done = sem("probsT_ps"), sem("probsT_sb"), sem("av_done")
        inv_ready, oT_copied = sem("inv_ready"), sem("oT_copied")
        x2_ready, h2_kept = sem("x2_ready"), sem("h2_kept")
        x2_stored, chosen_ready = sem("x2_stored"), sem("chosen_ready")
        slot_ready, scattered = sem("slot_ready"), sem("scattered")
        table_ready, pads_written = sem("table_ready"), sem("pads_written")
        shift_ready, exp_ready = sem("shift_ready"), sem("exp_ready")
        zeroed = sem("zeroed")
        w_loaded = [sem(f"w_loaded{i}") for i in range(2)]
        w_hi_ready = sem("w_hi_ready")
        w1_lo_ready = sem("w1_lo_ready")
        w23_lo_ready = sem("w23_lo_ready")
        xe_loaded = [sem(f"xe_loaded{i}") for i in range(2)]
        xe_ps, x_hi_ready, x_ready = sem("xe_ps"), sem("x_hi_ready"), sem("x_ready")
        expert_ready, rows_known = sem("expert_ready"), sem("rows_known")
        a_ps, b_ps, down_ps = sem("a_ps"), sem("b_ps"), sem("down_ps")
        silu_ready, product_ready = sem("silu_ready"), sem("product_ready")
        g_hi_ready, g_lo_ready = sem("g_hi_ready"), sem("g_lo_ready")
        y_sb, yT_ps, y_rows_ready = sem("y_sb"), sem("yT_ps"), sem("y_rows_ready")
        y_stored, y_added, out_stored = sem("y_stored"), sem("y_added"), sem("out_stored")

        pos_rows = pos_dram.rearrange("h (s w) -> s h w", w=POSW)

        def shifted(h, t):
            base = pos_dram[h:h + 1, 0:TP * POSW]
            return bass.AP(base.tensor, base.offset + T + t * P * NPOS, [[NPOS, P], [1, T]])

        block = ctx.enter_context(nc.Block())
        COLUMNS = ["tok_b_z", "tok_b_f", "tok_b_o", "attn_bq", "attn_bk", "attn_pos_bias_u", "attn_pos_bias_v",
                   "attn_ln_w", "attn_ln_b"]
        GATES_IN, WEIGHTS_IN = 3 + 3, 5 + 2 + (len(COLUMNS) - 3) + 4

        @block.sync
        def _(sp):
            for i, n in enumerate(["tok_W_z", "tok_W_f", "tok_W_o"]):
                sp.dma_start(gate_raw[:, i, :], a[n].rearrange("h d k -> h (d k)")).then_inc(gates_in, 16)

            def load_x(b):
                wait(sp, xT_ps, b)
                sp.dma_start(x_in[:, 0:NT - 1, :], a["x"][bass.ds(b, 1), 0:(NT - 1) * P, :].rearrange(
                    "o (t p) d -> p (o t) d", p=P)).then_inc(x_loaded, 16)
                sp.dma_start(x_in[0:X_LAST, NT - 1, :], a["x"][bass.ds(b, 1), (NT - 1) * P:T_IN, :].rearrange(
                    "o p d -> (o p) d")).then_inc(x_loaded, 16)
            load_x(0)
            for i, n in enumerate(COLUMNS):
                sp.dma_start(cols[:, i:i + 1], a[n].rearrange("(p o) -> p o", o=1)).then_inc(gates_in if i < 3 else weights_in, 16)
            for i, n in enumerate(["attn_Wq", "attn_Wk", "attn_Wv", "attn_Wo", "attn_Wp"]):
                sp.dma_start(att_raw[:, i, :], a[n]).then_inc(weights_in, 16)
            sp.dma_start(pos_raw[:, 0:3, :], a["attn_pos_emb"][0:3 * P, :].rearrange("(t p) d -> p t d", p=P)).then_inc(weights_in, 16)
            sp.dma_start(pos_raw[0:NPOS - 3 * P, 3, :], a["attn_pos_emb"][3 * P:NPOS, :]).then_inc(weights_in, 16)
            for dst, n in ((bv_row, "attn_bv"), (bo_row, "attn_bo"), (rb_row, "ffn_routing_bias")):
                src = a[n].rearrange("(o n) -> o n", o=1)
                sp.dma_start(dst[:, :], src.to_broadcast([P, src.shape[1]])).then_inc(weights_in, 16)
            sp.dma_start(gate_w[:, :], a["ffn_gate_w"]).then_inc(weights_in, 16)
            sp.wait_ge(consts_ready, 1)
            sp.dma_start(sum_dram[NTILES * P:NTILES * P + GT, :].rearrange("(t p) d -> p t d", p=P), pad_rows[:, :, 0:D]).then_inc(zeroed, 16)
            with sp.Fori(1, B) as b:
                load_x(b)

            def write_pos(b, h):
                wait(sp, pos_sb, UNITS * b + NT * h + NT, sp_gate)
                wait(sp, pos_read[h % 4], 16 * NT * (2 * b - 1 + h // 4))
                sp.dma_start(pos_rows[:, h, :].rearrange("(t p) w -> p t w", p=P), pos_out[:, h % 2, :, :]).then_inc(
                    pos_written[h % 2], 16)

            def read_pos(b, h):
                wait(sp, scored, UNITS * b + NT * (h - 3))
                wait(sp, pos_written[h % 2], 16 * (4 * b + h // 2 + 1))
                for t in range(NT):
                    sp.dma_start(pos_in[:, h % 4, t, :], shifted(h, t)).then_inc(pos_read[h % 4], 16)

            def sp_body(b, att, prev, nxt):
                order = []
                if nxt:
                    done = {m: s for s, ms in POS_AT.items() for m in ms}
                    order += [(done[NT * h + NT - 1] + 0.5, write_pos, b + 1, h) for h in range(NH)]
                if att:
                    order += [(NT * h + 2.2, read_pos, b, h + 4) for h in range(4)]
                if nxt:
                    order += [(NT * h + 2.2 if att else 23.6 + h, read_pos, b + 1, h - 4) for h in range(4, NH)]
                if prev:
                    order += [(9.1, None, b, 0)]
                for _, what, bb, h in sorted(order, key=lambda o: o[0]):
                    if what is not None:
                        what(bb, h)
                        continue
                    wait(sp, x2_ready, bb)
                    sp.dma_start(xs_dram[bass.ds((bb - 1) * TP, TP), :].rearrange("(t p) d -> p t d", p=P),
                                 x2).then_inc(x2_stored, 16)

            def load_weights(w, s, w1, w2, w3a, w3b):
                wait(sp, w1_lo_ready, 2 * (w - 1))
                sp.dma_start(raw1[s][:, :], w1).then_inc(w_loaded[s], 16)
                wait(sp, w23_lo_ready, 4 * (w - 2) + 2)
                sp.dma_start(raw2[s][:, :], w2).then_inc(w_loaded[s], 16)
                wait(sp, w23_lo_ready, 4 * (w - 1))
                sp.dma_start(raw3[s][:, 0:F3 - D].rearrange("p (c d) -> p c d", d=D), w3a).then_inc(w_loaded[s], 16)
                sp.dma_start(raw3[s][0:F_LAST, F3 - D:F3], w3b).then_inc(w_loaded[s], 16)

            def load_shared_x(j, s):
                wait(sp, xe_ps, j - 1)
                sp.dma_start(xe[:, s, :, 0:D], xs_dram[bass.ds(j * GT, GT), :].rearrange("(t p) d -> p t d", p=P)).then_inc(xe_loaded[s], 16)

            sp_body(-1, False, False, True)
            sp_body(0, True, False, True)
            with sp.Fori(1, 1 + LOOP) as b:
                sp_body(b, True, True, True)
            sp.wait_ge(hx_done, B)
            load_weights(0, 0, a["ffn_sw1"], a["ffn_sw2"],
                         a["ffn_sw3"][0:(FC - 1) * P, :].rearrange("(c p) d -> p c d", p=P), a["ffn_sw3"][(FC - 1) * P:F, :])
            sp_body(B - 2, True, True, True)
            sp_body(B - 1, True, True, False)
            sp.wait_ge(scored, UNITS * B)
            sp.wait_ge(x2_stored, 16 * (B - 1))
            load_shared_x(0, 0)
            load_shared_x(1, 1)

            def load_routed_weights(w, s):
                e = sp.value_load(table[0:1, 0, bass.ds(w - 1, 1)], min_val=0, max_val=E - 1)
                load_weights(w, s, a["ffn_w1"][bass.ds(e, 1), :, :].rearrange("o d f -> (o d) f"),
                             a["ffn_w2"][bass.ds(e, 1), :, :].rearrange("o d f -> (o d) f"),
                             a["ffn_w3"][bass.ds(e, 1), 0:(FC - 1) * P, :].rearrange("o (c p) d -> p (o c) d", p=P),
                             a["ffn_w3"][bass.ds(e, 1), (FC - 1) * P:F, :].rearrange("o p d -> (o p) d"))

            def load_routed_x(r, s):
                wait(sp, xe_ps, r + SHARED - 1, sp_gate)
                wait(sp, rows_known, r - 1, sp_gate)
                row = sp.value_load(table[0:1, 1, bass.ds(r, 1)], min_val=0, max_val=ZERO_ROW)
                sp.dma_start(xe[:, s, :, :], xg_dram[bass.ds(row, GT), :].rearrange("(t p) d -> p t d", p=P)).then_inc(xe_loaded[s], 16)

            def store_y(j, s):
                sp.wait_ge(y_rows_ready, j + 1)
                sp.dma_start(sum_dram[bass.ds(j * GT, GT), :].rearrange("(t p) d -> p t d", p=P), y_rows[:, s, :, :]).then_inc(y_stored, 16)

            sp_body(B, False, True, False)
            sp.wait_ge(x2_stored, 16 * B)
            load_shared_x(2, 0)
            load_shared_x(3, 1)
            store_y(0, 0)
            with sp.Fori(1, SHARED // 2 - 3) as i:
                for s in range(2):
                    load_shared_x(2 * i + s + 2, s)
                    store_y(2 * i + s - 1, 1 - s)

            def write_pads(experts):
                for e in experts:
                    row = sp.value_load(pad_row[0:1, e:e + 1], min_val=0, max_val=ZERO_ROW - GT)
                    sp.dma_start(xg_dram[bass.ds(row, GT), :].rearrange("(t p) d -> p t d", p=P), pad_rows[:, :, :]).then_inc(pads_written, 16)

            sp.wait_ge(table_ready, 1)
            sp.wait_ge(scattered, 16 * B * NT * TOPK)
            for n, j in enumerate(range(SHARED - 6, SHARED - 2)):
                load_shared_x(j + 2, j % 2)
                store_y(j - 1, (j - 1) % 2)
                write_pads(range(n * E // 4, (n + 1) * E // 4))
                if n < 2:
                    load_routed_weights(n + 1, 1 - n)
            sp.dma_start(xg_dram[ZERO_ROW:ZERO_ROW + GT, :].rearrange("(t p) d -> p t d", p=P), pad_rows[:, :, :]).then_inc(pads_written, 16)
            sp.wait_ge(pads_written, 16 * (E + 1))
            for j in range(SHARED - 2, SHARED + 2):
                if j >= SHARED:
                    load_routed_weights(j - SHARED + 3, (j + 1) % 2)
                load_routed_x(j + 2 - SHARED, j % 2)
                if j <= SHARED:
                    store_y(j - 1, (j - 1) % 2)
            with sp.Fori(1, ROUTED // 2 - 1) as i:
                for s in range(2):
                    load_routed_weights(2 * i + s + 3, 1 - s)
                    load_routed_x(2 * i + s + 2, s)

            sp.wait_ge(y_added, 32 * ROUTED)
            for b in range(B):
                sp.dma_start(out[b, :, :], sum_dram[b * TP:b * TP + T, :]).then_inc(out_stored, 16)
            sp.wait_ge(out_stored, 16 * B)

        @block.gpsimd
        def _(pool):
            g = nc.gpsimd
            step = Steps(pool, pool_step, pool_gate)

            def pw(sem_, value):
                wait(pool, sem_, value, pool_gate)

            step.did(g.memset(ones[:], 1.0))
            step.settle()
            g.affine_select(out=ident[:], in_=ones[:], compare_op=ALU.is_equal, fill=0.0, base=0, pattern=[[-1, P]],
                            channel_multiplier=1).then_inc(ident_ready, 1)
            step.did(g.memset(template[:], 0.0))
            step.did(g.memset(pad_rows[:, :, :], 0.0))
            step.did(g.memset(x2_row[:, :, :], 0.0))
            step.did(g.memset(v_diag[:, :, :, :], 0.0))
            step.settle()
            step.did(g.affine_select(out=tri[:], in_=ones[:], compare_op=ALU.is_gt, fill=0.0, base=0,
                                     pattern=[[1, P]], channel_multiplier=-1))
            step.did(g.affine_select(out=head_rows[:], in_=ones[0:NH, :], compare_op=ALU.is_ge, fill=0.0, base=0,
                                     pattern=[[1, D]], channel_multiplier=-HD))
            for n, copies in enumerate(((0, 2), (1, 3), (0, 1), (2, 3))):
                tv = template[:, n, :].rearrange("p (i c f) -> p i c f", i=2, c=4)
                for c in copies:
                    step.did(g.memset(tv[:, :, c, :], 1.0))
            step.settle()
            step.did(g.affine_select(out=head_rows[:], in_=head_rows[:], compare_op=ALU.is_ge, fill=0.0, base=HD - 1,
                                     pattern=[[-1, D]], channel_multiplier=HD))
            for n, spread in enumerate((spread_q_hi, spread_q_lo, spread_k_hi, spread_k_lo)):
                for j in range(NPAIR):
                    step.did(g.affine_select(out=spread[:, j, :], in_=template[:, n, :], compare_op=ALU.is_equal, fill=0.0,
                                             base=-2 * HD * j, pattern=[[-HD, 2], [0, 4], [-1, HD]], channel_multiplier=1))
            step.did(g.iota(iota_e[:], pattern=[[1, E]], base=0, channel_multiplier=0, allow_small_or_imprecise_dtypes=True))
            step.did(g.iota(region_e[:], pattern=[[REGION, E]], base=0, channel_multiplier=0, allow_small_or_imprecise_dtypes=True))
            step.did(g.iota(iota_tile[:], pattern=[[1, 64]], base=0, channel_multiplier=0, allow_small_or_imprecise_dtypes=True))
            step.did(g.iota(dump_rows[:], pattern=[[P * TOPK, NT], [1, TOPK]], base=DUMP_ROW, channel_multiplier=TOPK,
                            allow_small_or_imprecise_dtypes=True))
            for t in range(2):
                step.did(g.iota(pad_rows[:, t, AT_ID:AT_ID + 1], pattern=[[1, 1]], base=NTILES * P + t * P, channel_multiplier=1,
                                allow_small_or_imprecise_dtypes=True))
            step.did(g.iota(ids_f[:], pattern=[[P, NT]], base=0, channel_multiplier=1, allow_small_or_imprecise_dtypes=True))
            step.did(g.memset(minus_half[:], -0.5))
            step.did(g.memset(before[:], 0.0))
            step.did(g.memset(hT[:, T:TP], 0.0))
            step.did(g.memset(probs[:, :, T:TP], 0.0))
            step.did(g.memset(pos_out[:, :, :, 0:1], 0.0))
            step.did(g.memset(posT[:, NPOS:512], 0.0))
            step.settle()
            step.did(g.affine_select(out=valid[:], in_=ones[:, 0:NT * TOPK], compare_op=ALU.is_gt, fill=0.0, base=T,
                                     pattern=[[-P, NT], [0, TOPK]], channel_multiplier=-1))
            step.did(g.affine_select(out=dump_rows[:], in_=dump_rows[:], compare_op=ALU.is_ge, fill=0.0, base=-T,
                                     pattern=[[P, NT], [0, TOPK]], channel_multiplier=1))
            step.settle()
            g.memset(vareps[:], 1.0).then_inc(consts_ready, 1)

            def inverse_root(n):
                pw(var_ready, n + 1)
                step.did(g.tensor_scalar_add(vareps[:], mv[:, :, 1], EPS))
                step.settle()
                g.tensor_tensor(rstd[:], vareps[:], minus_half[:], ALU.pow).then_inc(rstd_ready, 1)

            def pool_mixer(b):
                inverse_root(2 * b)
                inverse_root(2 * b + 1)
                pw(hx_ready, b + 1)
                g.tensor_tensor(HX[:, bass.ds(b, 1), :].rearrange("p o (t d) -> p (o t) d", d=D),
                                hx_part[:].rearrange("p (t d) -> p t d", d=D),
                                bo_row[:, :].unsqueeze(1).to_broadcast([P, NT, D]), ALU.add).then_inc(hx_done, 1)

            def split(sem_, n, t, hi, lo, w):
                pw(sem_, n)
                g.tensor_tensor(lo[:, 0:w], t[:, 0:w], hi[:, 0:w].bitcast(F32), ALU.subtract).then_inc(split_ready, 1)

            pw(weights_in, 16 * WEIGHTS_IN)
            split(t_ready, 1, t_k, hi_k, lo_k, 512)

            def copy_hn(b):
                pw(hn_ready, b + 1)
                g.tensor_copy(hnb[:, :], hnT[:, bass.ds(b * TP, TP)]).then_inc(hnb_ready, 1)

            PER = 2
            with pool.Fori(0, B - 1) as b:
                step.enter(b, PER)
                pool_mixer(b)
            step.leave(B - 1, PER)

            def diag(b, h):
                pw(av_done, NH * (b - 1) + h + 1)
                g.tensor_copy(v_diag[:, :, h, h * HD:(h + 1) * HD], v_rows[:, :, h * HD:(h + 1) * HD]).then_inc(v_diag_ready, 1)

            def split_low(w, s, piece):
                pw(w_hi_ready, 6 * w + piece + 1)
                raw, hi, lo = (raw2, hi2, lo2) if piece < 4 else (raw3, hi3, lo3)
                for rows, part in parts_of(piece):
                    ins = g.tensor_tensor(lo[s][0:rows, part], raw[s][0:rows, part], hi[s][0:rows, part].bitcast(F32), ALU.subtract)
                ins.then_inc(w23_lo_ready, 1)

            def pool_body(b, att, prev, nxt):
                started = not (isinstance(b, int) and b <= 0)
                if nxt:
                    pw(misc_ps, jobs_before(b) + 1)
                    split(hi_ready, 3 * b + 4, t_qv, hi_qv, lo_qv, TP)
                    split(hi_ready, 3 * b + 5, t_qu, hi_qu, lo_qu, TP)
                    split(hi_ready, 3 * b + 6, t_k, hi_k, lo_k, TP)
                if att and started:
                    for h in range(NH - 3, NH):
                        diag(b, h)
                if prev:
                    inverse_root(2 * B + b - 1)
                heads = list(range(NH - 3 if att else NH)) if nxt else []
                if nxt:
                    pw(misc_free, jobs_before(b) + 1 + [name for _, name, _ in side_jobs(prev, nxt)].index("v"))
                if nxt and not (isinstance(b, int) and b >= B - 2):
                    copy_hn(b + 2)
                for h in heads[:3]:
                    diag(b + 1, h)
                if isinstance(b, int) and b == B - 1:
                    pw(hnb_ready, B)
                    pw(misc_ps, jobs_before(B - 1))
                    for piece in range(2, 6):
                        split_low(0, 0, piece)
                if prev:
                    pw(slot_ready, b)
                    g.tensor_copy(H2[:, bass.ds(b - 1, 1), :].rearrange("p o (t d) -> p (o t) d", d=D), h2[:, :, :]).then_inc(h2_kept, 1)
                    for t in range(NT):
                        for k in range(TOPK):
                            c = t * TOPK + k
                            pool.indirect_dma_start(xg_dram[:, :], bass.IndirectOffsetOnAxis(slot_i[:, c:c + 1], 0),
                                                    x2_row[:, t, :], None).then_inc(scattered, 16)
                for h in heads[3:]:
                    diag(b + 1, h)

            PER = 1
            copy_hn(0)
            pool_mixer(B - 1)
            pool_body(-1, False, False, True)
            pool_body(0, True, False, True)
            with pool.Fori(1, 1 + LOOP) as b:
                step.enter(b - 1, PER)
                pool_body(b, True, True, True)
            step.leave(LOOP, PER)
            pool_body(B - 2, True, True, True)
            pool_body(B - 1, True, True, False)
            pool_body(B, False, True, False)

            def add_rows(r, s):
                pw(y_rows_ready, SHARED + r + 1)
                pw(y_added, 32 * r)
                for t in range(2):
                    pool.indirect_dma_start(sum_dram[:, :], bass.IndirectOffsetOnAxis(row_id[:, s, t:t + 1], 0),
                                            y_rows[:, s, t, :], None, compute_op=ALU.add).then_inc(y_added, 16)

            def pool_tile(r, s, split, add):
                if split:
                    for piece in range(2, 6):
                        split_low(r + 2, s, piece)
                if add:
                    add_rows(r - 1, 1 - s)

            for piece in range(2, 6):
                split_low(1, 1, piece)
            pool_tile(0, 0, True, False)
            pw(y_stored, 16 * SHARED)
            pw(zeroed, 16)
            pool_tile(1, 1, True, True)
            with pool.Fori(1, ROUTED // 2 - 1) as i:
                for s in range(2):
                    pool_tile(2 * i + s, s, True, True)
            pool_tile(ROUTED - 2, 0, True, True)
            pool_tile(ROUTED - 1, 1, False, True)
            add_rows(ROUTED - 1, 1)

        @block.tensor
        def _(pe):
            mm, tr = nc.tensor.matmul, nc.tensor.transpose
            pe.wait_ge(gates_in, 16 * GATES_IN)
            pe.wait_ge(ident_ready, 1)
            for i in range(3):
                for k in range(2):
                    ins = tr(bank[i // 2][:, (2 * i + k) % 4 * P:((2 * i + k) % 4 + 1) * P],
                             gate_raw[:, i, :].rearrange("h (d k) -> h k d", k=2)[:, k, :], ident[:])
                if i > 0:
                    ins.then_inc(setup_ps, 1)

            def pe_attention_setup():
                pe.wait_ge(weights_in, 16 * WEIGHTS_IN)
                pe.wait_ge(consts_ready, 1)
                for n in range(5):
                    ins = tr(bank[4 + n // 4][:, n % 4 * P:(n % 4 + 1) * P], att_raw[:, n, :], ident[:])
                    if n >= 3:
                        ins.then_inc(setup_ps, 1)
                for t in range(4):
                    rows = P if t < 3 else NPOS - 3 * P
                    ins = tr(bank[6][:, t * P:t * P + rows], pos_raw[0:rows, t, :], ident[0:rows, 0:rows])
                ins.then_inc(setup_ps, 1)
                pe.wait_ge(setup_sb, 5)
                mm(bank[7][:, :], wT[:, 10, :], posT[:, :], start=True, stop=True).then_inc(setup_ps, 1)
                pe.wait_ge(split_ready, 1)
                for j in range(NPAIR):
                    pe.wait_ge(setup_sb, 5 + j)
                    mm(bank[6 + j % 2][:, :], spread_k_hi[:, j, :], hi_k[:, :], start=True, stop=False)
                    mm(bank[6 + j % 2][:, :], spread_k_lo[:, j, :], lo_k[:, :], start=False, stop=True).then_inc(setup_ps, 1)

            def pe_gates(b):
                pe.wait_ge(x_loaded, 32 * b + 32)
                for t in range(NT):
                    rows = P if t < NT - 1 else X_LAST
                    ins = tr(bank[0][:, t * P:t * P + rows], x_in[0:rows, t, :], ident[0:rows, 0:rows])
                ins.then_inc(xT_ps, 1)
                pe.wait_ge(xT_sb, b + 1)
                for i in range(3):
                    mm(bank[1 + i][:, 0:T], wT[:, 2 * i, :], xT[:, 0:T], start=True, stop=False)
                    mm(bank[1 + i][:, 0:T], wT[:, 2 * i + 1, :], xT[:, 1:T_IN], start=False, stop=True).then_inc(conv_ps, 1)

            def pe_h(b):
                pe.wait_ge(hT_ready, b + 1)
                for t in range(NT):
                    ins = tr(bank[4][:, t * P:(t + 1) * P], hT[:, t * P:(t + 1) * P], ident[:])
                ins.then_inc(h_ps, 1)

            def pe_n2(b):
                pe.wait_ge(n2_ready, b + 1)
                for t in range(NT):
                    ins = tr(bank[5][:, t * P:(t + 1) * P], n2[:, t, :], ident[:])
                ins.then_inc(n2_ps, 1)
            pe.wait_ge(setup_sb, 2)
            pe_gates(0)
            pe_attention_setup()
            pe.wait_ge(setup_sb, 10)
            with pe.Fori(0, B - 1) as b:
                pe_h(b)
                pe_gates(b + 1)
                pe_n2(b)
            pe_h(B - 1)

            mi = bank[7]

            def side(b, pos_in_list, name, j):
                index = jobs_before(b) + pos_in_list
                wait(pe, misc_free, index)
                if name == "q":
                    pe.wait_ge(hnb_ready, b + 2)
                    ins = mm(mi[:, 0:TP], wT[:, 6, :], hnb[:, :], start=True, stop=True)
                elif name == "k":
                    ins = mm(mi[:, 0:TP], wT[:, 7, :], hnb[:, :], start=True, stop=True)
                elif name == "v":
                    for t in range(NT):
                        ins = mm(mi[:, t * P:(t + 1) * P], hnb[:, t * P:(t + 1) * P], wT[:, 8, :], start=True, stop=True)
                elif name in ("sqv", "squ", "sk"):
                    hi, lo, sh, sl = {"sqv": (hi_qv, lo_qv, spread_q_hi, spread_q_lo),
                                      "squ": (hi_qu, lo_qu, spread_q_hi, spread_q_lo),
                                      "sk": (hi_k, lo_k, spread_k_hi, spread_k_lo)}[name]
                    if j == 0:
                        pe.wait_ge(split_ready, 3 * b + {"sqv": 5, "squ": 6, "sk": 7}[name])
                    mm(mi[:, 0:TP], sh[:, j, :], hi[:, 0:TP], start=True, stop=False)
                    ins = mm(mi[:, 0:TP], sl[:, j, :], lo[:, 0:TP], start=False, stop=True)
                elif name == "rt":
                    pe.wait_ge(inv_ready, b)
                    for t in range(NT):
                        ins = tr(mi[0:NH, t * P:(t + 1) * P], inv_rowsum[:].rearrange("p (h t) -> p t h", t=NT)[:, t, :], ident[:])
                elif name == "rb":
                    ins = mm(mi[:, 0:TP], head_rows[:, :], inv_T[:, :], start=True, stop=True)
                elif name == "wo":
                    for t in range(NT):
                        ins = mm(mi[:, t * P:(t + 1) * P], oT[:, t * P:(t + 1) * P], wT[:, 9, :], start=True, stop=True)
                elif name == "x2t":
                    pe.wait_ge(x2_ready, b)
                    for t in range(NT):
                        ins = tr(mi[:, t * P:(t + 1) * P], x2[:, t, :], ident[:])
                elif name == "gate":
                    for t in range(NT):
                        ins = mm(mi[:, t * E:(t + 1) * E], x2T[:, t * P:(t + 1) * P], gate_w[:, :], start=True, stop=True)
                elif name == "count":
                    pe.wait_ge(chosen_ready, b)
                    flat = chosen[:, :, :].rearrange("p t e -> p (t e)")
                    mm(mi[:, 0:NT * E], tri[:, :], flat, start=True, stop=True)
                    ins = mm(mi[:, NT * E:2 * NT * E], ones[:, :], flat, start=True, stop=True)
                ins.then_inc(misc_ps, 1)

            def pe_body(b, att, prev, nxt, slots=range(UNITS + 2)):
                jobs = side_jobs(prev, nxt)
                where = {(name, j): i for i, (_, name, j) in enumerate(jobs)}
                started = not (isinstance(b, int) and b <= 0)
                for s in slots:
                    u = UNITS * b + s
                    for i, (at, name, j) in enumerate(jobs):
                        if at == s:
                            side(b, i, name, j)
                    if (att and s < UNITS - 1) or (nxt and s == UNITS - 1):
                        h, t = (s + 1) // NT % NH, (s + 1) % NT
                        pair, half = h // 2, 64 * (h % 2)
                        wait(pe, scored, u)
                        if h % 2 == 0 and t == 0 and s == UNITS - 1:
                            pe.wait_ge(misc_free, jobs_before(b) + where["squ", 0] + 1)
                        elif pair == NPAIR - 1 and h % 2 == 0 and t == 0:
                            pe.wait_ge(misc_free, jobs_before(b))
                        mm(bank[(s + 1) % 2][:, 0:T], qu_stack[half:half + 64, pair, t * P:(t + 1) * P],
                           k_stack[half:half + 64, pair, 0:T], start=True, stop=True).then_inc(content_ps, 1)
                    if nxt:
                        for m in POS_AT.get(s, []):
                            h1, t1 = m // NT, m % NT
                            pair, half = h1 // 2, 64 * (h1 % 2)
                            if m % (2 * NT) == 0:
                                pe.wait_ge(misc_free, jobs_before(b) + where["sqv", pair] + 1)
                            wait(pe, pos_sb, UNITS * (b + 1) + m - 1)
                            mm(bank[2 + m % 2][:, :], qv_stack[half:half + 64, pair, t1 * P:(t1 + 1) * P],
                               p_stack[half:half + 64, pair, :], start=True, stop=True).then_inc(pos_ps, 1)
                    if (att and 1 <= s < UNITS) or (s == 0 and started):
                        wait(pe, probs_ready, u)
                        wait(pe, probsT_sb, u - 2)
                        for c in range(NT):
                            ins = tr(bank[4 + (s + 1) % 2][:, c * P:(c + 1) * P], probs[:, (s + 1) % 2, c * P:(c + 1) * P], ident[:])
                        ins.then_inc(probsT_ps, 1)
                    if (att and 5 <= s < UNITS) or (s < 5 and started):
                        gh = NH * b + (s - 5) // NT
                        hh, c = (s - 5) // NT % NH, (s - 5) % NT
                        if c == 0:
                            wait(pe, probsT_sb, NT * gh + NT)
                            pe.wait_ge(v_diag_ready, gh + 1)
                            if hh == 0:
                                wait(pe, oT_copied, b)
                        rows = P if c < NT - 1 else T_LAST
                        ins = mm(bank[6][:, 0:TP], v_diag[0:rows, c, hh, :], probsT[0:rows, hh % 2, c, :],
                                 start=hh == 0 and c == 0, stop=hh == NH - 1 and c == NT - 1)
                        if c == NT - 1:
                            ins.then_inc(av_done, 1)

            pe_body(-1, False, False, True, FIRST)
            pe.wait_ge(hn_ready, B - 1)
            pe_n2(B - 1)
            pe_body(-1, False, False, True, AFTER_FIRST)
            pe_body(0, True, False, True)
            with pe.Fori(1, 1 + LOOP) as b:
                pe_body(b, True, True, True)
            pe_body(B - 2, True, True, True)
            pe_body(B - 1, True, True, False)
            pe_body(B, False, True, False, ATTENTION_END)

            def late_slot(j, c):
                if isinstance(j, int) and (j, c) in SLOT_IN_TILE:
                    pe_body(B, False, True, False, [SLOT_IN_TILE[j, c]])

            def chunks(c):
                return [k for k in (2 * c, 2 * c + 1) if k < FC]

            def width(k):
                return P if k < FC - 1 else F_LAST

            def transposes(j, s, n):
                pe.wait_ge(xe_loaded[s], 16 * n)
                wait(pe, x_ready, j)
                for t in range(2):
                    ins = tr(bank[6][:, t * P:(t + 1) * P], xe[:, s, t, 0:D], ident[:])
                ins.then_inc(xe_ps, 1)

            def y_transposes(j, s):
                wait(pe, y_sb, j + 1)
                if isinstance(j, int) and j == 0:
                    pe.wait_ge(misc_free, jobs_before(B) + J_PREV)
                wait(pe, y_rows_ready, j)
                for t in range(2):
                    ins = tr(bank[7][:, t * P:(t + 1) * P], yT[:, s, t * P:(t + 1) * P], ident[:])
                ins.then_inc(yT_ps, 1)

            def up(s, c, first_bank, hi, lo, sem_):
                for i, k in enumerate(chunks(c)):
                    dst = bank[first_bank + c % 2][0:width(k), i * GT:(i + 1) * GT]
                    cols_ = slice(k * P, k * P + width(k))
                    mm(dst, hi[:, cols_], x_hi[:, s, :], start=True, stop=False)
                    mm(dst, hi[:, cols_], x_lo[:, s, :], start=False, stop=False)
                    ins = mm(dst, lo[:, cols_], x_hi[:, s, :], start=False, stop=True)
                ins.then_inc(sem_, 1)

            def down(j, s, ws, w, c):
                if c == 0:
                    wait(pe, y_sb, j - 1)
                    if w is not None:
                        wait(pe, w23_lo_ready, 4 * w + 3)
                if c == (FC + 1) // 4 and w is not None:
                    wait(pe, w23_lo_ready, 4 * w + 4)
                pe.wait_ge(g_lo_ready, PAIRS * j + c + 1)
                for i, k in enumerate(chunks(c)):
                    dst, rows = bank[4 + s][:, 0:GT], width(k)
                    wh, wl = hi3[ws][0:rows, k * D:(k + 1) * D], lo3[ws][0:rows, k * D:(k + 1) * D]
                    gh, gl = (x_[0:rows, c % 2, i * GT:(i + 1) * GT] for x_ in (g_hi, g_lo))
                    mm(dst, wh, gh, start=k == 0, stop=False)
                    mm(dst, wh, gl, start=False, stop=False)
                    ins = mm(dst, wl, gh, start=False, stop=k == FC - 1)
                ins.then_inc(down_ps, 1)

            def tile(j, s, ws, w, prev_ws, after):
                first = isinstance(j, int) and j == 0
                wait(pe, x_ready, j + 1)
                for c in range(PAIRS):
                    if w is not None and c == 0:
                        pe.wait_ge(w1_lo_ready, 2 * w + 2)
                    wait(pe, silu_ready, PAIRS * j + c - 1)
                    up(s, c, 0, hi1[ws], lo1[ws], a_ps)
                    if w is not None and c == 0:
                        pe.wait_ge(w23_lo_ready, 4 * w + 2)
                    wait(pe, product_ready, PAIRS * j + c - 1)
                    up(s, c, 2, hi2[ws], lo2[ws], b_ps)
                    if c >= 2:
                        down(j, s, ws, w, c - 2)
                    elif not first:
                        down(j - 1, 1 - s, prev_ws, None, PAIRS - 2 + c)
                    if c == 1 and after is not None:
                        transposes(j + 1, 1 - s, after)
                    if c == 3 and not first:
                        y_transposes(j - 1, 1 - s)
                    late_slot(j, c)

            pe.wait_ge(scored, UNITS * B)
            pe.wait_ge(pos_sb, UNITS * B)
            pe.wait_ge(probsT_sb, UNITS * B)
            pe.wait_ge(oT_copied, B)
            transposes(0, 0, 1)
            tile(0, 0, 0, 0, 0, 1)
            tile(1, 1, 0, None, 0, 2)
            with pe.Fori(1, SHARED // 2) as i:
                for s in range(2):
                    tile(2 * i + s, s, 0, None, 0, i + 1 + s)
            tile(SHARED, 0, 1, 1, 0, SHARED // 2 + 1)
            tile(SHARED + 1, 1, 0, 2, 1, SHARED // 2 + 2)
            HALF = (SHARED + ROUTED) // 2
            with pe.Fori(SHARED // 2 + 1, HALF - 1) as i:
                for s in range(2):
                    tile(2 * i + s, s, 1 - s, 2 * i + s - SHARED + 1, s, i + 1 + s)
            tile(2 * HALF - 2, 0, 1, ROUTED - 1, 0, HALF)
            tile(2 * HALF - 1, 1, 0, ROUTED, 1, None)
            down(2 * HALF - 1, 1, 0, None, PAIRS - 2)
            down(2 * HALF - 1, 1, 0, None, PAIRS - 1)
            y_transposes(2 * HALF - 1, 1)

        @block.scalar
        def _(act):
            f = nc.scalar.activation
            step = Steps(act, act_step)
            act.wait_ge(gates_in, 16 * GATES_IN)
            for n in range(2):
                act.wait_ge(setup_ps, n + 1)
                w = 4 - 2 * n
                nc.scalar.copy(wT[:, 4 * n:4 * n + w, :].rearrange("p a b -> p (a b)"), bank[n][:, 0:w * P]).then_inc(setup_sb, 1)

            def act_attention_setup():
                act.wait_ge(setup_ps, 3)
                nc.scalar.copy(wT[:, 6:10, :].rearrange("p a b -> p (a b)"), bank[4][:, :]).then_inc(setup_sb, 1)
                act.wait_ge(setup_ps, 4)
                nc.scalar.copy(wT[:, 10, :], bank[5][:, 0:P]).then_inc(setup_sb, 1)
                act.wait_ge(setup_ps, 5)
                nc.scalar.copy(posT[:, 0:NPOS], bank[6][:, 0:NPOS]).then_inc(setup_sb, 1)
                act.wait_ge(setup_ps, 6)
                nc.scalar.copy(hi_k[:, :], bank[7][:, :])
                nc.scalar.copy(t_k[:, :], bank[7][:, :]).then_inc(t_ready, 1)
                step.did(nc.scalar.mul(qbias[:, :], cols[:, 5:7], -0.25))
                step.did(nc.scalar.mul(quarter_bq[:, :], cols[:, 3:4], -0.25))
                step.settle()
                f(qbias[:, :], qbias[:, :], ACT.Identity, bias=quarter_bq[:, :]).then_inc(setup_sb, 1)
                for j in range(NPAIR):
                    act.wait_ge(setup_ps, 7 + j)
                    nc.scalar.copy(p_stack[:, j, :], bank[6 + j % 2][:, :]).then_inc(setup_sb, 1)

            def act_gates(b):
                act.wait_ge(xT_ps, b + 1)
                nc.scalar.copy(xT[:, 0:T_IN], bank[0][:, 0:T_IN]).then_inc(xT_sb, 1)
                for i, fn in enumerate((ACT.Tanh, ACT.Sigmoid, ACT.Sigmoid)):
                    act.wait_ge(conv_ps, 3 * b + i + 1)
                    if i == 0:
                        wait(act, hT_ready, b)
                    f(gates[:, i, :], bank[1 + i][:, 0:T], fn, bias=cols[:, i:i + 1]).then_inc(conv_sb, 1)

            def act_hn(b):
                act.wait_ge(n2_ps, b + 1)
                f(hnT[:, bass.ds(b * TP, TP)], bank[5][:, 0:TP], ACT.Identity, bias=cols[:, 8:9],
                  scale=cols[:, 7:8]).then_inc(hn_ready, 1)
            act_gates(0)
            act_attention_setup()
            with act.Fori(0, B - 1) as b:
                act_gates(b + 1)
                act_hn(b)
            mi = bank[7]

            def act_side(b, i, name, j):
                n = jobs_before(b) + i
                if name == "q":
                    act.wait_ge(misc_ps, n + 1)
                    wait(act, split_ready, 3 * b + 4)
                    f(t_qv[:, :], mi[:, 0:TP], ACT.Identity, bias=qbias[:, 1:2], scale=-0.25).then_inc(t_ready, 1)
                    f(t_qu[:, :], mi[:, 0:TP], ACT.Identity, bias=qbias[:, 0:1], scale=-0.25).then_inc(misc_free, 1)
                    act.wait_ge(t_ready, b + 3)
                    nc.scalar.copy(hi_qv[:, :], t_qv[:, :]).then_inc(hi_ready, 1)
                    act.wait_ge(misc_free, n + 1)
                    nc.scalar.copy(hi_qu[:, :], t_qu[:, :]).then_inc(hi_ready, 1)
                elif name == "k":
                    act.wait_ge(misc_ps, n + 1)
                    f(t_k[:, 0:TP], mi[:, 0:TP], ACT.Identity, bias=cols[:, 4:5]).then_inc(misc_free, 1)
                    act.wait_ge(misc_free, n + 1)
                    nc.scalar.copy(hi_k[:, 0:TP], t_k[:, 0:TP]).then_inc(hi_ready, 1)
                elif name in ("sqv", "squ", "sk"):
                    act.wait_ge(misc_ps, n + 1)
                    dst = {"sqv": qv_stack, "squ": qu_stack, "sk": k_stack}[name]
                    nc.scalar.copy(dst[:, j, :], mi[:, 0:TP]).then_inc(misc_free, 1)
                elif name == "x2t":
                    act.wait_ge(misc_ps, n + 1)
                    nc.scalar.copy(x2T[:, :], mi[:, 0:TP]).then_inc(misc_free, 1)

            def split_high(w, s, piece, loads):
                if piece == 0:
                    act.wait_ge(w_loaded[s], 64 * loads)
                raw, hi = ((raw1, hi1), (raw2, hi2), (raw3, hi3))[piece // 2]
                for rows, part in parts_of(piece):
                    ins = nc.scalar.copy(hi[s][0:rows, part], raw[s][0:rows, part])
                ins.then_inc(w_hi_ready, 1)

            def act_body(b, att, prev, nxt, slots=range(UNITS + 2)):
                jobs = side_jobs(prev, nxt)
                for s in slots:
                    u = UNITS * b + s
                    if nxt:
                        for m in POS_AT.get(s - 1, []):
                            h1, t1 = m // NT, m % NT
                            act.wait_ge(pos_ps, UNITS * (b + 1) + m + 1)
                            if t1 == 0:
                                wait(act, pos_written[h1 % 2], 16 * (4 * (b + 1) + h1 // 2))
                            nc.scalar.copy(pos_out[:, h1 % 2, t1, 1:POSW], bank[2 + m % 2][:, 0:NPOS]).then_inc(pos_sb, 1)
                    for i, (at, name, j) in enumerate(jobs):
                        if at == s:
                            act_side(b, i, name, j)
                    if att and s < UNITS:
                        act.wait_ge(scored, u + 1)
                        wait(act, probsT_ps, u - 1)
                        if s == 0:
                            wait(act, inv_ready, b)
                        f(probs[:, s % 2, 0:T], score[:, s % 2, :], ACT.Exp, bias=least[:, s % 2:s % 2 + 1], scale=-1.0,
                          accum_out=rowsum[:, s:s + 1]).then_inc(probs_ready, 1)
                    if isinstance(b, int) and b == B - 1 and s in SHARED_SPLITS:
                        piece = SHARED_SPLITS.index(s)
                        if piece == 4:
                            for i in range(2):
                                act.wait_ge(pos_written[i], 16 * NH * B // 2)
                        split_high(0, 0, piece, 1)
                    if s == 4 and prev:
                        act.wait_ge(av_done, NH * b)
                        nc.scalar.copy(oT_raw[:, :], bank[6][:, 0:TP]).then_inc(oT_copied, 1)
                    if s == 14 and prev:
                        act.wait_ge(shift_ready, b)
                        f(exp_v[:, :, :], shifted_v[:, :, :], ACT.Exp).then_inc(exp_ready, 1)

            act_body(-1, False, False, True, FIRST)
            act_hn(B - 1)
            act_body(-1, False, False, True, AFTER_FIRST)
            act_body(0, True, False, True)
            with act.Fori(1, 1 + LOOP) as b:
                act_body(b, True, True, True)
            act_body(B - 2, True, True, True)
            act_body(B - 1, True, True, False)
            act_body(B, False, True, False, ATTENTION_END)

            def late_slot(j, c):
                if isinstance(j, int) and (j, c) in SLOT_IN_TILE:
                    act_body(B, False, True, False, [SLOT_IN_TILE[j, c]])

            def g_high(j, s, c):
                act.wait_ge(product_ready, PAIRS * j + c + 1)
                wait(act, down_ps, PAIRS * j + c - 1)
                rows, w = (P, 2 * GT) if 2 * c + 1 < FC else (F_LAST, GT)
                nc.scalar.copy(g_hi[0:rows, c % 2, 0:w], product[0:rows, c % 2, 0:w]).then_inc(g_hi_ready, 1)

            def x_high(j, s):
                act.wait_ge(xe_ps, j + 1)
                wait(act, b_ps, PAIRS * (j - 1))
                nc.scalar.copy(x_hi[:, s, :], bank[6][:, 0:GT]).then_inc(x_hi_ready, 1)

            def copy_yT(j, s):
                act.wait_ge(down_ps, PAIRS * (j + 1))
                wait(act, yT_ps, j - 1)
                nc.scalar.copy(yT[:, s, :], bank[4 + s][:, 0:GT]).then_inc(y_sb, 1)

            def act_tile(j, s, split, loads, nxt):
                first = isinstance(j, int) and j == 0
                for c in range(PAIRS):
                    rows, w = (P, 2 * GT) if 2 * c + 1 < FC else (F_LAST, GT)
                    if c > 0:
                        g_high(j, s, c - 1)
                    elif not first:
                        g_high(j - 1, 1 - s, PAIRS - 1)
                    act.wait_ge(a_ps, PAIRS * j + c + 1)
                    wait(act, product_ready, PAIRS * j + c - 1)
                    f(act_a[0:rows, c % 2, 0:w], bank[c % 2][0:rows, 0:w], ACT.Silu).then_inc(silu_ready, 1)
                    if c == 2 and not first:
                        copy_yT(j - 1, 1 - s)
                    if c == 2 and nxt:
                        x_high(j + 1, 1 - s)
                    if split is not None:
                        split_high(split, s, c, loads)
                    late_slot(j, c)

            x_high(0, 0)
            act_tile(0, 0, None, None, True)
            act_tile(1, 1, None, None, True)
            with act.Fori(1, SHARED // 2 - 1) as i:
                for s in range(2):
                    act_tile(2 * i + s, s, None, None, True)
            act_tile(SHARED - 2, 0, None, None, True)
            act_tile(SHARED - 1, 1, 1, 1, True)
            HALF = (SHARED + ROUTED) // 2
            with act.Fori(SHARED // 2, HALF - 1) as i:
                for s in range(2):
                    act_tile(2 * i + s, s, 2 * i + s - SHARED + 2, i - SHARED // 2 + 2, True)
            act_tile(2 * HALF - 2, 0, ROUTED, ROUTED // 2 + 1, True)
            act_tile(2 * HALF - 1, 1, None, None, False)
            g_high(2 * HALF - 1, 1, PAIRS - 1)
            copy_yT(2 * HALF - 1, 1)

        @block.vector
        def _(dve):
            v = nc.vector
            step = Steps(dve, dve_step)

            def norm_stats(srcs):
                for t, src in enumerate(srcs):
                    step.did(v.bn_stats(stats[:, t, :], src))
                step.settle(dve_gate)
                for t in range(NT):
                    ins = v.bn_aggr(mv[:, t, :], stats[:, t, :])
                    if t == NT - 1:
                        ins.then_inc(var_ready, 1)

            def normalise(dst, srcs, n, sem_):
                dve.wait_ge(rstd_ready, n + 1)
                for t, src in enumerate(srcs):
                    ins = v.tensor_scalar(dst[:, t, :], src, mv[:, t, 0:1], rstd[:, t:t + 1], ALU.subtract, ALU.mult)
                    if sem_ is None:
                        step.did(ins)
                if sem_ is not None:
                    ins.then_inc(sem_, 1)

            def dve_scan(b):
                dve.wait_ge(conv_sb, 3 * b + 2)
                step.did(v.scalar_tensor_tensor(out=fz[:, :], in0=gates[:, 1, :], scalar=1.0, in1=gates[:, 0, :],
                                                op0=ALU.subtract, op1=ALU.mult))
                step.settle()
                step.did(v.tensor_tensor_scan(cell[:, :], gates[:, 1, :], fz[:, :], 0.0, ALU.mult, ALU.subtract))
                step.settle()
                dve.wait_ge(conv_sb, 3 * b + 3)
                v.tensor_tensor(hT[:, 0:T], cell[:, :], gates[:, 2, :], ALU.mult).then_inc(hT_ready, 1)

            def dve_norms(b):
                dve.wait_ge(h_ps, b + 1)
                h_rows = [bank[4][:, t * P:(t + 1) * P] for t in range(NT)]
                x1_rows = [x1[:, t, :] for t in range(NT)]
                norm_stats(h_rows)
                normalise(x1, h_rows, 2 * b, None)
                step.settle()
                norm_stats(x1_rows)
                wait(dve, hx_done, b)
                v.tensor_tensor(hx_part[:, :], bank[4][:, 0:TP], x1[:, :, :].rearrange("p t d -> p (t d)"), ALU.add).then_inc(hx_ready, 1)
                wait(dve, n2_ps, b)
                normalise(n2, x1_rows, 2 * b + 1, n2_ready)
            dve.wait_ge(consts_ready, 1)
            dve_scan(0)
            PER = 2 + 3 + 3 + 3
            with dve.Fori(0, B - 1) as b:
                step.enter(b, PER)
                dve_norms(b)
                dve_scan(b + 1)
            step.leave(B - 1, PER)
            dve_norms(B - 1)
            dve.wait_ge(setup_sb, 10)

            mi = bank[7]

            def dve_side(b, i, name, part):
                n = jobs_before(b) + i
                if name not in ("v", "rt", "rb", "wo", "gate", "count"):
                    return
                if part == 0:
                    dve.wait_ge(misc_ps, n + 1)
                if (name, part) == ("v", 0):
                    wait(dve, v_diag_ready, NH * (b + 1))
                    v.tensor_tensor(v_rows[:, :, :], mi[:, 0:TP].rearrange("p (t d) -> p t d", t=NT),
                                    bv_row[:, :].unsqueeze(1).to_broadcast([P, NT, D]), ALU.add).then_inc(misc_free, 1)
                elif (name, part) == ("rt", 0):
                    v.tensor_copy(inv_T[:, :], mi[0:NH, 0:TP]).then_inc(misc_free, 1)
                elif (name, part) == ("rb", 0):
                    dve.wait_ge(oT_copied, b)
                    v.tensor_tensor(oT[:, :], oT_raw[:, :], mi[:, 0:TP], ALU.mult).then_inc(misc_free, 1)
                elif (name, part) == ("wo", 0):
                    wait(dve, h2_kept, b - 1)
                    wait(dve, x2_stored, 16 * (b - 1))
                    wait(dve, scattered, 16 * NT * TOPK * (b - 1))
                    v.tensor_tensor(h2[:, :, :].rearrange("p t d -> p (t d)"), mi[:, 0:TP],
                                    HX[:, bass.ds(b - 1, 1), :].rearrange("p o d -> p (o d)"), ALU.add).then_inc(misc_free, 1)
                    dve.wait_ge(misc_free, n + 1)
                    norm_stats([h2[:, t, :] for t in range(NT)])
                elif (name, part) == ("wo", 1):
                    normalise(x2, [h2[:, t, :] for t in range(NT)], 2 * B + b - 1, x2_ready)
                elif (name, part) == ("gate", 0):
                    v.tensor_tensor(logits[:, :, :], mi[:, 0:NT * E].rearrange("p (t e) -> p t e", t=NT),
                                    rb_row[:, :].unsqueeze(1).to_broadcast([P, NT, E]), ALU.add).then_inc(misc_free, 1)
                    wait(dve, misc_free, n + 1, dve_gate)
                    for t in range(NT):
                        step.did(v.max(top_v[:, t, :], logits[:, t, :]))
                    step.settle(dve_gate)
                    for t in range(NT):
                        step.did(v.max_index(top_i[:, t, :], top_v[:, t, :], logits[:, t, :]))
                elif (name, part) == ("gate", 1):
                    step.settle()
                    wait(dve, exp_ready, b - 1)
                    v.tensor_tensor(shifted_v[:, :, :], top_v[:, :, 0:TOPK], top_v[:, :, 0:1].to_broadcast([P, NT, TOPK]),
                                    ALU.subtract).then_inc(shift_ready, 1)
                    step.did(v.tensor_copy(top_f[:, :, :], top_i[:, :, 0:TOPK]))
                    step.settle()
                    ranks = top_f[:, :, :].rearrange("p t k -> p (t k)")
                    step.did(v.tensor_tensor(onehot[:, :, :], ranks.unsqueeze(2).to_broadcast([P, NT * TOPK, E]),
                                             iota_e[:, :].unsqueeze(1).to_broadcast([P, NT * TOPK, E]), ALU.is_equal))
                elif (name, part) == ("gate", 2):
                    step.settle()
                    step.did(v.tensor_tensor(onehot[:, :, :], onehot[:, :, :],
                                             valid[:, :].unsqueeze(2).to_broadcast([P, NT * TOPK, E]), ALU.mult))
                    step.settle()
                    v.tensor_reduce(chosen[:, :, :], onehot[:, :, :].rearrange("p (t k) e -> p t e k", t=NT), AX.X,
                                    ALU.add).then_inc(chosen_ready, 1)
                elif (name, part) == ("count", 0):
                    for t in range(NT):
                        step.did(v.tensor_tensor(before[:, t + 1, :], before[:, t, :], mi[:, (NT + t) * E:(NT + t + 1) * E], ALU.add))
                        step.settle()
                    step.did(v.tensor_tensor(place[:, :, :], before[:, 0:NT, :], mi[:, 0:NT * E].rearrange("p (t e) -> p t e", t=NT), ALU.add))
                    step.settle()
                    v.tensor_copy(before[:, 0, :], before[:, NT, :]).then_inc(misc_free, 1)
                elif (name, part) == ("count", 1):
                    dve.wait_ge(misc_free, n + 1)
                    step.did(v.tensor_tensor(place[:, :, :], place[:, :, :], region_e[:, :].unsqueeze(1).to_broadcast([P, NT, E]), ALU.add))
                    step.settle()
                    step.did(v.tensor_tensor(picked[:, :, :].rearrange("p (t k) e -> p t k e", t=NT),
                                             onehot[:, :, :].rearrange("p (t k) e -> p t k e", t=NT),
                                             place[:, :, :].unsqueeze(2).to_broadcast([P, NT, TOPK, E]), ALU.mult))
                    step.settle()
                    step.did(v.tensor_reduce(slot_f[:, :], picked[:, :, :], AX.X, ALU.add))
                elif (name, part) == ("count", 2):
                    step.settle()
                    step.did(v.tensor_tensor(slot_f[:, :], slot_f[:, :], dump_rows[:, :], ALU.add))
                    dve.wait_ge(exp_ready, b)
                    step.did(v.tensor_reduce(exp_sum[:, :], exp_v[:, :, :], AX.X, ALU.add))
                    step.settle()
                    step.did(v.reciprocal(exp_sum[:, :], exp_sum[:, :]))
                    step.did(v.tensor_copy(x2_row[:, :, AT_E:AT_E + TOPK], top_f[:, :, :]))
                    step.did(v.tensor_copy(x2_row[:, :, AT_ID:AT_ID + 1], ids_f[:, :].unsqueeze(2)))
                    step.did(v.tensor_scalar(ids_f[:, :], ids_f[:, :], float(TP), None, ALU.add))
                    step.settle()
                    step.did(v.tensor_tensor(x2_row[:, :, AT_W:AT_W + TOPK], exp_v[:, :, :],
                                             exp_sum[:, :].unsqueeze(2).to_broadcast([P, NT, TOPK]), ALU.mult))
                    v.tensor_copy(slot_i[:, :], slot_f[:, :]).then_inc(slot_ready, 1)

            def split_low(w, s, piece):
                dve.wait_ge(w_hi_ready, 6 * w + piece + 1)
                for rows, part in parts_of(piece):
                    v.tensor_tensor(lo1[s][:, part], raw1[s][:, part], hi1[s][:, part].bitcast(F32), ALU.subtract).then_inc(w1_lo_ready, 1)

            def dve_body(b, att, prev, nxt, slots=range(UNITS + 2)):
                jobs = side_jobs(prev, nxt)
                started = not (isinstance(b, int) and b <= 0)
                for s in slots:
                    u = UNITS * b + s
                    h, t = s // NT, s % NT
                    if s == 0 and prev:
                        dve.wait_ge(probs_ready, UNITS * b)
                        v.reciprocal(inv_rowsum[:, :], rowsum[:, :]).then_inc(inv_ready, 1)
                    if att and s < UNITS:
                        dve.wait_ge(content_ps, u + 1)
                        if t == 0:
                            dve.wait_ge(pos_read[h % 4], 16 * NT * (2 * b + h // 4 + 1))
                        wait(dve, probs_ready, u - 1, dve_gate)
                        v.tensor_tensor_reduce(out=score[:, s % 2, :], in0=bank[s % 2][:, 0:T], in1=pos_in[:, h % 4, t, :],
                                               scale=1.0, scalar=3.0e38, op0=ALU.add, op1=ALU.min,
                                               accum_out=least[:, s % 2:s % 2 + 1]).then_inc(scored, 1)
                    if (att and 2 <= s < UNITS) or (s < 2 and started):
                        hh, tt = (s - 2) // NT % NH, (s - 2) % NT
                        dve.wait_ge(probsT_ps, u - 1)
                        if tt == 0:
                            wait(dve, av_done, NH * b + hh - 1)
                        v.tensor_copy(probsT[:, hh % 2, :, tt * P:(tt + 1) * P],
                                      bank[4 + s % 2][:, 0:TP].rearrange("p (c q) -> p c q", c=NT)).then_inc(probsT_sb, 1)
                    if isinstance(b, int) and b == B - 1 and s in (21, 22):
                        if s == 21:
                            dve.wait_ge(hnb_ready, B)
                        split_low(0, 0, s - 21)
                    for part in (2, 1, 0):
                        for i, (at, name, j) in enumerate(jobs):
                            if at == s - part:
                                dve_side(b, i, name, part)

            dve_body(-1, False, False, True)
            dve_body(0, True, False, True)
            with dve.Fori(1, 1 + LOOP) as b:
                step.enter(b - 1, DVE_PER_BATCH)
                dve_body(b, True, True, True)
            step.leave(LOOP, DVE_PER_BATCH)
            dve_body(B - 2, True, True, True)
            dve_body(B - 1, True, True, False)
            dve_body(B, False, True, False, ATTENTION_END)

            def late_slot(j, c):
                if isinstance(j, int) and (j, c) in SLOT_IN_TILE:
                    dve_body(B, False, True, False, [SLOT_IN_TILE[j, c]])

            def x_low(j, s):
                dve.wait_ge(x_hi_ready, j + 1)
                v.tensor_tensor(x_lo[:, s, :], bank[6][:, 0:GT], x_hi[:, s, :].bitcast(F32), ALU.subtract).then_inc(x_ready, 1)

            x_low(0, 0)

            def chain(ins):
                step.did(ins)
                step.settle()

            def tile_table(part):
                if part == 0:
                    chain(v.tensor_scalar(count_i[:, :], before[:, 0, :], float(GT - 1), None, ALU.add))
                    chain(v.tensor_scalar(count_i[:, :], count_i[:, :], GT.bit_length() - 1, None, ALU.logical_shift_right))
                    chain(v.tensor_copy(tiles_f[:, :], count_i[:, :]))
                    chain(v.tensor_tensor_scan(tiles_end[:, :], ones[:, 0:E], tiles_f[:, :], 0.0, ALU.mult, ALU.add))
                    chain(v.tensor_tensor(tiles_f[:, :], tiles_end[:, :], tiles_f[:, :], ALU.subtract))
                    chain(v.scalar_tensor_tensor(out=shift_e[:, :], in0=tiles_f[:, :], scalar=-float(GT), in1=region_e[:, :],
                                                 op0=ALU.mult, op1=ALU.add))
                    chain(v.tensor_tensor(pad_row[:, :], before[0:1, 0, :], region_e[0:1, :], ALU.add))
                each = [P, 64, E] if part < 3 else [1, 64, E]
                if part == 1:
                    chain(v.tensor_tensor(tile_cmp[:, :, :], iota_tile[:, :].unsqueeze(2).to_broadcast(each),
                                          tiles_end[:, :].unsqueeze(1).to_broadcast(each), ALU.is_ge))
                elif part == 2:
                    chain(v.tensor_reduce(tile_e[:, :], tile_cmp[:, :, :], AX.X, ALU.add))
                    chain(v.tensor_scalar(table[:, 0, :], tile_e[0:1, :], float(E - 1), None, ALU.min))
                elif part == 3:
                    chain(v.tensor_tensor(tile_cmp[0:1, :, :], tile_e[0:1, :].unsqueeze(2).to_broadcast(each),
                                          iota_e[0:1, :].unsqueeze(1).to_broadcast(each), ALU.is_equal))
                elif part == 4:
                    chain(v.tensor_tensor(tile_cmp[0:1, :, :], tile_cmp[0:1, :, :], shift_e[0:1, :].unsqueeze(1).to_broadcast(each), ALU.mult))
                elif part == 5:
                    chain(v.tensor_reduce(tile_row[:, :], tile_cmp[0:1, :, :], AX.X, ALU.add))
                    chain(v.scalar_tensor_tensor(out=tile_row[:, :], in0=iota_tile[0:1, :], scalar=float(GT), in1=tile_row[:, :],
                                                 op0=ALU.mult, op1=ALU.add))
                    chain(v.tensor_scalar(tile_fix[:, :], tile_row[:, :], -1.0, float(ZERO_ROW), ALU.mult, ALU.add))
                    chain(v.tensor_scalar(tile_cmp[0:1, :, 0], tile_e[0:1, :], float(E), None, ALU.is_ge))
                    chain(v.tensor_tensor(tile_fix[:, :], tile_fix[:, :], tile_cmp[0:1, :, 0], ALU.mult))
                    v.tensor_tensor(table[:, 1, :], tile_row[:, :], tile_fix[:, :], ALU.add).then_inc(table_ready, 1)

            def g_low(j, s, c):
                dve.wait_ge(g_hi_ready, PAIRS * j + c + 1)
                rows, w = (P, 2 * GT) if 2 * c + 1 < FC else (F_LAST, GT)
                v.tensor_tensor(g_lo[0:rows, c % 2, 0:w], product[0:rows, c % 2, 0:w], g_hi[0:rows, c % 2, 0:w].bitcast(F32),
                                ALU.subtract).then_inc(g_lo_ready, 1)

            def read_rows(r, s):
                dve.wait_ge(x_ready, SHARED + r + 1)
                wait(dve, y_added, 32 * (r - 1))
                v.tensor_copy(tile_expert[:, :], tile_e[:, bass.ds(r, 1)]).then_inc(expert_ready, 1)
                dve.wait_ge(expert_ready, r + 1)
                for t in range(2):
                    v.tensor_copy(row_id[:, s, t:t + 1], xe[:, s, t, AT_ID:AT_ID + 1])
                for t in range(2):
                    ins = v.scalar_tensor_tensor(out=same[:, t, :], in0=xe[:, s, t, AT_E:AT_E + TOPK], scalar=tile_expert[:, 0:1],
                                                 in1=xe[:, s, t, AT_W:AT_W + TOPK], op0=ALU.is_equal, op1=ALU.mult,
                                                 accum_out=row_weight[:, s, t:t + 1])
                ins.then_inc(rows_known, 1)

            def shared_rows(j, s):
                wait(dve, y_stored, 16 * (j - 1))
                dve.wait_ge(yT_ps, j + 1)
                v.tensor_tensor(y_rows[:, s, :, :].rearrange("p t d -> p (t d)"), bank[7][:, 0:GT],
                                H2_flat[:, bass.ds(j * GT, GT)], ALU.add).then_inc(y_rows_ready, 1)

            def routed_rows(j, s):
                wait(dve, y_added, 32 * (j - SHARED - 1))
                wait(dve, rows_known, j - SHARED + 1)
                dve.wait_ge(yT_ps, j + 1)
                for t in range(2):
                    ins = v.tensor_scalar(y_rows[:, s, t, :], bank[7][:, t * P:(t + 1) * P], row_weight[:, s, t:t + 1], None, ALU.mult)
                ins.then_inc(y_rows_ready, 1)

            def dve_tile(j, s, split, routed, prev, nxt):
                first = isinstance(j, int) and j == 0
                for c in range(PAIRS):
                    rows, w = (P, 2 * GT) if 2 * c + 1 < FC else (F_LAST, GT)
                    if c > 0:
                        g_low(j, s, c - 1)
                    elif not first:
                        g_low(j - 1, 1 - s, PAIRS - 1)
                    dve.wait_ge(silu_ready, PAIRS * j + c + 1)
                    dve.wait_ge(b_ps, PAIRS * j + c + 1)
                    wait(dve, g_lo_ready, PAIRS * j + c - 1)
                    v.tensor_tensor(product[0:rows, c % 2, 0:w], act_a[0:rows, c % 2, 0:w], bank[2 + c % 2][0:rows, 0:w],
                                    ALU.mult).then_inc(product_ready, 1)
                    if c == 4 and routed:
                        read_rows(j - SHARED, s)
                    if c in (1, 2) and split is not None:
                        split_low(split, s, c - 1)
                    if c == 5 and prev is not None:
                        prev(j - 1, 1 - s)
                    if c == 3 and nxt:
                        x_low(j + 1, 1 - s)
                    late_slot(j, c)
                    if isinstance(j, int) and j in (2, 3) and c % 2 == 0:
                        tile_table(3 * (j - 2) + c // 2)

            dve.wait_ge(h2_kept, B - 1)
            dve_tile(0, 0, None, False, None, True)
            for j in range(1, 4):
                dve_tile(j, j % 2, None, False, shared_rows, True)
            with dve.Fori(2, SHARED // 2 - 1) as i:
                for s in range(2):
                    dve_tile(2 * i + s, s, None, False, shared_rows, True)
            dve_tile(SHARED - 2, 0, None, False, shared_rows, True)
            dve.wait_ge(h2_kept, B)
            dve_tile(SHARED - 1, 1, 1, False, shared_rows, True)
            dve_tile(SHARED, 0, 2, True, shared_rows, True)
            dve_tile(SHARED + 1, 1, 3, True, routed_rows, True)
            HALF = (SHARED + ROUTED) // 2
            with dve.Fori(SHARED // 2 + 1, HALF - 1) as i:
                for s in range(2):
                    dve_tile(2 * i + s, s, 2 * i + s - SHARED + 2, True, routed_rows, True)
            dve_tile(2 * HALF - 2, 0, ROUTED, True, routed_rows, True)
            dve_tile(2 * HALF - 1, 1, None, True, routed_rows, False)
            g_low(2 * HALF - 1, 1, PAIRS - 1)
            routed_rows(2 * HALF - 1, 1)



def kernel(**inputs):
    import concourse.bacc as bacc
    from concourse.bass_utils import run_bass_kernel_spmd as run

    nc = bacc.Bacc("TRN2", target_bir_lowering=False, num_devices=1)
    arrays, aps = {}, {}
    for name, value in inputs.items():
        short = name.removeprefix("L0_")
        arrays[f"in_{short}"] = np.ascontiguousarray(value)
        v = arrays[f"in_{short}"]
        aps[short] = nc.dram_tensor(f"in_{short}", v.shape, mybir.dt.from_np(v.dtype), kind="ExternalInput").ap()
    out = nc.dram_tensor("out", (B, T, D), F32, kind="ExternalOutput").ap()
    build(nc, aps, out)
    r = run(nc, [arrays], core_ids=[0])
    return r.results[0]["out"]
```
